# Optimizing a Trainium2 kernel written in Bass

```python
import numpy as np
import jax
import jax.numpy as jnp

def _softmax(x, axis=-1):
    return jax.nn.softmax(x, axis=axis)

def _gelu(x):
    return jax.nn.gelu(x, approximate=True)

def _silu(x):
    return jax.nn.silu(x)

def _sigmoid(x):
    return jax.nn.sigmoid(x)

def _layernorm(x, axis=-1, eps=1e-05):
    m = jnp.mean(x, axis=axis, keepdims=True)
    v = jnp.var(x, axis=axis, keepdims=True)
    return (x - m) / jnp.sqrt(v + eps)

def _scatter_add(tgt, idx, src, axis=0):
    return tgt.at[idx].add(src)

def _segment_sum(src, seg, n):
    return jax.ops.segment_sum(src, seg, n)
kernel_name = 'mk_conv_attn_hybrid_d4_conv_nchw512_r4_16571d'

def setup_inputs(seed: int=0):
    np.random.seed(seed)
    _w = jnp.asarray

    def _rec_inputs():
        import jax
        import jax.numpy as jnp
        _gk = jax.random.key(seed)
        x = -7.109e-05 + 0.9999 * jax.random.normal(jax.random.fold_in(_gk, 1), (16, 128, 16, 16), jnp.float32)
        return x
    x = _rec_inputs()

    def _L0_conv_setup():
        import jax, jax.numpy as jnp
        import numpy as np
        THRESHOLD = 0.8
        EPS = 1e-12
        key = jax.random.key(seed)
        k1, k2 = jax.random.split(key)
        x = jax.random.normal(k1, (32, 128, 16, 16), dtype=jnp.float32)
        memory = jax.random.normal(k2, (256, 128), dtype=jnp.float32)
        return {'x': x, 'memory': memory}
    _L0_conv_all = _L0_conv_setup()
    _L0_conv_in = {k: v for k, v in _L0_conv_all.items() if k in ('memory',)}
    del _L0_conv_all

    def _L1_conv_setup():
        import jax, jax.numpy as jnp
        import numpy as np
        B, C, W, H = (16, 128, 32, 32)

        def spatial_shift1(y):
            c = y.shape[-1]
            cq = c // 4
            p0 = jnp.concatenate([y[:, :1, :, 0 * cq:1 * cq], y[:, :-1, :, 0 * cq:1 * cq]], axis=1)
            p1 = jnp.concatenate([y[:, 1:, :, 1 * cq:2 * cq], y[:, -1:, :, 1 * cq:2 * cq]], axis=1)
            p2 = jnp.concatenate([y[:, :, :1, 2 * cq:3 * cq], y[:, :, :-1, 2 * cq:3 * cq]], axis=2)
            p3 = jnp.concatenate([y[:, :, 1:, 3 * cq:], y[:, :, -1:, 3 * cq:]], axis=2)
            return jnp.concatenate([p0, p1, p2, p3], axis=-1)

        def spatial_shift2(y):
            c = y.shape[-1]
            cq = c // 4
            p0 = jnp.concatenate([y[:, :, :1, 0 * cq:1 * cq], y[:, :, :-1, 0 * cq:1 * cq]], axis=2)
            p1 = jnp.concatenate([y[:, :, 1:, 1 * cq:2 * cq], y[:, :, -1:, 1 * cq:2 * cq]], axis=2)
            p2 = jnp.concatenate([y[:, :1, :, 2 * cq:3 * cq], y[:, :-1, :, 2 * cq:3 * cq]], axis=1)
            p3 = jnp.concatenate([y[:, 1:, :, 3 * cq:], y[:, -1:, :, 3 * cq:]], axis=1)
            return jnp.concatenate([p0, p1, p2, p3], axis=-1)
        key = jax.random.key(seed)
        ks = jax.random.split(key, 9)
        s = 0.02
        return {'x': jax.random.normal(ks[0], (B, C, W, H), dtype=jnp.float32), 'w1': jax.random.normal(ks[1], (3 * C, C), dtype=jnp.float32) * s, 'b1': jax.random.normal(ks[2], (3 * C,), dtype=jnp.float32) * s, 'wa': jax.random.normal(ks[3], (C, C), dtype=jnp.float32) * s, 'ba': jax.random.normal(ks[4], (C,), dtype=jnp.float32) * s, 'wb': jax.random.normal(ks[5], (3 * C, C), dtype=jnp.float32) * s, 'bb': jax.random.normal(ks[6], (3 * C,), dtype=jnp.float32) * s, 'w2': jax.random.normal(ks[7], (C, C), dtype=jnp.float32) * s, 'b2': jax.random.normal(ks[8], (C,), dtype=jnp.float32) * s}
    _L1_conv_all = _L1_conv_setup()
    _L1_conv_in = {k: v for k, v in _L1_conv_all.items() if k in ('w1', 'b1', 'wa', 'ba', 'wb', 'bb', 'w2', 'b2')}
    del _L1_conv_all

    def _L2_attn_setup():
        import jax, jax.numpy as jnp
        import numpy as np
        TAU = 0.1
        N_HEADS = 8

        def rosa_scan(x):
            N, T, _ = x.shape
            n = jnp.arange(T)
            rows = n[:, None] + n[None, :]
            valid = rows < T
            rows_c = jnp.where(valid, rows, 0)
            cols = jnp.broadcast_to(n[:, None], (T, T))
            S = x[:, rows_c, cols]
            g = jnp.where(valid[None], S, 1.0)
            a = jnp.where(valid[None], S, 0.0)

            def comb(c1, c2):
                g0, a0 = c1
                g1, a1 = c2
                return (g1 * g0, g1 * a0 + a1)
            _, A = jax.lax.associative_scan(comb, (g, a), axis=1)
            d = n[:, None] - n[None, :]
            low = d >= 0
            dc = jnp.where(low, d, 0)
            colmat = jnp.broadcast_to(n[None, :], (T, T))
            return jnp.where(low[None], A[:, colmat, dc], 0.0)

        def rosa_attn_score(x, tau):
            T = x.shape[-1]
            r = jnp.arange(T, dtype=x.dtype)
            p = r[None, :] / (r[:, None] + 1.0)
            x = x + p
            mask = jnp.arange(T)[:, None] < jnp.arange(T)[None, :]
            x = jnp.where(mask, -jnp.inf, x)
            return jax.nn.softmax(x / tau, axis=-1)
        key = jax.random.key(seed)
        ks = jax.random.split(key, 5)
        B, T, D, Hd = (2, 256, 128, 16)
        x = jax.random.normal(ks[0], (B, T, D), dtype=jnp.float32)
        wq = jax.random.normal(ks[1], (D, D), dtype=jnp.float32) * 0.05
        wk = jax.random.normal(ks[2], (D, D), dtype=jnp.float32) * 0.05
        wv = jax.random.normal(ks[3], (D, D), dtype=jnp.float32) * 0.05
        wo = jax.random.normal(ks[4], (D, Hd), dtype=jnp.float32) * 0.05
        return {'x': x, 'wq': wq, 'wk': wk, 'wv': wv, 'wo': wo}
    _L2_attn_all = _L2_attn_setup()
    _L2_attn_in = {k: v for k, v in _L2_attn_all.items() if k in ('wq', 'wk', 'wv', 'wo')}
    del _L2_attn_all

    def _L2_ffn_setup():
        import jax, jax.numpy as jnp
        import numpy as np
        E = 16
        TOP_K = 2
        D = 128
        I = 512
        I_SH = 256
        B, S = (2, 256)
        key = jax.random.key(seed)
        ks = jax.random.split(key, 8)
        sc_d = 1.0 / np.sqrt(D)
        sc_i = 1.0 / np.sqrt(I)
        sc_ish = 1.0 / np.sqrt(I_SH)
        return {'hidden_states': jax.random.normal(ks[0], (B, S, D), jnp.float32), 'gate_w': jax.random.normal(ks[1], (E, D), jnp.float32) * sc_d, 'wg': jax.random.normal(ks[2], (E, I, D), jnp.float32) * sc_d, 'wu': jax.random.normal(ks[3], (E, I, D), jnp.float32) * sc_d, 'wd': jax.random.normal(ks[4], (E, D, I), jnp.float32) * sc_i, 'swg': jax.random.normal(ks[5], (I_SH, D), jnp.float32) * sc_d, 'swu': jax.random.normal(ks[6], (I_SH, D), jnp.float32) * sc_d, 'swd': jax.random.normal(ks[7], (D, I_SH), jnp.float32) * sc_ish}
    _L2_ffn_all = _L2_ffn_setup()
    _L2_ffn_in = {k: v for k, v in _L2_ffn_all.items() if k in ('gate_w', 'wg', 'wu', 'wd', 'swg', 'swu', 'swd')}
    del _L2_ffn_all

    def _L3_attn_setup():
        import jax, jax.numpy as jnp
        import numpy as np
        B, T, D = (2, 1024, 128)
        H = 8
        HD = D // H
        key = jax.random.key(seed)
        k1, k2, k3 = jax.random.split(key, 3)
        x = jax.random.normal(k1, (B, T, D), dtype=jnp.float32)
        w_qkv = jax.random.normal(k2, (3 * D, D), dtype=jnp.float32) * (1.0 / np.sqrt(D))
        w_out = jax.random.normal(k3, (D, D), dtype=jnp.float32) * (1.0 / np.sqrt(D))
        return {'x': x, 'w_qkv': w_qkv, 'w_out': w_out}
    _L3_attn_all = _L3_attn_setup()
    _L3_attn_in = {k: v for k, v in _L3_attn_all.items() if k in ('w_qkv', 'w_out')}
    del _L3_attn_all

    def _L3_ffn_setup():
        import jax, jax.numpy as jnp
        import numpy as np
        TOP_K = 2
        key = jax.random.key(seed)
        ks = jax.random.split(key, 6)
        B, T, C, E, H = (4, 1024, 128, 8, 512)
        x = jax.random.normal(ks[0], (B, T, C), dtype=jnp.float32)
        W_router = jax.random.normal(ks[1], (C, E), dtype=jnp.float32) * 0.02
        W1 = jax.random.normal(ks[2], (E, C, H), dtype=jnp.float32) * 0.02
        b1 = jnp.zeros((E, H), dtype=jnp.float32)
        W2 = jax.random.normal(ks[3], (E, H, C), dtype=jnp.float32) * 0.02
        b2 = jnp.zeros((E, C), dtype=jnp.float32)
        return {'x': x, 'W_router': W_router, 'W1': W1, 'b1': b1, 'W2': W2, 'b2': b2}
    _L3_ffn_all = _L3_ffn_setup()
    _L3_ffn_in = {k: v for k, v in _L3_ffn_all.items() if k in ('W_router', 'W1', 'b1', 'W2', 'b2')}
    del _L3_ffn_all
    return {'x': x, 'L0_conv_memory': _L0_conv_in['memory'], 'L1_conv_w1': _L1_conv_in['w1'], 'L1_conv_b1': _L1_conv_in['b1'], 'L1_conv_wa': _L1_conv_in['wa'], 'L1_conv_ba': _L1_conv_in['ba'], 'L1_conv_wb': _L1_conv_in['wb'], 'L1_conv_bb': _L1_conv_in['bb'], 'L1_conv_w2': _L1_conv_in['w2'], 'L1_conv_b2': _L1_conv_in['b2'], 'L2_attn_wq': _L2_attn_in['wq'], 'L2_attn_wk': _L2_attn_in['wk'], 'L2_attn_wv': _L2_attn_in['wv'], 'L2_attn_wo': _L2_attn_in['wo'], 'L2_ffn_gate_w': _L2_ffn_in['gate_w'], 'L2_ffn_wg': _L2_ffn_in['wg'], 'L2_ffn_wu': _L2_ffn_in['wu'], 'L2_ffn_wd': _L2_ffn_in['wd'], 'L2_ffn_swg': _L2_ffn_in['swg'], 'L2_ffn_swu': _L2_ffn_in['swu'], 'L2_ffn_swd': _L2_ffn_in['swd'], 'L3_attn_w_qkv': _L3_attn_in['w_qkv'], 'L3_attn_w_out': _L3_attn_in['w_out'], 'L3_ffn_W_router': _L3_ffn_in['W_router'], 'L3_ffn_W1': _L3_ffn_in['W1'], 'L3_ffn_b1': _L3_ffn_in['b1'], 'L3_ffn_W2': _L3_ffn_in['W2'], 'L3_ffn_b2': _L3_ffn_in['b2']}

def reference(x, L0_conv_memory, L1_conv_w1, L1_conv_b1, L1_conv_wa, L1_conv_ba, L1_conv_wb, L1_conv_bb, L1_conv_w2, L1_conv_b2, L2_attn_wq, L2_attn_wk, L2_attn_wv, L2_attn_wo, L2_ffn_gate_w, L2_ffn_wg, L2_ffn_wu, L2_ffn_wd, L2_ffn_swg, L2_ffn_swu, L2_ffn_swd, L3_attn_w_qkv, L3_attn_w_out, L3_ffn_W_router, L3_ffn_W1, L3_ffn_b1, L3_ffn_W2, L3_ffn_b2):
    import jax
    import jax.numpy as jnp

    def _L0_conv_ref(x, memory):
        import jax, jax.numpy as jnp
        import numpy as np
        THRESHOLD = 0.8
        EPS = 1e-12
        B, C, H, W = x.shape
        x_flat = x.reshape(B, C, H * W).transpose(0, 2, 1)
        x_norm = x_flat / jnp.maximum(jnp.linalg.norm(x_flat, axis=-1, keepdims=True), EPS)
        mem_norm = memory / jnp.maximum(jnp.linalg.norm(memory, axis=-1, keepdims=True), EPS)
        sim = jnp.einsum('bnc,mc->bnm', x_norm, mem_norm)
        max_val = jnp.max(sim, axis=-1)
        max_idx = jnp.argmax(sim, axis=-1)
        mem_selected = memory[max_idx]
        mask = (max_val > THRESHOLD).astype(x.dtype)[..., None]
        masked = mem_selected * mask
        return masked.transpose(0, 2, 1).reshape(B, C, H, W)

    def _L1_conv_ref(x, w1, b1, wa, ba, wb, bb, w2, b2):
        import jax, jax.numpy as jnp
        import numpy as np
        B, C, W, H = (16, 128, 32, 32)

        def spatial_shift1(y):
            c = y.shape[-1]
            cq = c // 4
            p0 = jnp.concatenate([y[:, :1, :, 0 * cq:1 * cq], y[:, :-1, :, 0 * cq:1 * cq]], axis=1)
            p1 = jnp.concatenate([y[:, 1:, :, 1 * cq:2 * cq], y[:, -1:, :, 1 * cq:2 * cq]], axis=1)
            p2 = jnp.concatenate([y[:, :, :1, 2 * cq:3 * cq], y[:, :, :-1, 2 * cq:3 * cq]], axis=2)
            p3 = jnp.concatenate([y[:, :, 1:, 3 * cq:], y[:, :, -1:, 3 * cq:]], axis=2)
            return jnp.concatenate([p0, p1, p2, p3], axis=-1)

        def spatial_shift2(y):
            c = y.shape[-1]
            cq = c // 4
            p0 = jnp.concatenate([y[:, :, :1, 0 * cq:1 * cq], y[:, :, :-1, 0 * cq:1 * cq]], axis=2)
            p1 = jnp.concatenate([y[:, :, 1:, 1 * cq:2 * cq], y[:, :, -1:, 1 * cq:2 * cq]], axis=2)
            p2 = jnp.concatenate([y[:, :1, :, 2 * cq:3 * cq], y[:, :-1, :, 2 * cq:3 * cq]], axis=1)
            p3 = jnp.concatenate([y[:, 1:, :, 3 * cq:], y[:, -1:, :, 3 * cq:]], axis=1)
            return jnp.concatenate([p0, p1, p2, p3], axis=-1)
        c = x.shape[1]
        xp = jnp.transpose(x, (0, 2, 3, 1))
        y = jnp.einsum('bwhc,oc->bwho', xp, w1) + b1
        x1 = spatial_shift1(y[..., :c])
        x2 = spatial_shift2(y[..., c:2 * c])
        x3 = y[..., 2 * c:]
        a = jnp.sum(x1 + x2 + x3, axis=(1, 2))
        hat = jax.nn.gelu(a @ wa.T + ba, approximate=False) @ wb.T + bb
        bar = jax.nn.softmax(hat.reshape(-1, 3, c), axis=1)
        g = bar[:, :, None, None, :]
        out = g[:, 0] * x1 + g[:, 1] * x2 + g[:, 2] * x3
        z = jnp.einsum('bwhc,oc->bwho', out, w2) + b2
        return jnp.transpose(z, (0, 3, 1, 2))

    def _L2_attn_ref(x, wq, wk, wv, wo):
        import jax, jax.numpy as jnp
        import numpy as np
        TAU = 0.1
        N_HEADS = 8

        def rosa_scan(x):
            N, T, _ = x.shape
            n = jnp.arange(T)
            rows = n[:, None] + n[None, :]
            valid = rows < T
            rows_c = jnp.where(valid, rows, 0)
            cols = jnp.broadcast_to(n[:, None], (T, T))
            S = x[:, rows_c, cols]
            g = jnp.where(valid[None], S, 1.0)
            a = jnp.where(valid[None], S, 0.0)

            def comb(c1, c2):
                g0, a0 = c1
                g1, a1 = c2
                return (g1 * g0, g1 * a0 + a1)
            _, A = jax.lax.associative_scan(comb, (g, a), axis=1)
            d = n[:, None] - n[None, :]
            low = d >= 0
            dc = jnp.where(low, d, 0)
            colmat = jnp.broadcast_to(n[None, :], (T, T))
            return jnp.where(low[None], A[:, colmat, dc], 0.0)

        def rosa_attn_score(x, tau):
            T = x.shape[-1]
            r = jnp.arange(T, dtype=x.dtype)
            p = r[None, :] / (r[:, None] + 1.0)
            x = x + p
            mask = jnp.arange(T)[:, None] < jnp.arange(T)[None, :]
            x = jnp.where(mask, -jnp.inf, x)
            return jax.nn.softmax(x / tau, axis=-1)
        B, T, D = x.shape
        H = N_HEADS
        Hd = D // H
        tau = TAU
        iq = jax.nn.softmax((x @ wq).reshape(B, T, H, Hd) / tau, axis=-1)
        ik = jax.nn.softmax((x @ wk).reshape(B, T, H, Hd) / tau, axis=-1)
        iv = jax.nn.softmax((x @ wv).reshape(B, T, H, Hd) / tau, axis=-1)
        a = jnp.einsum('bthd,bshd->bhts', iq, ik)
        a = rosa_scan(a.reshape(B * H, T, T)).reshape(B, H, T, T)
        a = rosa_attn_score(a, tau)
        o = jnp.einsum('bhts,bshd->bhtd', a, iv)
        xv = wo.reshape(H, Hd, Hd)
        o = jnp.einsum('bhtd,hde->bhte', o, xv)
        return o.transpose(0, 2, 1, 3).reshape(B, T, D)

    def _L2_ffn_ref(hidden_states, gate_w, wg, wu, wd, swg, swu, swd):
        import jax, jax.numpy as jnp
        import numpy as np
        E = 16
        TOP_K = 2
        D = 128
        I = 512
        I_SH = 256
        B, S = (2, 256)
        b, s, d = hidden_states.shape
        x = hidden_states.reshape(-1, d)
        logits = x @ gate_w.T
        scores = jax.nn.softmax(logits, axis=-1)
        topk_w, topk_idx = jax.lax.top_k(scores, TOP_K)
        cw = jnp.sum(jax.nn.one_hot(topk_idx, E, dtype=x.dtype) * topk_w[..., None], axis=1)
        g = jnp.einsum('td,eid->tei', x, wg)
        u = jnp.einsum('td,eid->tei', x, wu)
        h = jax.nn.silu(g) * u
        out_e = jnp.einsum('tei,edi->ted', h, wd)
        y = jnp.einsum('ted,te->td', out_e, cw)
        sh = jax.nn.silu(x @ swg.T) * (x @ swu.T)
        y = y + sh @ swd.T
        return y.reshape(b, s, d)

    def _L3_attn_ref(x, w_qkv, w_out):
        import jax, jax.numpy as jnp
        import numpy as np
        B, T, D = (2, 1024, 128)
        H = 8
        HD = D // H
        b, t, d = x.shape
        qkv = x @ w_qkv.T
        q, k, v = jnp.split(qkv, 3, axis=-1)

        def split_heads(a):
            return a.reshape(b, t, H, HD).transpose(0, 2, 1, 3)
        q, k, v = (split_heads(q), split_heads(k), split_heads(v))
        scale = 1.0 / np.sqrt(HD).astype(np.float32)
        scores = jnp.einsum('bhqd,bhkd->bhqk', q, k) * scale
        causal = jnp.tril(jnp.ones((t, t), dtype=bool))
        scores = jnp.where(causal[None, None], scores, -jnp.inf)
        attn = jax.nn.softmax(scores, axis=-1)
        out = jnp.einsum('bhqk,bhkd->bhqd', attn, v)
        out = out.transpose(0, 2, 1, 3).reshape(b, t, d)
        return out @ w_out.T

    def _L3_ffn_ref(x, W_router, W1, b1, W2, b2):
        import jax, jax.numpy as jnp
        import numpy as np
        TOP_K = 2
        B, T, C = x.shape
        E = W_router.shape[1]
        x_flat = x.reshape(B * T, C)
        logits = x_flat @ W_router
        probs = jax.nn.softmax(logits, axis=-1)
        topk_p, topk_i = jax.lax.top_k(probs, TOP_K)
        topk_p = topk_p / topk_p.sum(axis=-1, keepdims=True)
        combine = (jax.nn.one_hot(topk_i, E, dtype=x_flat.dtype) * topk_p[..., None]).sum(axis=1)
        out = jnp.zeros_like(x_flat)
        for e in range(E):
            h = jax.nn.relu(x_flat @ W1[e] + b1[e])
            y = h @ W2[e] + b2[e]
            out = out + combine[:, e:e + 1] * y
        return out.reshape(B, T, C)

    def _gn(v, G=32, eps=1e-05):
        B_, C_, H_, W_ = v.shape
        g = v.reshape(B_, G, C_ // G, H_, W_)
        m = jnp.mean(g, axis=(2, 3, 4), keepdims=True)
        s = jnp.var(g, axis=(2, 3, 4), keepdims=True)
        return ((g - m) / jnp.sqrt(s + eps)).reshape(v.shape)

    def _ln_c(v, eps=1e-06):
        m = jnp.mean(v, axis=1, keepdims=True)
        s = jnp.var(v, axis=1, keepdims=True)
        return (v - m) / jnp.sqrt(s + eps)

    def _ln_t(v, eps=1e-05):
        m = jnp.mean(v, axis=-1, keepdims=True)
        s = jnp.var(v, axis=-1, keepdims=True)
        return (v - m) / jnp.sqrt(s + eps)

    def _to_tokens(v):
        B_, C_, H_, W_ = v.shape
        return v.reshape(B_, C_, H_ * W_).transpose(0, 2, 1)

    def _from_tokens(t, like):
        B_, C_, H_, W_ = like.shape
        return t.transpose(0, 2, 1).reshape(B_, C_, H_, W_)
    x = x + _L0_conv_ref(_gn(x), L0_conv_memory)
    x = x + _L1_conv_ref(_gn(x), L1_conv_w1, L1_conv_b1, L1_conv_wa, L1_conv_ba, L1_conv_wb, L1_conv_bb, L1_conv_w2, L1_conv_b2)
    t = _to_tokens(x)
    t = t + _L2_attn_ref(_ln_t(t), L2_attn_wq, L2_attn_wk, L2_attn_wv, L2_attn_wo)
    t = t + _L2_ffn_ref(_ln_t(t), L2_ffn_gate_w, L2_ffn_wg, L2_ffn_wu, L2_ffn_wd, L2_ffn_swg, L2_ffn_swu, L2_ffn_swd)
    t = t + _L3_attn_ref(_ln_t(t), L3_attn_w_qkv, L3_attn_w_out)
    t = t + _L3_ffn_ref(_ln_t(t), L3_ffn_W_router, L3_ffn_W1, L3_ffn_b1, L3_ffn_W2, L3_ffn_b2)
    x = _from_tokens(t, x)
    return x

_drawn_inputs = setup_inputs


def setup_inputs(seed=0):
    import zlib

    import numpy as np

    out = dict(_drawn_inputs(seed))
    spreads = {'L3_ffn_b1': (0.0, 0.425), 'L3_ffn_b2': (0.0, 0.1)}
    factors = {'L1_conv_b1': 4.41,
     'L1_conv_wa': 3.825,
     'L1_conv_ba': 200.0,
     'L1_conv_wb': 3.171,
     'L1_conv_bb': 200.0}
    for name, (base, spread) in spreads.items():
        noise = np.random.default_rng([zlib.crc32(name.encode()), seed]).standard_normal(out[name].shape)
        drawn = base * np.exp(spread * noise) if base else spread * noise
        out[name] = jnp.asarray(drawn.astype(out[name].dtype))
    for name, factor in factors.items():
        out[name] = (out[name] * factor).astype(out[name].dtype)
    return out
```

```python
from contextlib import ExitStack

import concourse.bass as bass
from concourse import mybir
import numpy as np

F32 = mybir.dt.float32
BF16 = mybir.dt.bfloat16
I32 = mybir.dt.int32
U32 = mybir.dt.uint32
ALU = mybir.AluOpType
ACT = mybir.ActivationFunctionType
AX = mybir.AxisListType

P = 128
C = 128
B, HH, WW = 16, 16, 16
T = HH * WW
NT = B * T // P
MEM = 256
NH, HD = 8, 16
BH = B * NH


class Space:

    def __init__(self, nc, ctx):
        self.nc, self.ctx = nc, ctx
        self.sems = []
        ctx.callback(self.give_back)

    def sb(self, name, shape, dt=F32):
        return self.ctx.enter_context(self.nc.sbuf_tensor(name, shape, dt))

    def ps(self, name, shape, dt=F32):
        return self.ctx.enter_context(self.nc.psum_tensor(name, shape, dt))

    def sem(self, name):
        self.sems.append(self.nc.alloc_semaphore(name))
        return self.sems[-1]

    def give_back(self):
        if self.sems:
            self.nc.clear_and_free_semaphores(self.sems)
            self.nc.all_engine_barrier()


def in_turn(eng, n, depth, body):
    for j in range(min(depth, n)):
        body(j, j, True)
    if n > depth:
        assert n % depth == 0
        with eng.Fori(1, n // depth) as i:
            for u in range(depth):
                body(i * depth + u, u, False)


def prepare_and_first_norm(nc, top, x, memory, keep):
    with ExitStack() as ctx:
        s = Space(nc, ctx)
        mem_rows = s.sb("mem_rows", [P, 2, C])
        mem_sq = s.sb("mem_sq", [P, 2, C])
        mem_norm = s.sb("mem_norm", [P, 4])
        ps_mem = s.ps("ps_mem", [P, 512])
        x_in = [s.sem(f"x_in{i}") for i in range(4)]
        mem_in = s.sem("mem_in")
        const_ready = s.sem("const_ready")
        mem_step = s.sem("mem_step")
        mem_len = s.sem("mem_len")
        mem_turned = s.sem("mem_turned")
        bn_done = s.sem("bn_done")
        g = norm_space(nc, s, "gn0")
        block = ctx.enter_context(nc.Block())

        @block.sync
        def _(sp):
            sp.dma_start(mem_rows[:], memory.rearrange("(m p) c -> p m c", p=P)).then_inc(mem_in, 16)
            for i in range(4):
                sp.dma_start(keep.xc[:, 4 * i:4 * i + 4, :],
                             x[4 * i:4 * i + 4].rearrange("b c h w -> c b (h w)")).then_inc(x_in[i], 16)

        @block.gpsimd
        def _(pool):
            pool.memset(keep.ident[:], 0.0).then_inc(const_ready, 1)
            pool.memset(keep.group4[:], 0.25).then_inc(const_ready, 1)
            pool.memset(keep.ones[:], 1.0).then_inc(const_ready, 1)
            pool.wait_ge(const_ready, 3)
            pool.affine_select(out=keep.ident[:], in_=keep.ident[:], compare_op=ALU.not_equal, fill=1.0,
                               base=0, pattern=[[-1, P]], channel_multiplier=1).then_inc(const_ready, 1)
            v = keep.group4[:].rearrange("p (g k) -> p g k", k=4)
            pool.affine_select(out=v, in_=v, compare_op=ALU.is_ge, fill=0.0,
                               base=0, pattern=[[-4, 32], [0, 4]], channel_multiplier=1).then_inc(const_ready, 1)
            pool.wait_ge(const_ready, 5)
            pool.affine_select(out=v, in_=v, compare_op=ALU.is_ge, fill=0.0,
                               base=3, pattern=[[4, 32], [0, 4]], channel_multiplier=-1).then_inc(const_ready, 1)

        @block.scalar
        def _(act):
            act.wait_ge(mem_len, 2)
            act.activation(mem_norm[:, 2:4], mem_norm[:, 0:2], ACT.Sqrt).then_inc(mem_len, 1)
            norm_scalar(act, g)

        @block.vector
        def _(dve):
            dve.wait_ge(mem_in, 16)
            for m in range(2):
                dve.tensor_tensor_reduce(mem_sq[:, m, :], mem_rows[:, m, :], mem_rows[:, m, :], 1.0, 0.0,
                                         ALU.mult, ALU.add, mem_norm[:, m:m + 1]).then_inc(mem_len, 1)
            dve.wait_ge(mem_len, 3)
            dve.tensor_scalar(mem_norm[:, 0:2], mem_norm[:, 2:4], 1e-12, None, ALU.max).then_inc(mem_len, 1)
            dve.wait_ge(mem_len, 4)
            dve.reciprocal(mem_norm[:, 2:4], mem_norm[:, 0:2]).then_inc(mem_len, 1)
            dve.wait_ge(mem_len, 5)
            for m in range(2):
                dve.tensor_scalar(mem_rows[:, m, :], mem_rows[:, m, :], mem_norm[:, 2 + m:3 + m], None,
                                  ALU.mult).then_inc(mem_step, 1)
            for i in range(4):
                dve.wait_ge(x_in[i], 16)
                with dve.Fori(4 * i, 4 * i + 4) as b:
                    dve.bn_stats(keep.bn[:, b, :], keep.xc[:, b, :]).then_inc(bn_done, 1)
            dve.wait_ge(mem_turned, 1)
            dve.tensor_copy(keep.mem_t[:], ps_mem[:, 0:MEM]).then_inc(mem_step, 1)
            dve.wait_ge(bn_done, B)
            norm_vector(dve, g, keep)

        @block.tensor
        def _(pe):
            pe.wait_ge(const_ready, 6)
            pe.wait_ge(mem_step, 2)
            for m in range(2):
                last = pe.transpose(ps_mem[:, m * P:(m + 1) * P], mem_rows[:, m, :], keep.ident[:])
            last.then_inc(mem_turned, 1)
            norm_tensor(pe, g, keep)


class norm_space:

    def __init__(self, nc, s, name):
        self.mv = s.sb(name + "_mv", [P, B, 2])
        self.both = s.sb(name + "_both", [P, 2, B])
        self.sq = s.sb(name + "_sq", [P, B])
        self.group = s.sb(name + "_group", [P, 2, B])
        self.gvar = s.sb(name + "_gvar", [P, B])
        self.gstd = s.sb(name + "_gstd", [P, B])
        self.ps = s.ps(name + "_ps", [P, 512])
        self.aggregated = s.sem(name + "_aggregated")
        self.channel = s.sem(name + "_channel")
        self.summed = s.sem(name + "_summed")
        self.step = s.sem(name + "_step")
        self.rstd = s.sem(name + "_rstd")


def norm_vector(dve, g, keep, eps=1e-5):
    for b in range(B):
        dve.bn_aggr(g.mv[:, b, :], keep.bn[:, b, :]).then_inc(g.aggregated, 1)
    dve.wait_ge(g.aggregated, B)
    mean, var = g.mv[:, :, 0], g.mv[:, :, 1]
    dve.tensor_tensor(g.sq[:], mean, mean, ALU.mult).then_inc(g.channel, 1)
    dve.tensor_copy(g.both[:, 0, :], mean).then_inc(g.channel, 1)
    dve.wait_ge(g.channel, 2)
    dve.tensor_tensor(g.both[:, 1, :], var, g.sq[:], ALU.add).then_inc(g.channel, 1)
    dve.wait_ge(g.summed, 1)
    dve.tensor_copy(g.group[:].rearrange("p a b -> p (a b)"), g.ps[:, 0:2 * B]).then_inc(g.step, 1)
    dve.wait_ge(g.step, 1)
    dve.tensor_tensor(g.sq[:], g.group[:, 0, :], g.group[:, 0, :], ALU.mult).then_inc(g.step, 1)
    dve.wait_ge(g.step, 2)
    dve.scalar_tensor_tensor(g.gvar[:], g.group[:, 1, :], eps, g.sq[:], ALU.add, ALU.subtract).then_inc(g.step, 1)
    dve.wait_ge(g.rstd, 1)
    dve.reciprocal(keep.rstd[:], g.gstd[:]).then_inc(g.step, 1)
    dve.wait_ge(g.step, 4)
    dve.scalar_tensor_tensor(keep.shift[:], g.group[:, 0, :], -1.0, keep.rstd[:], ALU.mult, ALU.mult).then_inc(g.step, 1)


def norm_scalar(act, g):
    act.wait_ge(g.step, 3)
    act.activation(g.gstd[:], g.gvar[:], ACT.Sqrt).then_inc(g.rstd, 1)


def norm_tensor(pe, g, keep):
    pe.wait_ge(g.channel, 3)
    pe.matmul(g.ps[:, 0:2 * B], keep.group4[:], g.both[:].rearrange("p a b -> p (a b)"),
              start=True, stop=True).then_inc(g.summed, 1)


def memory_lookup(nc, top, memory, keep):
    with ExitStack() as ctx:
        s = Space(nc, ctx)
        xn = s.sb("xn", [P, 2, 2, P])
        sq = s.sb("sq", [P, 2, 2, P])
        length = s.sb("length", [P, 2, 2])
        best = s.sb("best", [P, 2, 2, 8])
        where = s.sb("where", [P, 2, 2, 8], U32)
        least = s.sb("least", [P, 2, 2])
        hit = s.sb("hit", [P, 2, 2])
        row = s.sb("row", [P, 2, 2, C])
        rowm = s.sb("rowm", [P, 2, 2, C])
        ps_sim = [s.ps(f"ps_sim{i}", [P, 2, MEM]) for i in range(2)]
        ps_len = [s.ps(f"ps_len{i}", [P, 512]) for i in range(2)]
        ps_row = [s.ps(f"ps_row{i}", [P, 512]) for i in range(2)]
        g = norm_space(nc, s, "gn1")
        normed = s.sem("l0_normed")
        squared = s.sem("l0_squared")
        similar = s.sem("l0_similar")
        len_ready = s.sem("l0_len_ready")
        looked = s.sem("l0_looked")
        gathered = [s.sem(f"l0_gathered{u}") for u in range(4)]
        masked = s.sem("l0_masked")
        turned = s.sem("l0_turned")
        added = s.sem("l0_added")
        bn_done = s.sem("l0_bn_done")
        block = ctx.enter_context(nc.Block())

        @block.scalar
        def _(act):
            def image(b, u, early):
                if not early:
                    act.wait_ge(similar, b - 1)
                act.activation(xn[:, u].rearrange("p a b -> p (a b)"), keep.xc[:, b, :], ACT.Identity,
                               bias=keep.shift[:, bass.ds(b, 1)], scale=keep.rstd[:, bass.ds(b, 1)]).then_inc(normed, 1)
                act.wait_ge(normed, b + 1)
                act.activation(sq[:, u], xn[:, u], ACT.Square).then_inc(squared, 1)
                if not early:
                    act.wait_ge(looked, 6 * (b - 1))
                act.wait_ge(similar, b + 1)
                act.activation(length[:, u, :], ps_len[u][:, 0:2], ACT.Sqrt).then_inc(len_ready, 1)

            in_turn(act, B, 2, image)
            norm_scalar(act, g)

        @block.tensor
        def _(pe):
            def turn(b, u):
                pe.wait_ge(masked, 2 * (b + 1))
                for h in range(2):
                    last = pe.transpose(ps_row[u][:, h * P:(h + 1) * P], rowm[:, u, h, :], keep.ident[:])
                last.then_inc(turned, 1)

            def image(b, u, early):
                pe.wait_ge(squared, b + 1)
                if not early:
                    pe.wait_ge(looked, 6 * (b - 1))
                for h in range(2):
                    pe.matmul(ps_sim[u][:, h, :], xn[:, u, h, :], keep.mem_t[:], start=True, stop=True)
                for h in range(2):
                    last = pe.matmul(ps_len[u][:, h:h + 1], sq[:, u, h, :], keep.ones[:, 0:1], start=True, stop=True)
                last.then_inc(similar, 1)
                if not early or b > 0:
                    turn(b - 1, 1 - u)

            in_turn(pe, B, 2, image)
            turn(B - 1, 1)
            norm_tensor(pe, g, keep)

        @block.gpsimd
        def _(pool):
            def image(b, u, early):
                pool.wait_ge(looked, 6 * b + 4)
                if not early:
                    pool.wait_ge(masked, 2 * (b - 1))
                pool.sem_inc(keep.waited)
                for h in range(2):
                    pool.indirect_dma_start(row[:, u, h, :], None, memory,
                                            bass.IndirectOffsetOnAxis(where[:, u, h, 0:1], 0)).then_inc(gathered[2 * u + h], 16)

            in_turn(pool, B, 2, image)

        @block.vector
        def _(dve):
            def finish(b, u):
                for h in range(2):
                    dve.wait_ge(gathered[2 * u + h], 8 * (b - u) + 16)
                    if h == 0:
                        if not isinstance(b, int) or b >= 2:
                            dve.wait_ge(turned, b - 1)
                    dve.tensor_scalar(rowm[:, u, h, :], row[:, u, h, :], hit[:, u, h:h + 1], None,
                                      ALU.mult).then_inc(masked, 1)
                dve.wait_ge(turned, b + 1)
                dve.tensor_tensor(keep.xc[:, b, :], keep.xc[:, b, :], ps_row[u][:, 0:T], ALU.add).then_inc(added, 1)
                dve.wait_ge(added, b + 1)
                dve.bn_stats(keep.bn[:, b, :], keep.xc[:, b, :]).then_inc(bn_done, 1)

            def image(b, u, early):
                dve.wait_ge(similar, b + 1)
                if not early:
                    dve.wait_ge(gathered[2 * u + 1], 8 * (b - u))
                    dve.wait_ge(masked, 2 * (b - 1))
                dve.sem_inc(keep.waited)
                for h in range(2):
                    dve.max(best[:, u, h, :], ps_sim[u][:, h, :]).then_inc(looked, 1)
                dve.wait_ge(looked, 6 * b + 2)
                dve.sem_inc(keep.waited)
                for h in range(2):
                    dve.max_index(where[:, u, h, :], best[:, u, h, :], ps_sim[u][:, h, :]).then_inc(looked, 1)
                dve.wait_ge(len_ready, b + 1)
                dve.tensor_scalar(least[:, u, :], length[:, u, :], 1e-12, 0.8, ALU.max, ALU.mult).then_inc(looked, 1)
                dve.wait_ge(looked, 6 * b + 5)
                dve.tensor_tensor(hit[:, u, :], best[:, u, :, 0], least[:, u, :], ALU.is_gt).then_inc(looked, 1)
                dve.wait_ge(looked, 6 * b + 6)
                if not early or b > 0:
                    finish(b - 1, 1 - u)

            in_turn(dve, B, 2, image)
            finish(B - 1, 1)
            dve.wait_ge(bn_done, B)
            k = SecondNorm(keep)
            norm_vector(dve, g, k)


class SecondNorm:

    def __init__(self, keep):
        self.bn, self.rstd, self.shift = keep.bn, keep.rstd2, keep.shift2


SHIFTS = [(0, 1), (2, 1), (1, 0), (1, 2), (1, 1)]
DOWN, UP, RIGHT, LEFT, STAY = range(5)
BRANCH_SHIFT = [[DOWN, UP, RIGHT, LEFT], [RIGHT, LEFT, DOWN, UP], [STAY] * 4]
GATE_OF_SHIFT = [0, 0, 1, 1, 2]
Q = 32


def gates(nc, top, w1_rows, w1_t, b1, wa_t, ba, wb_t, bb, w2_t, b2, keep):
    with ExitStack() as ctx:
        s = Space(nc, ctx)
        w1t = s.sb("w1t_sb", [P, 3 * C])
        wat = s.sb("wat_sb", [P, C])
        wbt = s.sb("wbt_sb", [P, 3 * C])
        b1s = s.sb("b1s", [P, 3])
        bas = s.sb("bas", [P, 1])
        bbs = s.sb("bbs", [P, 3])
        b2s = s.sb("b2s", [P, 1])
        bsum = s.sb("bsum", [P, 2])
        edge = s.sb("edge", [P, 5, B])
        diff = s.sb("diff", [P, 2, B])
        sums = s.sb("sums", [P, 5, B])
        pooled = s.sb("pooled", [P, B])
        hidden = s.sb("hidden", [P, B])
        hat = s.sb("hat", [P, 3, B])
        peak = s.sb("peak", [P, B])
        total = s.sb("total", [P, B])
        gate = s.sb("gate", [P, 3, B])
        mixed = s.sb("mixed", [P, B])
        ps_pool = s.ps("ps_pool", [P, 512])
        ps_hid = s.ps("ps_hid", [P, 512])
        ps_hat = s.ps("ps_hat", [P, 512])
        ps_bias = s.ps("ps_bias", [P, 512])
        w_in = s.sem("l1_w_in")
        rows_in = s.sem("l1_rows_in")
        zeroed = s.sem("l1_zeroed")
        padded = s.sem("l1_padded")
        edged = s.sem("l1_edged")
        summed = s.sem("l1_summed")
        pool_ps = s.sem("l1_pool_ps")
        pool_sb = s.sem("l1_pool_sb")
        hid_ps = s.sem("l1_hid_ps")
        hid_sb = s.sem("l1_hid_sb")
        hat_ps = s.sem("l1_hat_ps")
        soft = s.sem("l1_soft")
        exped = s.sem("l1_exped")
        bias_ps = s.sem("l1_bias_ps")
        block = ctx.enter_context(nc.Block())
        pad = keep.pad
        inner = pad[:, :, 1:17, 1:17]

        @block.sync
        def _(sp):
            for dst, src in ((w1t[:], w1_t), (wat[:], wa_t), (wbt[:], wb_t), (keep.w2t[:], w2_t),
                             (b1s[:], b1), (bas[:], ba),
                             (bbs[:], bb), (b2s[:], b2)):
                sp.dma_start(dst, src).then_inc(w_in, 16)
            sp.wait_ge(zeroed, 1)
            for k in range(2):
                for q in range(4):
                    sp.dma_start(keep.w1s[Q * q:Q * q + Q, BRANCH_SHIFT[k][q], :],
                                 w1_rows[k * C + Q * q:k * C + Q * q + Q, :]).then_inc(rows_in, 16)
            sp.dma_start(keep.w1s[:, STAY, :], w1_rows[2 * C:3 * C, :]).then_inc(rows_in, 16)
            sp.wait_ge(rows_in, 16 * 9)

        @block.gpsimd
        def _(pool):
            pool.memset(keep.w1s[:], 0.0).then_inc(zeroed, 1)

        @block.scalar
        def _(act):
            with act.Fori(0, B) as b:
                act.activation(pad[:, b, 1:17, 1:17], keep.xc[:, b, :].rearrange("p (h w) -> p h w", w=WW),
                               ACT.Identity, bias=keep.shift2[:, bass.ds(b, 1)],
                               scale=keep.rstd2[:, bass.ds(b, 1)]).then_inc(padded, 1)
            act.wait_ge(hid_ps, 1)
            act.activation(hidden[:], ps_hid[:, 0:B], ACT.Gelu, bias=bas[:, 0:1]).then_inc(hid_sb, 1)
            act.wait_ge(soft, 6)
            act.activation(gate[:], hat[:], ACT.Exp).then_inc(exped, 1)

        @block.vector
        def _(dve):
            dve.wait_ge(w_in, 16 * 8)
            dve.tensor_reduce(bsum[:, 0:1], b1s[:], AX.X, ALU.add).then_inc(pool_sb, 1)
            dve.wait_ge(pool_sb, 1)
            dve.tensor_scalar(bsum[:, 1:2], bsum[:, 0:1], float(T), None, ALU.mult).then_inc(pool_sb, 1)
            dve.wait_ge(padded, B)
            for dst, src in ((pad[:, :, 0, 1:17], pad[:, :, 1, 1:17]), (pad[:, :, 17, 1:17], pad[:, :, 16, 1:17]),
                             (pad[:, :, 1:17, 0], pad[:, :, 1:17, 1]), (pad[:, :, 1:17, 17], pad[:, :, 1:17, 16])):
                dve.tensor_copy(dst, src).then_inc(edged, 1)
            for n, src in enumerate((pad[:, :, 1, 1:17], pad[:, :, 16, 1:17], pad[:, :, 1:17, 1], pad[:, :, 1:17, 16])):
                dve.tensor_reduce(edge[:, n, :], src, AX.X, ALU.add).then_inc(summed, 1)
            dve.tensor_reduce(sums[:, STAY, :], inner, AX.XY, ALU.add).then_inc(summed, 1)
            dve.wait_ge(summed, 5)
            dve.tensor_tensor(diff[:, 0, :], edge[:, 0, :], edge[:, 1, :], ALU.subtract).then_inc(summed, 1)
            dve.tensor_tensor(diff[:, 1, :], edge[:, 2, :], edge[:, 3, :], ALU.subtract).then_inc(summed, 1)
            dve.wait_ge(summed, 7)
            for n, (d, op) in enumerate(((0, ALU.add), (0, ALU.subtract), (1, ALU.add), (1, ALU.subtract))):
                dve.tensor_tensor(sums[:, n, :], sums[:, STAY, :], diff[:, d, :], op).then_inc(summed, 1)
            dve.wait_ge(pool_ps, 1)
            dve.wait_ge(pool_sb, 2)
            dve.tensor_scalar(pooled[:], ps_pool[:, 0:B], bsum[:, 1:2], None, ALU.add).then_inc(pool_sb, 1)
            dve.wait_ge(hat_ps, 1)
            for k in range(3):
                dve.tensor_scalar(hat[:, k, :], ps_hat[:, k * B:(k + 1) * B], bbs[:, k:k + 1], None, ALU.add).then_inc(soft, 1)
            dve.wait_ge(soft, 3)
            dve.tensor_tensor(peak[:], hat[:, 0, :], hat[:, 1, :], ALU.max).then_inc(soft, 1)
            dve.wait_ge(soft, 4)
            dve.tensor_tensor(peak[:], peak[:], hat[:, 2, :], ALU.max).then_inc(soft, 1)
            dve.wait_ge(soft, 5)
            dve.tensor_tensor(hat[:], hat[:], peak[:, None, :].to_broadcast([P, 3, B]), ALU.subtract).then_inc(soft, 1)
            dve.wait_ge(exped, 1)
            dve.tensor_tensor(total[:], gate[:, 0, :], gate[:, 1, :], ALU.add).then_inc(soft, 1)
            dve.wait_ge(soft, 7)
            dve.tensor_tensor(total[:], total[:], gate[:, 2, :], ALU.add).then_inc(soft, 1)
            dve.wait_ge(soft, 8)
            dve.reciprocal(peak[:], total[:]).then_inc(soft, 1)
            dve.wait_ge(soft, 9)
            dve.tensor_tensor(gate[:], gate[:], peak[:, None, :].to_broadcast([P, 3, B]), ALU.mult).then_inc(soft, 1)
            dve.wait_ge(soft, 10)
            for half, (a, b) in enumerate(((0, 1), (1, 0))):
                rows = slice(64 * half, 64 * half + 64)
                dve.tensor_copy(keep.gate[rows, 0, :], gate[rows, a, :]).then_inc(soft, 1)
                dve.tensor_copy(keep.gate[rows, 1, :], gate[rows, b, :]).then_inc(soft, 1)
            dve.tensor_copy(keep.gate[:, 2, :], gate[:, 2, :]).then_inc(soft, 1)
            dve.tensor_scalar(mixed[:], gate[:, 0, :], b1s[:, 0:1], None, ALU.mult).then_inc(soft, 1)
            for k in (1, 2):
                dve.wait_ge(soft, 15 + k)
                dve.scalar_tensor_tensor(mixed[:], gate[:, k, :], b1s[:, k:k + 1], mixed[:], ALU.mult, ALU.add).then_inc(soft, 1)
            dve.wait_ge(bias_ps, 1)
            dve.tensor_scalar(keep.zbias[:], ps_bias[:, 0:B], b2s[:, 0:1], None, ALU.add).then_inc(soft, 1)

        @block.tensor
        def _(pe):
            pe.wait_ge(w_in, 16 * 8)
            pe.wait_ge(summed, 11)
            for q in range(4):
                for k in range(3):
                    last = pe.matmul(ps_pool[Q * q:Q * q + Q, 0:B], w1t[:, k * C + Q * q:k * C + Q * q + Q],
                                     sums[:, BRANCH_SHIFT[k][q], :], start=(k == 0), stop=(k == 2))
            last.then_inc(pool_ps, 1)
            pe.wait_ge(pool_sb, 3)
            pe.matmul(ps_hid[:, 0:B], wat[:], pooled[:], start=True, stop=True).then_inc(hid_ps, 1)
            pe.wait_ge(hid_sb, 1)
            for k in range(3):
                last = pe.matmul(ps_hat[:, k * B:(k + 1) * B], wbt[:, k * C:(k + 1) * C], hidden[:], start=True, stop=True)
            last.then_inc(hat_ps, 1)
            pe.wait_ge(soft, 18)
            pe.matmul(ps_bias[:, 0:B], keep.w2t[:], mixed[:], start=True, stop=True).then_inc(bias_ps, 1)


def shifted_convolution(nc, top, keep):
    with ExitStack() as ctx:
        s = Space(nc, ctx)
        w2g = s.sb("w2g", [P, 2, 3, C])
        both = s.sb("both", [P, 2, 5, C])
        xnew = s.sb("xnew", [P, 2, 2, P])
        ps_both = [s.ps(f"ps_both{i}", [P, 2, 512]) for i in range(2)]
        ps_z = [s.ps(f"ps_z{i}", [P, 512]) for i in range(2)]
        ps_t = [s.ps(f"ps_t{i}", [P, 512]) for i in range(2)]
        gated = s.sem("cv_gated")
        joined = s.sem("cv_joined")
        copied = s.sem("cv_copied")
        shifted = s.sem("cv_shifted")
        added = s.sem("cv_added")
        turned = s.sem("cv_turned")
        stored = s.sem("cv_stored")
        block = ctx.enter_context(nc.Block())

        @block.vector
        def _(dve):
            def gate(b, u, early):
                if not early:
                    dve.wait_ge(joined, b - 1)
                for k in range(3):
                    dve.tensor_scalar(w2g[:, u, k, :], keep.w2t[:], keep.gate[:, k, bass.ds(b, 1)], None,
                                      ALU.mult).then_inc(gated, 1)

            def add(b, u, early):
                dve.wait_ge(shifted, b + 1)
                if not early:
                    dve.wait_ge(turned, b - 1)
                dve.scalar_tensor_tensor(xnew[:, u].rearrange("p a b -> p (a b)"), ps_z[u][:, 0:T],
                                         keep.zbias[:, bass.ds(b, 1)], keep.xc[:, b, :], ALU.add, ALU.add).then_inc(added, 1)

            gate(0, 0, True)
            gate(1, 1, True)
            add(0, 0, True)
            gate(2, 0, False)
            add(1, 1, True)
            with dve.Fori(1, B // 2 - 1) as i:
                gate(2 * i + 1, 1, False)
                add(2 * i, 0, False)
                gate(2 * i + 2, 0, False)
                add(2 * i + 1, 1, False)
            gate(B - 1, 1, False)
            add(B - 2, 0, False)
            add(B - 1, 1, False)

        @block.scalar
        def _(act):
            def image(b, u, early):
                act.wait_ge(joined, b + 1)
                if not early:
                    act.wait_ge(shifted, b - 1)
                act.activation(both[:, u, 0:4, :], ps_both[u][:, 0, :].rearrange("p (a b) -> p a b", b=C), ACT.Copy).then_inc(copied, 1)
                act.activation(both[:, u, 4, :], ps_both[u][:, 1, 0:C], ACT.Copy).then_inc(copied, 1)
                act.wait_ge(turned, b + 1)
                act.activation(keep.t[:, bass.ds(2 * b, 2), :], ps_t[u][:, 0:T].rearrange("p (a b) -> p a b", b=C),
                               ACT.Copy).then_inc(stored, 1)

            in_turn(act, B, 2, image)

        @block.tensor
        def _(pe):
            def join(b, u, early):
                pe.wait_ge(gated, 3 * b + 3)
                if not early:
                    pe.wait_ge(copied, 2 * (b - 1))
                for n in range(5):
                    last = pe.matmul(ps_both[u][:, n // 4, n % 4 * C:n % 4 * C + C], keep.w1s[:, n, :],
                                     w2g[:, u, GATE_OF_SHIFT[n], :], start=True, stop=True)
                last.then_inc(joined, 1)

            def shift(b, u, early):
                pe.wait_ge(copied, 2 * b + 2)
                if not early:
                    pe.wait_ge(added, b - 1)
                for n, (di, dj) in enumerate(SHIFTS):
                    last = pe.matmul(ps_z[u][:, 0:T], both[:, u, n, :], keep.pad[:, b, di:di + HH, dj:dj + WW],
                                     start=(n == 0), stop=(n == 4))
                last.then_inc(shifted, 1)

            def turn(b, u, early):
                pe.wait_ge(added, b + 1)
                if not early:
                    pe.wait_ge(stored, b - 1)
                for h in range(2):
                    last = pe.transpose(ps_t[u][:, h * P:(h + 1) * P], xnew[:, u, h, :], keep.ident[:])
                last.then_inc(turned, 1)

            join(0, 0, True)
            join(1, 1, True)
            shift(0, 0, True)
            turn(0, 0, True)
            join(2, 0, False)
            shift(1, 1, True)
            turn(1, 1, True)
            with pe.Fori(1, B // 2 - 1) as i:
                join(2 * i + 1, 1, False)
                shift(2 * i, 0, False)
                turn(2 * i, 0, False)
                join(2 * i + 2, 0, False)
                shift(2 * i + 1, 1, False)
                turn(2 * i + 1, 1, False)
            join(B - 1, 1, False)
            shift(B - 2, 0, False)
            turn(B - 2, 0, False)
            shift(B - 1, 1, False)
            turn(B - 1, 1, False)


def lagged(eng, n, depth, parts):
    most = max(lag for lag, _ in parts)
    first = -(-(most + depth) // depth) * depth
    assert n % depth == 0 and n > first

    def step(k, slot, early_steps):
        for lag, body in parts:
            if not early_steps or 0 <= k - lag < n:
                body(k - lag, (slot - lag) % depth, early_steps and k - lag < depth)

    for k in range(first):
        step(k, k, True)
    with eng.Fori(first // depth, n // depth) as i:
        for u in range(depth):
            step(i * depth + u, u, False)
    for k in range(n, n + most):
        step(k, k, True)


def token_stats(nc, top, keep, name, eps=1e-5):
    with ExitStack() as ctx:
        s = Space(nc, ctx)
        bn = s.sb(name + "_bn", [P, NT, 6])
        mv = s.sb(name + "_mv", [P, NT, 2])
        var = s.sb(name + "_var", [P, NT])
        counted = s.sem(name + "_counted")
        step = s.sem(name + "_step")
        rooted = s.sem(name + "_rooted")
        block = ctx.enter_context(nc.Block())

        @block.scalar
        def _(act):
            act.wait_ge(step, 1)
            act.activation(keep.tscale[:], var[:], ACT.Sqrt).then_inc(rooted, 1)

        @block.vector
        def _(dve):
            with dve.Fori(0, NT) as j:
                dve.bn_stats(bn[:, j, :], keep.t[:, j, :]).then_inc(counted, 1)
            dve.wait_ge(counted, NT)
            for j in range(NT):
                dve.bn_aggr(mv[:, j, :], bn[:, j, :]).then_inc(counted, 1)
            dve.wait_ge(counted, 2 * NT)
            dve.tensor_scalar(var[:], mv[:, :, 1], eps, None, ALU.add).then_inc(step, 1)
            dve.wait_ge(rooted, 1)
            dve.reciprocal(keep.tscale[:], keep.tscale[:]).then_inc(step, 1)
            dve.wait_ge(step, 2)
            dve.scalar_tensor_tensor(keep.tshift[:], mv[:, :, 0], -1.0, keep.tscale[:], ALU.mult, ALU.mult).then_inc(step, 1)


def soft_projections(nc, top, wqkv, wo, q_dram, keep):
    NG = 3 * NH
    with ExitStack() as ctx:
        s = Space(nc, ctx)
        w = s.sb("r_w", [P, 3 * C])
        q_t = s.sb("r_q_t", [P, B * T])
        q_out = s.sem("r_q_out")
        wos = s.sb("r_wo", [P, HD])
        wod = s.sb("r_wod", [P, NH, HD])
        xn = s.sb("r_xn", [P, 2, C])
        xt = s.sb("r_xt", [P, 2, P])
        peak = s.sb("r_peak", [P, 2, NG])
        e = s.sb("r_e", [P, 2, NG, HD])
        total = s.sb("r_total", [P, 2, NG])
        inv = s.sb("r_inv", [P, 2, NG])
        soft = s.sb("r_soft", [P, 2, NG, HD])
        vt = s.sb("r_vt", [P, 2, P])
        ps_x = [s.ps(f"r_ps_x{i}", [P, 512]) for i in range(2)]
        ps_q = [s.ps(f"r_ps_q{i}", [P, 512]) for i in range(2)]
        ps_t = [s.ps(f"r_ps_t{i}", [P, 512]) for i in range(2)]
        ps_v = [s.ps(f"r_ps_v{i}", [P, 512]) for i in range(2)]
        w_in = s.sem("r_w_in")
        spread = s.sem("r_spread")
        normed = s.sem("r_normed")
        turned = s.sem("r_turned")
        xt_ready = s.sem("r_xt_ready")
        projected = s.sem("r_projected")
        peaked = s.sem("r_peaked")
        centred = s.sem("r_centred")
        exped = s.sem("r_exped")
        summed = s.sem("r_summed")
        inverted = s.sem("r_inverted")
        softened = s.sem("r_softened")
        soft_turned = s.sem("r_soft_turned")
        unpacked = s.sem("r_unpacked")
        mixed = s.sem("r_mixed")
        v_ready = s.sem("r_v_ready")
        block = ctx.enter_context(nc.Block())

        @block.sync
        def _(sp):
            sp.dma_start(w[:], wqkv).then_inc(w_in, 16)
            sp.dma_start(wos[:], wo).then_inc(w_in, 16)
            for i in range(4):
                sp.wait_ge(unpacked, 3 * NT // 4 * (i + 1))
                part = slice(i * B * T // 4, (i + 1) * B * T // 4)
                sp.dma_start(q_dram[:, part], q_t[:, part]).then_inc(q_out, 16)
            sp.wait_ge(q_out, 64)

        @block.gpsimd
        def _(pool):
            pool.memset(keep.head8[:], 1.0).then_inc(spread, 1)
            pool.memset(keep.vp[:], 1.0).then_inc(spread, 1)
            pool.wait_ge(w_in, 32)
            pool.tensor_copy(wod[:], wos[:, None, :].to_broadcast([P, NH, HD])).then_inc(spread, 1)
            pool.wait_ge(spread, 3)
            for n, (v, pat) in enumerate(((wod[:], [0, HD]), (keep.head8[:], None))):
                more = [pat] if pat else []
                pool.affine_select(out=v, in_=v, compare_op=ALU.is_ge, fill=0.0, base=0,
                                   pattern=[[-HD, NH]] + more, channel_multiplier=1).then_inc(spread, 1)
            pool.wait_ge(spread, 5)
            for n, (v, pat) in enumerate(((wod[:], [0, HD]), (keep.head8[:], None))):
                more = [pat] if pat else []
                pool.affine_select(out=v, in_=v, compare_op=ALU.is_ge, fill=0.0, base=HD - 1,
                                   pattern=[[HD, NH]] + more, channel_multiplier=-1).then_inc(spread, 1)

        @block.scalar
        def _(act):
            def norm(j, u, early):
                if not early:
                    act.wait_ge(turned, j - 1)
                act.activation(xn[:, u, :], keep.t[:, j, :], ACT.Identity, bias=keep.tshift[:, bass.ds(j, 1)],
                               scale=keep.tscale[:, bass.ds(j, 1)]).then_inc(normed, 1)

            def exp(j, u, early):
                act.wait_ge(centred, j + 1)
                act.activation(e[:, u], e[:, u], ACT.Exp, scale=10.0).then_inc(exped, 1)

            def unpack(j, u, early):
                act.wait_ge(soft_turned, j + 1)
                act.activation(q_t[:, bass.ds(j * P, P)], ps_t[u][:, 0:P], ACT.Copy).then_inc(unpacked, 1)
                act.activation(keep.k_t[:, bass.ds(j * P, P)], ps_t[u][:, P:2 * P], ACT.Copy).then_inc(unpacked, 1)
                if not early:
                    act.wait_ge(mixed, j - 1)
                act.activation(vt[:, u, :], ps_t[u][:, 2 * P:3 * P], ACT.Copy).then_inc(unpacked, 1)

            lagged(act, NT, 2, [(0, norm), (2, unpack), (1, exp)])

        @block.vector
        def _(dve):
            def x_out(j, u, early):
                dve.wait_ge(turned, j + 1)
                if not early:
                    dve.wait_ge(projected, j - 1)
                dve.tensor_copy(xt[:, u, :], ps_x[u][:, 0:P]).then_inc(xt_ready, 1)

            def centre(j, u, early):
                q = ps_q[u][:, 0:3 * C].rearrange("p (g d) -> p g d", d=HD)
                dve.wait_ge(projected, j + 1)
                dve.tensor_reduce(peak[:, u, :], q, AX.X, ALU.max).then_inc(peaked, 1)
                dve.wait_ge(peaked, j + 1)
                if not early:
                    dve.wait_ge(softened, j - 1)
                dve.tensor_tensor(e[:, u], q, peak[:, u, :, None].to_broadcast([P, NG, HD]), ALU.subtract).then_inc(centred, 1)

            def soften(j, u, early):
                dve.wait_ge(exped, j + 1)
                dve.tensor_reduce(total[:, u, :], e[:, u], AX.X, ALU.add).then_inc(summed, 1)
                dve.wait_ge(summed, j + 1)
                dve.reciprocal(inv[:, u, :], total[:, u, :]).then_inc(inverted, 1)
                dve.wait_ge(inverted, j + 1)
                if not early:
                    dve.wait_ge(soft_turned, j - 1)
                dve.tensor_tensor(soft[:, u], e[:, u], inv[:, u, :, None].to_broadcast([P, NG, HD]), ALU.mult).then_inc(softened, 1)

            def v_out(j, u, early):
                dve.wait_ge(mixed, j + 1)
                dve.tensor_copy(keep.vp[:, j, :, 0:HD], ps_v[u][:, 0:C].rearrange("p (h d) -> p h d", d=HD)).then_inc(v_ready, 1)

            dve.wait_ge(spread, 7)
            lagged(dve, NT, 2, [(1, x_out), (2, soften), (1, centre), (3, v_out)])

        @block.tensor
        def _(pe):
            def turn(j, u, early):
                pe.wait_ge(normed, j + 1)
                if not early:
                    pe.wait_ge(xt_ready, j - 1)
                pe.transpose(ps_x[u][:, 0:P], xn[:, u, :], keep.ident[:]).then_inc(turned, 1)

            def project(j, u, early):
                pe.wait_ge(xt_ready, j + 1)
                if not early:
                    pe.wait_ge(centred, j - 1)
                pe.matmul(ps_q[u][:, 0:3 * C], xt[:, u, :], w[:], start=True, stop=True).then_inc(projected, 1)

            def turn_soft(j, u, early):
                pe.wait_ge(softened, j + 1)
                if not early:
                    pe.wait_ge(unpacked, 3 * (j - 1))
                for n in range(3):
                    last = pe.transpose(ps_t[u][:, n * P:(n + 1) * P], soft[:, u, n * NH:(n + 1) * NH, :], keep.ident[:])
                last.then_inc(soft_turned, 1)

            def mix(j, u, early):
                pe.wait_ge(unpacked, 3 * j + 3)
                if not early:
                    pe.wait_ge(v_ready, j - 1)
                pe.matmul(ps_v[u][:, 0:C], vt[:, u, :], wod[:], start=True, stop=True).then_inc(mixed, 1)

            pe.wait_ge(w_in, 32)
            pe.wait_ge(spread, 7)
            lagged(pe, NT, 2, [(1, turn), (2, turn_soft), (1, project), (2, mix)])


QUARTER = 64
GROUP = 4
NGROUP = T // GROUP
PER_Q = QUARTER // GROUP
ZR = 3


def rosa_attention(nc, top, q_dram, keep):
    with ExitStack() as ctx:
        s = Space(nc, ctx)
        held = [s.sb(f"a_held{i}", [P, QUARTER, BH]) for i in range(4)]
        qx = s.sb("a_qx", [P, 2, QUARTER, NH])
        q_in = s.sb("a_q_in", [P, 4, QUARTER])
        iota_i = s.sb("a_iota_i", [P, T], I32)
        iota = s.sb("a_iota", [P, T])
        prior = s.sb("a_prior", [P, 4, T])
        y = s.sb("a_y", [P, 2, T + 1])
        z = s.sb("a_z", [P, ZR, GROUP, T])
        peak = s.sb("a_peak", [P, 2, GROUP])
        bias = s.sb("a_bias", [P, 2, GROUP])
        inv = s.sb("a_inv", [P, 2, NH])
        o = s.sb("a_o", [P, 2, NH, HD])
        ps_row = [s.ps(f"a_ps_row{i}", [P, 2, 512]) for i in range(2)]
        ps_back = [s.ps(f"a_ps_back{i}", [P, 512]) for i in range(2)]
        ps_score = s.ps("a_ps_score", [P, 512])
        ps_o = s.ps("a_ps_o", [P, 512])
        iota_ready = s.sem("a_iota_ready")
        q_loaded = [s.sem(f"a_q_loaded{i}") for i in range(4)]
        cleared = s.sem("a_cleared")
        qx_ready = s.sem("a_qx_ready")
        scored = s.sem("a_scored")
        score_held = s.sem("a_score_held")
        row_turned = s.sem("a_row_turned")
        prior_ready = s.sem("a_prior_ready")
        scanned = s.sem("a_scanned")
        peaked = s.sem("a_peaked")
        bias_ready = s.sem("a_bias_ready")
        exped = s.sem("a_exped")
        back_turned = s.sem("a_back_turned")
        back_act = s.sem("a_back_act")
        back_dve = s.sem("a_back_dve")
        summed = s.sem("a_summed")
        inverted = s.sem("a_inverted")
        scaled = s.sem("a_scaled")
        added = s.sem("a_added")
        block = ctx.enter_context(nc.Block())

        place = [[0], [1], [2, 3], [0, 1]]
        chunks = [1, 1, 2, 2]
        score_no = {}
        for q in range(4):
            for b in range(B):
                for k in range(chunks[q]):
                    score_no[q, b, k] = len(score_no)
        back_no = {}
        for g in range(NGROUP):
            for k in range(chunks[g // PER_Q]):
                back_no[g, k] = len(back_no)

        def before(no):
            return (no + 1) // 2, no // 2

        def sums_at(g):
            q, i = divmod(g, PER_Q)
            return [(q - 1, 2 * (i - 2) + n) for n in range(2)] if q >= 1 and 2 <= i < 10 else []

        def scores_at(g):
            q, i = divmod(g, PER_Q)
            return [(q + 1, 2 * (i - 6) + n) for n in range(2)] if q < 3 and 6 <= i < 14 else []

        last_sums = [(3, b) for b in range(B)]

        @block.tensor
        def _(pe):
            def score(q, b):
                n = B * q + b
                pe.wait_ge(qx_ready, n + 1)
                for k in range(chunks[q]):
                    no = score_no[q, b, k]
                    if no:
                        pe.wait_ge(score_held, no)
                    pe.matmul(ps_score[:], keep.k_t[:, (2 * b + k) * P:(2 * b + k + 1) * P],
                              qx[:, n % 2], start=True, stop=True).then_inc(scored, 1)

            def turn_rows(g):
                q = g // PER_Q
                pe.wait_ge(score_held, score_no[q, B - 1, chunks[q] - 1] + 1)
                if g >= 2:
                    pe.wait_ge(scanned, GROUP * (g - 1))
                for i in range(GROUP):
                    for k in range(chunks[q]):
                        at = (i * chunks[q] + k) * P
                        last = pe.transpose(ps_row[g % 2][:, at // 512, at % 512:at % 512 + P],
                                            held[place[q][k]][:, GROUP * g % QUARTER + i, :], keep.ident[:])
                last.then_inc(row_turned, 1)

            def turn_back(g):
                q = g // PER_Q
                pe.wait_ge(exped, GROUP * (g + 1))
                for k in range(chunks[q]):
                    no = back_no[g, k]
                    if no >= 2:
                        a, d = before(no - 1)
                        if no % 2 == 0:
                            pe.wait_ge(back_act, a)
                        else:
                            pe.wait_ge(back_dve, d)
                    for i in range(GROUP):
                        last = pe.transpose(ps_back[no % 2][:, i * P:(i + 1) * P],
                                            z[:, g % ZR, i, k * P:(k + 1) * P], keep.ident[:])
                    last.then_inc(back_turned, 1)

            def weigh(q, b):
                n = B * q + b
                if b == 0:
                    a, d = before(back_no[PER_Q * q + PER_Q - 1, chunks[q] - 1] + 1)
                    pe.wait_ge(back_act, a)
                    pe.wait_ge(back_dve, d)
                if n:
                    pe.wait_ge(scaled, n)
                rows = slice(QUARTER * (q % 2), QUARTER * (q % 2) + QUARTER)
                for h in range(NH):
                    for k in range(chunks[q]):
                        last = pe.matmul(ps_o[rows, h * (HD + 1):(h + 1) * (HD + 1)], held[place[q][k]][:, :, NH * b + h],
                                         keep.vp[:, 2 * b + k, h, :], start=(k == 0), stop=(k == chunks[q] - 1))
                last.then_inc(summed, 1)

            for b in range(B):
                score(0, b)
            turn_rows(0)
            for g in range(NGROUP):
                if g + 1 < NGROUP:
                    turn_rows(g + 1)
                if g >= 1:
                    turn_back(g - 1)
                for q, b in sums_at(g):
                    weigh(q, b)
                for q, b in scores_at(g):
                    score(q, b)
            turn_back(NGROUP - 1)
            for q, b in last_sums:
                weigh(q, b)

        @block.scalar
        def _(act):
            def hold(q, b):
                for k in range(chunks[q]):
                    act.wait_ge(scored, score_no[q, b, k] + 1)
                    if q == 3:
                        act.wait_ge(summed, B + b + 1)
                    act.activation(held[place[q][k]][:, :, NH * b:NH * b + NH],
                                   ps_score[:].rearrange("p (t h) -> p t h", h=NH), ACT.Copy).then_inc(score_held, 1)

            def back(g):
                q = g // PER_Q
                for k in range(chunks[q]):
                    no = back_no[g, k]
                    if no % 2 == 0:
                        act.wait_ge(back_turned, no + 1)
                        r = GROUP * g % QUARTER
                        act.activation(held[place[q][k]][:, r:r + GROUP, :].rearrange("p a b -> p (a b)"),
                                       ps_back[0][:], ACT.Copy).then_inc(back_act, 1)

            def exp(g):
                act.wait_ge(bias_ready, g + 1)
                for i in range(GROUP):
                    n = GROUP * g + i + 1
                    act.activation(z[:, g % ZR, i, 0:n], z[:, g % ZR, i, 0:n], ACT.Exp, bias=bias[:, g % 2, i:i + 1],
                                   scale=10.0).then_inc(exped, 1)

            for b in range(B):
                hold(0, b)
            act.wait_ge(cleared, 2)
            for g in range(NGROUP):
                if g >= 1:
                    back(g - 1)
                for q, b in scores_at(g):
                    hold(q, b)
                exp(g)
            back(NGROUP - 1)

        @block.vector
        def _(dve):
            def scan(r):
                g, i = divmod(r, GROUP)
                nk = chunks[g // PER_Q]
                if i == 0:
                    dve.wait_ge(row_turned, g + 1)
                if r == 0:
                    dve.wait_ge(cleared, 3)
                else:
                    dve.wait_ge(scanned, r)
                if r >= 2:
                    dve.wait_ge(peaked, r - 1)
                at = i * nk * P
                dve.scalar_tensor_tensor(y[:, r % 2, 1:r + 2], y[:, (r + 1) % 2, 0:r + 1], 1.0,
                                         ps_row[g % 2][:, at // 512, at % 512:at % 512 + r + 1],
                                         ALU.add, ALU.mult).then_inc(scanned, 1)

            def add_prior(r):
                g, i = divmod(r, GROUP)
                if i == 0 and g >= ZR:
                    dve.wait_ge(back_turned, back_no[g - ZR, chunks[(g - ZR) // PER_Q] - 1] + 1)
                if i == 0 and g >= 2:
                    dve.wait_ge(exped, GROUP * (g - 1))
                dve.wait_ge(prior_ready, r + 1)
                dve.wait_ge(scanned, r + 1)
                dve.tensor_tensor_reduce(z[:, g % ZR, i, 0:r + 1], y[:, r % 2, 1:r + 2], prior[:, r % 4, 0:r + 1],
                                         1.0, -3.0e38, ALU.add, ALU.max, peak[:, g % 2, i:i + 1]).then_inc(peaked, 1)

            def back(g):
                q = g // PER_Q
                for k in range(chunks[q]):
                    no = back_no[g, k]
                    if no % 2 == 1:
                        dve.wait_ge(back_turned, no + 1)
                        r = GROUP * g % QUARTER
                        dve.tensor_copy(held[place[q][k]][:, r:r + GROUP, :].rearrange("p a b -> p (a b)"),
                                        ps_back[1][:]).then_inc(back_dve, 1)

            def scale(q, b):
                n = B * q + b
                rows = slice(QUARTER * (q % 2), QUARTER * (q % 2) + QUARTER)
                sums = ps_o[rows, 0:NH * (HD + 1)].rearrange("p (h d) -> p h d", d=HD + 1)
                dve.wait_ge(summed, n + 1)
                dve.reciprocal(inv[rows, n % 2, :], sums[:, :, HD]).then_inc(inverted, 1)
                dve.wait_ge(inverted, n + 1)
                if n >= 2:
                    dve.wait_ge(added, n - 1)
                dve.tensor_tensor(o[rows, n % 2], sums[:, :, 0:HD],
                                  inv[rows, n % 2, :, None].to_broadcast([QUARTER, NH, HD]), ALU.mult).then_inc(scaled, 1)

            for g in range(NGROUP):
                for i in range(GROUP):
                    scan(GROUP * g + i)
                    if g or i:
                        add_prior(GROUP * g + i - 1)
                    if i == 0 and g:
                        dve.wait_ge(peaked, GROUP * g)
                        dve.tensor_scalar(bias[:, (g - 1) % 2, :], peak[:, (g - 1) % 2, :], -10.0, None, ALU.mult).then_inc(bias_ready, 1)
                if g >= 2:
                    back(g - 2)
                for q, b in (sums_at(g - 1) if g else []):
                    scale(q, b)
            add_prior(T - 1)
            dve.wait_ge(peaked, T)
            dve.tensor_scalar(bias[:, (NGROUP - 1) % 2, :], peak[:, (NGROUP - 1) % 2, :], -10.0, None, ALU.mult).then_inc(bias_ready, 1)
            back(NGROUP - 2)
            back(NGROUP - 1)
            for q, b in last_sums:
                scale(q, b)

        @block.sync
        def _(sp):
            for n in range(4 * B):
                q, b = divmod(n, B)
                if n >= 4:
                    sp.wait_ge(qx_ready, n - 3)
                at = T * b + QUARTER * q
                sp.dma_start(q_in[:, n % 4, :], q_dram[:, at:at + QUARTER]).then_inc(q_loaded[n % 4], 16)

        @block.gpsimd
        def _(pool):
            def expand(q, b):
                n = B * q + b
                if n >= 2:
                    p, c = divmod(n - 2, B)
                    pool.wait_ge(scored, score_no[p, c, chunks[p] - 1] + 1)
                pool.wait_ge(q_loaded[n % 4], 16 * (n // 4 + 1))
                pool.tensor_tensor(qx[:, n % 2], q_in[:, n % 4, :, None].to_broadcast([P, QUARTER, NH]),
                                   keep.head8[:, None, :].to_broadcast([P, QUARTER, NH]), ALU.mult).then_inc(qx_ready, 1)

            def position(r):
                if r >= 4:
                    pool.wait_ge(peaked, r - 3)
                pool.tensor_scalar(prior[:, r % 4, 0:r + 1], iota[:, 0:r + 1], 1.0 / (r + 1), None, ALU.mult).then_inc(prior_ready, 1)

            def add(q, b):
                n = B * q + b
                rows = slice(QUARTER * (q % 2), QUARTER * (q % 2) + QUARTER)
                pool.wait_ge(prior_ready, priors)
                pool.wait_ge(qx_ready, expanded)
                pool.wait_ge(scaled, n + 1)
                at = keep.t[rows, 2 * b + q // 2, :].rearrange("p (h d) -> p h d", d=HD)
                pool.tensor_tensor(at, at, o[rows, n % 2], ALU.add).then_inc(added, 1)

            pool.memset(z[:].rearrange("p a b c -> p (a b c)"), 0.0).then_inc(cleared, 1)
            pool.memset(y[:].rearrange("p a b -> p (a b)"), 0.0).then_inc(cleared, 1)
            pool.iota(iota_i[:], pattern=[[1, T]], base=0, channel_multiplier=0).then_inc(iota_ready, 1)
            pool.wait_ge(iota_ready, 1)
            pool.tensor_copy(iota[:], iota_i[:]).then_inc(iota_ready, 1)
            pool.wait_ge(iota_ready, 2)
            pool.memset(bias[:].rearrange("p a b -> p (a b)"), 0.0).then_inc(cleared, 1)
            for r in range(GROUP):
                position(r)
            for b in range(B):
                expand(0, b)
            for g in range(NGROUP):
                if g + 1 < NGROUP:
                    for i in range(GROUP):
                        position(GROUP * (g + 1) + i)
                for q, b in scores_at(g):
                    expand(q, b)
                priors = min(GROUP * (g + 2), T)
                expanded = B + sum(len(scores_at(i)) for i in range(g + 1))
                for q, b in (sums_at(g - 1) if g else []):
                    add(q, b)
                    pool.wait_ge(added, B * q + b + 1)
            for q, b in last_sums:
                add(q, b)
                pool.wait_ge(added, B * q + b + 1)


TOPK = 2
HID = 512
KC = HID // P
SLOTS = 80 * P
XR = 4


class Moe:

    def __init__(self, s, name, experts, swiglu):
        self.name, self.n, self.swiglu = name, experts, swiglu
        self.tiles = (B * T * TOPK // P + experts) // 2 * 2
        self.up = [s.sb(f"{name}_up{i}", [P, experts, HID]) for i in range(2 if swiglu else 1)]
        self.down = s.sb(f"{name}_down", [P, experts, KC, C])
        if not swiglu:
            self.b1 = s.sb(f"{name}_b1", [P, experts, HID])
            self.b2 = s.sb(f"{name}_b2", [P, experts, C])
        self.slot = s.sb(f"{name}_slot", [P, NT, TOPK], U32)
        self.weight = s.sb(f"{name}_weight", [P, TOPK, NT])
        self.of_tile = s.sb(f"{name}_of_tile", [P, self.tiles], I32)
        self.up_in = [s.sem(f"{name}_up_in{i}") for i in range(2)]
        self.down_in = s.sem(f"{name}_down_in")


def load_experts(sp, m, up, down, b1=None, b2=None):
    half = m.n // 2
    for lot in range(2):
        part = slice(lot * half, (lot + 1) * half)
        for dst, src in zip(m.up, up):
            sp.dma_start(dst[:, part], src[:, part]).then_inc(m.up_in[lot], 16)
        sp.dma_start(m.down[:, part], down[:, part]).then_inc(m.down_in, 16)
    if b1 is not None:
        sp.dma_start(m.b1[:], b1[None, :, :].to_broadcast([P, m.n, HID])).then_inc(m.down_in, 16)
        sp.dma_start(m.b2[:], b2[None, :, :].to_broadcast([P, m.n, C])).then_inc(m.down_in, 16)


def route(nc, top, m, router, loads, xn, keep):
    E, N = m.n, NT * m.n
    name = m.name
    with ExitStack() as ctx:
        s = Space(nc, ctx)

        def sb(what, shape, dt=F32):
            return s.sb(f"{name}_{what}", shape, dt)

        def sem(what):
            return s.sem(f"{name}_{what}")

        w = sb("router", [P, E])
        xs = sb("xs", [P, 2, C])
        xt = sb("xt", [P, 2, P])
        lg = sb("lg", [P, NT, E])
        low = sb("low", [P, NT, E])
        pick = [sb(f"pick{k}", [P, NT, E]) for k in range(TOPK)]
        both = sb("both", [P, NT, E])
        tmp = sb("tmp", [P, NT, E])
        run = [sb(f"run{i}", [P, E, NT]) for i in range(2)]
        own = sb("own", [P, E, NT])
        at = sb("at", [P, NT])
        inv = sb("inv", [P, NT])
        idx = sb("idx", [P, NT])
        slot_f = sb("slot_f", [P, NT, TOPK])
        order_i = sb("order_i", [P, E], I32)
        order = sb("order", [P, E])
        number_i = sb("number_i", [P, m.tiles], I32)
        number = sb("number", [P, m.tiles])
        before = sb("before", [P, P])
        count = sb("count", [P, E])
        whole_i = sb("whole_i", [P, E], I32)
        whole = sb("whole", [P, E])
        end = [sb(f"end{i}", [P, E]) for i in range(2)]
        first = sb("first", [P, E])
        passed = sb("passed", [P, m.tiles, E])
        of_f = sb("of_f", [P, m.tiles])
        ps_x = [s.ps(f"{name}_ps_x{i}", [P, 512]) for i in range(2)]
        ps_l = [s.ps(f"{name}_ps_l{i}", [P, 512]) for i in range(2)]
        ps_in = s.ps(f"{name}_ps_in", [P, 512])
        ps_all = s.ps(f"{name}_ps_all", [P, 512])
        w_in, const = sem("w_in"), sem("const")
        normed, turned, xt_ready, logits, lg_ready = (sem(x) for x in ("normed", "turned", "xt_ready", "logits", "lg_ready"))
        step, exped, ranked = sem("step"), sem("exped"), sem("ranked")
        block = ctx.enter_context(nc.Block())

        @block.sync
        def _(sp):
            sp.dma_start(w[:], router).then_inc(w_in, 16)
            loads(sp)

        @block.gpsimd
        def _(pool):
            pool.memset(before[:], 1.0).then_inc(const, 1)
            pool.iota(order_i[:], pattern=[[1, E]], base=-64, channel_multiplier=0).then_inc(const, 1)
            pool.iota(number_i[:], pattern=[[1, m.tiles]], base=0, channel_multiplier=0).then_inc(const, 1)
            pool.wait_ge(const, 3)
            pool.affine_select(out=before[:], in_=before[:], compare_op=ALU.is_gt, fill=0.0, base=0,
                               pattern=[[1, P]], channel_multiplier=-1).then_inc(const, 1)
            pool.tensor_copy(order[:], order_i[:]).then_inc(const, 1)
            pool.tensor_copy(number[:], number_i[:]).then_inc(const, 1)

        @block.scalar
        def _(act):
            def norm(j, u, early):
                scale, shift = keep.tscale[:, bass.ds(j, 1)], keep.tshift[:, bass.ds(j, 1)]
                if not early:
                    act.wait_ge(turned, j - 1)
                act.activation(xs[:, u, :], keep.t[:, j, :], ACT.Identity, bias=shift, scale=scale).then_inc(normed, 1)
                act.activation(xn[:, j, :], keep.t[:, j, :], ACT.Identity, bias=shift, scale=scale).then_inc(normed, 1)

            in_turn(act, NT, 2, norm)
            act.wait_ge(step, 2)
            act.activation(lg[:], lg[:], ACT.Exp).then_inc(exped, 1)

        @block.tensor
        def _(pe):
            def turn(j, u, early):
                pe.wait_ge(normed, 2 * j + 1)
                if not early:
                    pe.wait_ge(xt_ready, j - 1)
                pe.transpose(ps_x[u][:, 0:P], xs[:, u, :], keep.ident[:]).then_inc(turned, 1)

            def project(j, u, early):
                pe.wait_ge(xt_ready, j + 1)
                if not early:
                    pe.wait_ge(lg_ready, j - 1)
                pe.matmul(ps_l[u][:, 0:E], xt[:, u, :], w[:], start=True, stop=True).then_inc(logits, 1)

            pe.wait_ge(w_in, 16)
            lagged(pe, NT, 2, [(0, turn), (1, project)])
            pe.wait_ge(ranked, 1)
            pe.wait_ge(const, 6)
            pe.matmul(ps_in[:, 0:N], before[:], both[:].rearrange("p a b -> p (a b)"), start=True, stop=True).then_inc(ranked, 1)
            pe.matmul(ps_all[:, 0:N], keep.ones[:], both[:].rearrange("p a b -> p (a b)"), start=True, stop=True).then_inc(ranked, 1)

        @block.vector
        def _(dve):
            def x_out(j, u, early):
                dve.wait_ge(turned, j + 1)
                if not early:
                    dve.wait_ge(logits, j - 1)
                dve.tensor_copy(xt[:, u, :], ps_x[u][:, 0:P]).then_inc(xt_ready, 1)

            def logits_out(j, u, early):
                dve.wait_ge(logits, j + 1)
                dve.tensor_copy(lg[:, j, :], ps_l[u][:, 0:E]).then_inc(lg_ready, 1)

            lagged(dve, NT, 2, [(0, x_out), (1, logits_out)])
            dve.wait_ge(lg_ready, NT)
            dve.wait_ge(const, 6)
            done = [0]

            def then(ins):
                ins.then_inc(step, 1)
                done[0] += 1
                dve.wait_ge(step, done[0])

            def over(v):
                return v[:, :, None].to_broadcast([P, NT, E])

            orders = order[:, None, :].to_broadcast([P, NT, E])
            then(dve.tensor_reduce(at[:], lg[:], AX.X, ALU.max))
            then(dve.tensor_tensor(lg[:], lg[:], over(at), ALU.subtract))
            dve.wait_ge(exped, 1)
            then(dve.tensor_reduce(at[:], lg[:], AX.X, ALU.add))
            then(dve.reciprocal(inv[:], at[:]))
            then(dve.tensor_tensor(lg[:], lg[:], over(inv), ALU.mult))
            for k in range(TOPK):
                then(dve.tensor_reduce(m.weight[:, k, :], lg[:], AX.X, ALU.max))
                then(dve.tensor_tensor(tmp[:], lg[:], over(m.weight[:, k, :]), ALU.is_equal))
                then(dve.tensor_tensor(low[:], tmp[:], orders, ALU.mult))
                then(dve.tensor_reduce(idx[:], low[:], AX.X, ALU.min))
                then(dve.tensor_tensor(pick[k][:], orders, over(idx), ALU.is_equal))
                if k == 0:
                    then(dve.scalar_tensor_tensor(lg[:], pick[0][:], -4.0, lg[:], ALU.mult, ALU.add))
            dve.tensor_tensor(both[:], pick[0][:], pick[1][:], ALU.add).then_inc(ranked, 1)
            if not m.swiglu:
                then(dve.tensor_tensor(at[:], m.weight[:, 0, :], m.weight[:, 1, :], ALU.add))
                then(dve.reciprocal(inv[:], at[:]))
                then(dve.tensor_tensor(m.weight[:], m.weight[:], inv[:, None, :].to_broadcast([P, TOPK, NT]), ALU.mult))
            dve.wait_ge(ranked, 3)
            then(dve.tensor_copy(own[:], ps_all[:, 0:N].rearrange("p (j e) -> p e j", e=E)))
            src, n, d = own, 0, 1
            while d < NT:
                dst = run[n % 2]
                then(dve.tensor_copy(dst[:, :, 0:d], src[:, :, 0:d]))
                then(dve.tensor_tensor(dst[:, :, d:], src[:, :, d:], src[:, :, 0:NT - d], ALU.add))
                src, n, d = dst, n + 1, 2 * d
            then(dve.tensor_scalar(count[:], src[:, :, NT - 1], float(P - 1), None, ALU.add))
            then(dve.tensor_copy(whole_i[:], count[:]))
            then(dve.tensor_scalar(whole_i[:], whole_i[:], 7, None, ALU.arith_shift_right))
            then(dve.tensor_copy(whole[:], whole_i[:]))
            ends, n, d = whole, 0, 1
            while d < E:
                dst = end[n % 2]
                then(dve.tensor_copy(dst[:, 0:d], ends[:, 0:d]))
                then(dve.tensor_tensor(dst[:, d:], ends[:, d:], ends[:, 0:E - d], ALU.add))
                ends, n, d = dst, n + 1, 2 * d
            then(dve.tensor_tensor(first[:], ends[:], whole[:], ALU.subtract))
            then(dve.tensor_tensor(own[:], src[:], own[:], ALU.subtract))
            then(dve.scalar_tensor_tensor(own[:], first[:, :, None].to_broadcast([P, E, NT]), float(P), own[:], ALU.mult, ALU.add))
            then(dve.tensor_tensor(both[:], ps_in[:, 0:N].rearrange("p (j e) -> p j e", e=E),
                                   own[:].rearrange("p e j -> p j e"), ALU.add))
            for k in range(TOPK):
                then(dve.tensor_tensor(tmp[:], both[:], pick[k][:], ALU.mult))
                then(dve.tensor_reduce(slot_f[:, :, k], tmp[:], AX.X, ALU.add))
            then(dve.tensor_copy(m.slot[:], slot_f[:]))
            then(dve.tensor_tensor(passed[:], number[:, :, None].to_broadcast([P, m.tiles, E]),
                                   ends[:, None, :].to_broadcast([P, m.tiles, E]), ALU.is_ge))
            then(dve.tensor_reduce(of_f[:], passed[:], AX.X, ALU.add))
            then(dve.tensor_scalar(of_f[:], of_f[:], float(E - 1), None, ALU.min))
            then(dve.tensor_copy(m.of_tile[:], of_f[:]))


def dispatch(nc, top, m, xs_dram, xn, shared, keep):
    with ExitStack() as ctx:
        s = Space(nc, ctx)
        sent = [s.sem(f"{m.name}_sent{i}") for i in range(4)]
        if shared is not None:
            up, down = shared
            H = up.shape[1] // 2
            HC = H // P
            ws = s.sb("sh_up", [P, 2 * H])
            wd = s.sb("sh_down", [P, HC, C])
            xs = s.sb("sh_xs", [P, 2, C])
            xt = s.sb("sh_xt", [P, 2, P])
            act_g = s.sb("sh_act", [P, 2, H])
            hid = s.sb("sh_hid", [P, 2, H])
            ht = s.sb("sh_ht", [P, 2, HC, P])
            ps_x = [s.ps(f"sh_ps_x{i}", [P, 512]) for i in range(2)]
            ps_u = [s.ps(f"sh_ps_u{i}", [P, 512]) for i in range(2)]
            ps_h = [s.ps(f"sh_ps_h{i}", [P, 512]) for i in range(2)]
            ps_y = [s.ps(f"sh_ps_y{i}", [P, 512]) for i in range(2)]
            w_in, staged, turned, xt_ready, upped, silued, multiplied, h_turned, ht_ready, downed, added = (
                s.sem("sh_" + x) for x in ("w_in", "staged", "turned", "xt_ready", "upped", "silued", "multiplied",
                                           "h_turned", "ht_ready", "downed", "added"))
        block = ctx.enter_context(nc.Block())

        @block.gpsimd
        def _(pool):
            for j in range(NT):
                for k in range(TOPK):
                    n = TOPK * j + k
                    pool.indirect_dma_start(xs_dram, bass.IndirectOffsetOnAxis(m.slot[:, j, k:k + 1], 0),
                                            xn[:, j, :], None).then_inc(sent[n % 4], 16)
            for i in range(4):
                pool.wait_ge(sent[i], 16 * NT * TOPK // 4)

        if shared is None:
            return

        @block.sync
        def _(sp):
            sp.dma_start(ws[:], up).then_inc(w_in, 16)
            sp.dma_start(wd[:], down).then_inc(w_in, 16)

        @block.scalar
        def _(act):
            def stage(j, u, early):
                if not early:
                    act.wait_ge(turned, j - 1)
                act.activation(xs[:, u, :], xn[:, j, :], ACT.Copy).then_inc(staged, 1)

            def silu(j, u, early):
                act.wait_ge(upped, j + 1)
                if not early:
                    act.wait_ge(multiplied, j - 1)
                act.activation(act_g[:, u, :], ps_u[u][:, 0:H], ACT.Silu).then_inc(silued, 1)

            def h_out(j, u, early):
                act.wait_ge(h_turned, j + 1)
                if not early:
                    act.wait_ge(downed, j - 1)
                act.activation(ht[:, u], ps_h[u][:, 0:H].rearrange("p (a b) -> p a b", b=P), ACT.Copy).then_inc(ht_ready, 1)

            lagged(act, NT, 2, [(0, stage), (2, h_out), (1, silu)])

        @block.vector
        def _(dve):
            def x_out(j, u, early):
                dve.wait_ge(turned, j + 1)
                if not early:
                    dve.wait_ge(upped, j - 1)
                dve.tensor_copy(xt[:, u, :], ps_x[u][:, 0:P]).then_inc(xt_ready, 1)

            def multiply(j, u, early):
                dve.wait_ge(silued, j + 1)
                if not early:
                    dve.wait_ge(h_turned, j - 1)
                dve.tensor_tensor(hid[:, u, :], act_g[:, u, :], ps_u[u][:, H:2 * H], ALU.mult).then_inc(multiplied, 1)

            def add(j, u, early):
                dve.wait_ge(downed, j + 1)
                dve.tensor_tensor(keep.t[:, j, :], keep.t[:, j, :], ps_y[u][:, 0:C], ALU.add).then_inc(added, 1)

            lagged(dve, NT, 2, [(0, x_out), (1, multiply), (3, add)])

        @block.tensor
        def _(pe):
            def turn(j, u, early):
                pe.wait_ge(staged, j + 1)
                if not early:
                    pe.wait_ge(xt_ready, j - 1)
                pe.transpose(ps_x[u][:, 0:P], xs[:, u, :], keep.ident[:]).then_inc(turned, 1)

            def up_(j, u, early):
                pe.wait_ge(xt_ready, j + 1)
                if not early:
                    pe.wait_ge(multiplied, j - 1)
                pe.matmul(ps_u[u][:, 0:2 * H], xt[:, u, :], ws[:], start=True, stop=True).then_inc(upped, 1)

            def turn_h(j, u, early):
                pe.wait_ge(multiplied, j + 1)
                if not early:
                    pe.wait_ge(ht_ready, j - 1)
                for k in range(HC):
                    last = pe.transpose(ps_h[u][:, k * P:(k + 1) * P], hid[:, u, k * P:(k + 1) * P], keep.ident[:])
                last.then_inc(h_turned, 1)

            def down_(j, u, early):
                pe.wait_ge(ht_ready, j + 1)
                if not early:
                    pe.wait_ge(added, j - 1)
                for k in range(HC):
                    last = pe.matmul(ps_y[u][:, 0:C], ht[:, u, k, :], wd[:, k, :], start=(k == 0), stop=(k == HC - 1))
                last.then_inc(downed, 1)

            pe.wait_ge(w_in, 32)
            lagged(pe, NT, 2, [(0, turn), (2, turn_h), (1, up_), (3, down_)])


def experts(nc, top, m, xs_dram, ys_dram, keep):
    name, M = m.name, m.tiles
    with ExitStack() as ctx:
        s = Space(nc, ctx)
        xin = s.sb(f"{name}_xin", [P, XR, C])
        xt = s.sb(f"{name}_ext", [P, 2, P])
        act_g = s.sb(f"{name}_act", [P, 2, HID])
        hid = s.sb(f"{name}_hid", [P, 2, HID])
        ht = s.sb(f"{name}_ht", [P, 2, KC, P])
        yout = s.sb(f"{name}_yout", [P, XR, C])
        ps_x = s.ps(f"{name}_eps_x", [P, 512])
        ps_y = s.ps(f"{name}_eps_y", [P, 512])
        ps_h = [s.ps(f"{name}_eps_h{i}", [P, 512]) for i in range(2)]
        ps_g = [s.ps(f"{name}_eps_g{i}", [P, 512]) for i in range(2)]
        ps_u = [s.ps(f"{name}_eps_u{i}", [P, 512]) for i in range(2)] if m.swiglu else ps_g
        loaded = [s.sem(f"{name}_loaded{i}") for i in range(XR)]
        stored = [s.sem(f"{name}_stored{i}") for i in range(XR)]
        turned, xt_ready, upped, silued, hid_ready, h_turned, ht_ready, downed, y_ready = (
            s.sem(f"{name}_e_" + x) for x in ("turned", "xt_ready", "upped", "silued", "hid_ready", "h_turned",
                                              "ht_ready", "downed", "y_ready"))
        block = ctx.enter_context(nc.Block())

        def expert(eng, j):
            return eng.value_load(m.of_tile[0:1, bass.ds(j, 1)], min_val=0, max_val=m.n - 1)

        @block.sync
        def _(sp):
            def load(j, u, early):
                if not early:
                    sp.wait_ge(turned, j - XR + 1)
                sp.dma_start(xin[:, u, :], xs_dram[bass.ds(j * P, P), :]).then_inc(loaded[u], 16)

            in_turn(sp, M, XR, load)

        @block.gpsimd
        def _(pool):
            def store(j, u, early):
                pool.wait_ge(y_ready, j + 1)
                pool.dma_start(ys_dram[bass.ds(j * P, P), :], yout[:, u, :]).then_inc(stored[u], 16)

            in_turn(pool, M, XR, store)
            for u in range(XR):
                pool.wait_ge(stored[u], 16 * M // XR)

        @block.tensor
        def _(pe):
            def turn(j, u, early):
                pe.wait_ge(loaded[u], 4 * (j - u) + 16)
                if not isinstance(j, int) or j:
                    pe.wait_ge(xt_ready, j)
                pe.transpose(ps_x[:, 0:P], xin[:, u, :], keep.ident[:]).then_inc(turned, 1)

            def up(j, u, early):
                e = expert(pe, j)
                pe.wait_ge(xt_ready, j + 1)
                if not early:
                    pe.wait_ge(hid_ready, j - 1)
                for ps, w in zip((ps_g[u % 2], ps_u[u % 2]), m.up):
                    last = pe.matmul(ps[:], xt[:, u % 2, :], w[:, e, :], start=True, stop=True)
                last.then_inc(upped, 1)

            def turn_h(j, u, early):
                pe.wait_ge(hid_ready, j + 1)
                if not early:
                    pe.wait_ge(ht_ready, j - 1)
                for k in range(KC):
                    last = pe.transpose(ps_h[u % 2][:, k * P:(k + 1) * P], hid[:, u % 2, k * P:(k + 1) * P], keep.ident[:])
                last.then_inc(h_turned, 1)

            def down(j, u, early):
                e = expert(pe, j)
                pe.wait_ge(ht_ready, j + 1)
                if not isinstance(j, int) or j:
                    pe.wait_ge(y_ready, j)
                for k in range(KC):
                    last = pe.matmul(ps_y[:, 0:C], ht[:, u % 2, k, :], m.down[:, e, k, :], start=(k == 0), stop=(k == KC - 1))
                last.then_inc(downed, 1)

            for lot in range(2):
                pe.wait_ge(m.up_in[lot], 16 * len(m.up))
            pe.wait_ge(m.down_in, 16 * (2 if m.swiglu else 4))
            lagged(pe, M, XR, [(0, turn), (2, turn_h), (1, up), (3, down)])

        @block.scalar
        def _(act):
            def silu(j, u, early):
                act.wait_ge(upped, j + 1)
                if not early:
                    act.wait_ge(hid_ready, j - 1)
                act.activation(act_g[:, u % 2, :], ps_g[u % 2][:], ACT.Silu).then_inc(silued, 1)

            def h_out(j, u, early):
                act.wait_ge(h_turned, j + 1)
                if not early:
                    act.wait_ge(downed, j - 1)
                act.activation(ht[:, u % 2], ps_h[u % 2][:].rearrange("p (a b) -> p a b", b=P),
                               ACT.Copy if m.swiglu else ACT.Relu).then_inc(ht_ready, 1)

            lagged(act, M, XR, [(2, h_out), (1, silu)] if m.swiglu else [(2, h_out)])

        @block.vector
        def _(dve):
            def x_out(j, u, early):
                dve.wait_ge(turned, j + 1)
                if not early:
                    dve.wait_ge(upped, j - 1)
                dve.tensor_copy(xt[:, u % 2, :], ps_x[:, 0:P]).then_inc(xt_ready, 1)

            def hidden(j, u, early):
                if not m.swiglu:
                    e = expert(dve, j)
                dve.wait_ge(silued if m.swiglu else upped, j + 1)
                if not early:
                    dve.wait_ge(h_turned, j - 1)
                if m.swiglu:
                    dve.tensor_tensor(hid[:, u % 2, :], act_g[:, u % 2, :], ps_u[u % 2][:], ALU.mult).then_inc(hid_ready, 1)
                else:
                    dve.tensor_tensor(hid[:, u % 2, :], ps_g[u % 2][:], m.b1[:, e, :], ALU.add).then_inc(hid_ready, 1)

            def y_out(j, u, early):
                if not m.swiglu:
                    e = expert(dve, j)
                dve.wait_ge(downed, j + 1)
                if not early:
                    dve.wait_ge(stored[u], 4 * (j - u))
                if m.swiglu:
                    dve.tensor_copy(yout[:, u, :], ps_y[:, 0:C]).then_inc(y_ready, 1)
                else:
                    dve.tensor_tensor(yout[:, u, :], ps_y[:, 0:C], m.b2[:, e, :], ALU.add).then_inc(y_ready, 1)

            if not m.swiglu:
                dve.wait_ge(m.down_in, 16 * 4)
            lagged(dve, M, XR, [(0, x_out), (1, hidden), (3, y_out)])


def combine(nc, top, m, ys_dram, keep):
    name = m.name
    with ExitStack() as ctx:
        s = Space(nc, ctx)
        y = s.sb(f"{name}_y", [P, 4, TOPK, C])
        fetched = [[s.sem(f"{name}_fetched{u}_{k}") for k in range(TOPK)] for u in range(4)]
        added = s.sem(f"{name}_added")
        block = ctx.enter_context(nc.Block())

        @block.gpsimd
        def _(pool):
            for j in range(NT):
                if j >= 4:
                    pool.wait_ge(added, TOPK * (j - 3))
                for k in range(TOPK):
                    pool.indirect_dma_start(y[:, j % 4, k, :], None, ys_dram[0:m.tiles * P, :],
                                            bass.IndirectOffsetOnAxis(m.slot[:, j, k:k + 1], 0)).then_inc(fetched[j % 4][k], 16)

        @block.vector
        def _(dve):
            def tile(j, u, early):
                for k in range(TOPK):
                    dve.wait_ge(fetched[u][k], 4 * (j - u) + 16)
                    if k or not isinstance(j, int) or j:
                        dve.wait_ge(added, TOPK * j + k)
                    dve.scalar_tensor_tensor(keep.t[:, j, :], y[:, u, k, :], m.weight[:, k, bass.ds(j, 1)],
                                             keep.t[:, j, :], ALU.mult, ALU.add).then_inc(added, 1)

            in_turn(dve, NT, 4, tile)


UN = 6


def timetable(eng, parts):
    most = max(lag + (UN - 1 if each else 0) for lag, each, _ in parts)
    span = 2 * UN
    first = -(-(most + span) // span) * span

    def step(base, u, static):
        for lag, each, body in parts:
            ahead, i = divmod(u - lag, UN)
            if not each and i:
                continue
            if static:
                if 0 <= ahead < B:
                    body(ahead, i, ahead % 2, ahead < 2)
            else:
                body(base + ahead, i, ahead % 2, False)

    for n in range(first):
        step(0, n, True)
    with eng.Fori(first // span, B // 2) as k:
        for u in range(span):
            step(2 * k, u, False)
    for n in range(B * UN, B * UN + most + 1):
        step(0, n, True)


def causal_attention(nc, top, wqk, wv, wout, keep):
    with ExitStack() as ctx:
        s = Space(nc, ctx)
        wqk_s = s.sb("c_wqk", [P, 2 * C])
        wv_s = s.sb("c_wv", [P, C])
        wout_s = s.sb("c_wout", [P, C])
        ident_b = s.sb("c_ident_b", [P, P], BF16)
        mask = s.sb("c_mask", [P, 2, 512], BF16)
        xn = s.sb("c_xn", [P, 2, 2, C])
        xt = s.sb("c_xt", [P, 2, T])
        q = s.sb("c_q", [P, 2, T])
        k_ = s.sb("c_k", [P, 2, T])
        kx = s.sb("c_kx", [P, 2, NH, T])
        vx = s.sb("c_vx", [P, 2, 2, NH, HD + 1])
        peak = s.sb("c_peak", [P, 2, 4])
        e = s.sb("c_e", [P, 3, 512])
        pt = s.sb("c_pt", [P, 2, 512])
        inv = s.sb("c_inv", [P, 2, 2 * NH])
        on = s.sb("c_on", [P, 2, 2 * NH, HD])
        ot = s.sb("c_ot", [P, 2, 2, P])
        ps_x = s.ps("c_ps_x", [P, 512])
        ps_qk = s.ps("c_ps_qk", [P, 512])
        ps_v = s.ps("c_ps_v", [P, 512])
        ps_o = s.ps("c_ps_o", [P, 512])
        ps_s = [s.ps(f"c_ps_s{i}", [P, 512]) for i in range(2)]
        ps_t = [s.ps(f"c_ps_t{i}", [P, 512]) for i in range(2)]
        (w_in, const, normed, turned, xt_ready, qk_done, v_done, qk_out, v_out, kx_ready, scored, peaked, centred,
         exped, e_turned, back_act, back_dve, weighed, inverted, o_ready, o_turned, ot_ready, y_done, added) = (
            s.sem("c_" + x) for x in ("w_in", "const", "normed", "turned", "xt_ready", "qk_done", "v_done", "qk_out",
                                      "v_out", "kx_ready", "scored", "peaked", "centred", "exped", "e_turned",
                                      "back_act", "back_dve", "weighed", "inverted", "o_ready", "o_turned",
                                      "ot_ready", "y_done", "added"))
        block = ctx.enter_context(nc.Block())

        def unit(i):
            return (0, 4 * i, 4, P) if i < 2 else (1, 2 * (i - 2), 2, T)

        def least(b, n):
            return min(b + n, B) if isinstance(b, int) else b + n

        @block.sync
        def _(sp):
            for dst, src in ((wqk_s, wqk), (wv_s, wv), (wout_s, wout)):
                sp.dma_start(dst[:], src).then_inc(w_in, 16)

        @block.gpsimd
        def _(pool):
            pool.tensor_copy(ident_b[:], keep.ident[:]).then_inc(const, 1)
            pool.memset(mask[:].rearrange("p a b -> p (a b)"), 0.0).then_inc(const, 1)
            pool.memset(vx[:].rearrange("p a b c d -> p (a b c d)"), 1.0).then_inc(const, 1)
            pool.wait_ge(const, 3)
            pool.affine_select(out=mask[:, 0, :].rearrange("p (a b) -> p a b", b=P), in_=mask[:, 0, :].rearrange("p (a b) -> p a b", b=P),
                               compare_op=ALU.is_ge, fill=-1e30, base=0, pattern=[[0, 4], [-1, P]],
                               channel_multiplier=1).then_inc(const, 1)
            pool.affine_select(out=mask[:, 1, :].rearrange("p (a b) -> p a b", b=T), in_=mask[:, 1, :].rearrange("p (a b) -> p a b", b=T),
                               compare_op=ALU.is_ge, fill=-1e30, base=P, pattern=[[0, 2], [-1, T]],
                               channel_multiplier=1).then_inc(const, 1)

            def spread(b, i, u, early):
                pool.wait_ge(qk_out, 2 * b + 2)
                if not early:
                    pool.wait_ge(scored, UN * (b - 1))
                pool.tensor_tensor(kx[:, u], k_[:, u, None, :].to_broadcast([P, NH, T]),
                                   keep.head8[:, :, None].to_broadcast([P, NH, T]), ALU.mult).then_inc(kx_ready, 1)

            timetable(pool, [(3, False, spread)])

        @block.scalar
        def _(act):
            def norm(b, i, u, early):
                if not early:
                    act.wait_ge(turned, b - 1)
                for h in range(2):
                    j = 2 * b + h
                    act.activation(xn[:, u, h, :], keep.t[:, j, :], ACT.Identity, bias=keep.tshift[:, bass.ds(j, 1)],
                                   scale=keep.tscale[:, bass.ds(j, 1)]).then_inc(normed, 1)

            def qk(b, i, u, early):
                act.wait_ge(qk_done, b + 1)
                if not early:
                    act.wait_ge(scored, UN * (b - 1))
                    act.wait_ge(kx_ready, b - 1)
                act.activation(q[:, u, :], ps_qk[:, 0:T], ACT.Copy).then_inc(qk_out, 1)
                act.activation(k_[:, u, :], ps_qk[:, T:2 * T], ACT.Copy).then_inc(qk_out, 1)

            def exp(b, i, u, early):
                act.wait_ge(centred, UN * b + i + 1)
                act.activation(e[:, i % 3, :], e[:, i % 3, :], ACT.Exp, scale=float(HD) ** -0.5).then_inc(exped, 1)

            def back(b, i, u, early):
                if i % 2 == 0:
                    act.wait_ge(e_turned, UN * b + i + 1)
                    if not early:
                        act.wait_ge(weighed, UN * b + i - 1)
                    elif UN * b + i >= 2:
                        act.wait_ge(weighed, UN * b + i - 1)
                    act.activation(pt[:, 0, :], ps_t[0][:], ACT.Copy).then_inc(back_act, 1)

            def ot_out(b, i, u, early):
                act.wait_ge(o_turned, b + 1)
                if not early:
                    act.wait_ge(y_done, b - 1)
                act.activation(ot[:, u].rearrange("p a b -> p (a b)"), ps_x[:, 0:T], ACT.Copy).then_inc(ot_ready, 1)

            timetable(act, [(0, False, norm), (3, False, qk), (9, True, back), (7, True, exp), (17, False, ot_out)])

        @block.vector
        def _(dve):
            def x_out(b, i, u, early):
                dve.wait_ge(turned, b + 1)
                if not early:
                    dve.wait_ge(v_done, b - 1)
                dve.tensor_copy(xt[:, u, :], ps_x[:, 0:T]).then_inc(xt_ready, 1)

            def v(b, i, u, early):
                dve.wait_ge(v_done, b + 1)
                if not early:
                    dve.wait_ge(weighed, UN * (b - 1))
                dve.tensor_copy(vx[:, u].rearrange("p a b c -> p (a b) c")[:, :, 0:HD],
                                ps_v[:, 0:2 * C].rearrange("p (a d) -> p a d", d=HD)).then_inc(v_out, 1)

            def centre(b, i, u, early):
                _, _, heads, keys = unit(i)
                n = UN * b + i
                sc = ps_s[i % 2][:].rearrange("p (h s) -> p h s", s=keys)
                dve.wait_ge(scored, n + 1)
                dve.tensor_reduce(peak[:, i % 2, 0:heads], sc, AX.X, ALU.max).then_inc(peaked, 1)
                dve.wait_ge(peaked, n + 1)
                if not early or UN * b + i >= 3:
                    dve.wait_ge(e_turned, n - 2)
                dve.tensor_tensor(e[:, i % 3, :].rearrange("p (h s) -> p h s", s=keys), sc,
                                  peak[:, i % 2, 0:heads, None].to_broadcast([P, heads, keys]), ALU.subtract).then_inc(centred, 1)

            def back(b, i, u, early):
                if i % 2 == 1:
                    dve.wait_ge(e_turned, UN * b + i + 1)
                    if not early or UN * b + i >= 2:
                        dve.wait_ge(weighed, UN * b + i - 1)
                    dve.tensor_copy(pt[:, 1, :], ps_t[1][:]).then_inc(back_dve, 1)

            def o_norm(b, i, u, early):
                sums = ps_o[:, 0:2 * NH * (HD + 1)].rearrange("p (g d) -> p g d", d=HD + 1)
                dve.wait_ge(weighed, UN * b + UN)
                dve.reciprocal(inv[:, u, :], sums[:, :, HD]).then_inc(inverted, 1)
                dve.wait_ge(inverted, b + 1)
                if not early:
                    dve.wait_ge(o_turned, b - 1)
                dve.tensor_tensor(on[:, u], sums[:, :, 0:HD], inv[:, u, :, None].to_broadcast([P, 2 * NH, HD]), ALU.mult).then_inc(o_ready, 1)

            def add(b, i, u, early):
                rows = keep.t[:, bass.ds(2 * b, 2), :]
                dve.wait_ge(y_done, b + 1)
                dve.tensor_tensor(rows, rows, ps_v[:, 0:2 * C].rearrange("p (a b) -> p a b", b=C), ALU.add).then_inc(added, 1)

            dve.wait_ge(const, 5)
            timetable(dve, [(1, False, x_out), (3, False, v), (9, True, back), (7, True, centre), (16, False, o_norm),
                            (18, False, add)])

        @block.tensor
        def _(pe):
            def turn_x(b, i, u, early):
                pe.wait_ge(normed, 2 * b + 2)
                if not early:
                    if not isinstance(b, int) or b >= 3:
                        pe.wait_ge(ot_ready, b - 2)
                if not isinstance(b, int) or b:
                    pe.wait_ge(xt_ready, b)
                for h in range(2):
                    last = pe.transpose(ps_x[:, h * P:(h + 1) * P], xn[:, u, h, :], keep.ident[:])
                last.then_inc(turned, 1)

            def project(b, i, u, early):
                pe.wait_ge(xt_ready, b + 1)
                if not isinstance(b, int) or b:
                    pe.wait_ge(qk_out, 2 * b)
                    pe.wait_ge(v_out, b)
                if not isinstance(b, int) or b >= 3:
                    pe.wait_ge(added, b - 2)
                for n in range(2):
                    last = pe.matmul(ps_qk[:, n * T:(n + 1) * T], wqk_s[:, n * C:(n + 1) * C], xt[:, u, :], start=True, stop=True)
                last.then_inc(qk_done, 1)
                for h in range(2):
                    last = pe.matmul(ps_v[:, h * C:(h + 1) * C], xt[:, u, h * P:(h + 1) * P], wv_s[:], start=True, stop=True)
                last.then_inc(v_done, 1)

            def score(b, i, u, early):
                tile, h0, heads, keys = unit(i)
                n = UN * b + i
                if i == 0:
                    pe.wait_ge(kx_ready, b + 1)
                if not early or UN * b + i >= 2:
                    pe.wait_ge(centred, n - 1)
                pe.matmul(ps_s[i % 2][:], ident_b[:], mask[:, tile, :], start=True, stop=False)
                pe.matmul(ps_s[i % 2][:], q[:, u, tile * P:(tile + 1) * P], kx[:, u, h0:h0 + heads, 0:keys],
                          start=False, stop=True).then_inc(scored, 1)

            def turn_e(b, i, u, early):
                pe.wait_ge(exped, UN * b + i + 1)
                if not early or UN * b + i >= 2:
                    pe.wait_ge(back_act if i % 2 == 0 else back_dve, 3 * b + i // 2)
                for n in range(4):
                    last = pe.transpose(ps_t[i % 2][:, n * P:(n + 1) * P], e[:, i % 3, n * P:(n + 1) * P], keep.ident[:])
                last.then_inc(e_turned, 1)

            def weigh(b, i, u, early):
                tile, h0, heads, keys = unit(i)
                pe.wait_ge(back_act if i % 2 == 0 else back_dve, 3 * b + i // 2 + 1)
                if i == 0 and (not isinstance(b, int) or b):
                    pe.wait_ge(o_ready, b)
                chunks = keys // P
                for n in range(heads):
                    h = h0 + n
                    at = (tile * NH + h) * (HD + 1)
                    for c in range(chunks):
                        last = pe.matmul(ps_o[:, at:at + HD + 1], pt[:, i % 2, (n * chunks + c) * P:(n * chunks + c + 1) * P],
                                         vx[:, u, c, h, :], start=(c == 0), stop=(c == chunks - 1))
                last.then_inc(weighed, 1)

            def turn_o(b, i, u, early):
                pe.wait_ge(o_ready, b + 1)
                pe.wait_ge(xt_ready, least(b, 3))
                if not isinstance(b, int) or b:
                    pe.wait_ge(ot_ready, b)
                for h in range(2):
                    last = pe.transpose(ps_x[:, h * P:(h + 1) * P], on[:, u, h * NH:(h + 1) * NH, :], keep.ident[:])
                last.then_inc(o_turned, 1)

            def project_o(b, i, u, early):
                pe.wait_ge(ot_ready, b + 1)
                pe.wait_ge(v_out, least(b, 3))
                if not isinstance(b, int) or b:
                    pe.wait_ge(added, b)
                for h in range(2):
                    last = pe.matmul(ps_v[:, h * C:(h + 1) * C], ot[:, u, h, :], wout_s[:], start=True, stop=True)
                last.then_inc(y_done, 1)

            pe.wait_ge(w_in, 48)
            pe.wait_ge(const, 5)
            timetable(pe, [(18, False, project_o), (1, False, turn_x), (2, False, project), (7, True, score),
                           (9, True, turn_e), (10, True, weigh), (17, False, turn_o)])


class Keep:
    pass


def hybrid(nc, a, out):
    q_dram = nc.dram_tensor("q_scratch", [P, B * T], F32, kind="Internal").ap()
    xs_dram = nc.dram_tensor("xs_scratch", [SLOTS, C], F32, kind="Internal").ap()
    ys_dram = nc.dram_tensor("ys_scratch", [SLOTS, C], F32, kind="Internal").ap()
    with ExitStack() as ctx:
        s = Space(nc, ctx)
        keep = Keep()
        keep.ident = s.sb("ident", [P, P])
        keep.ones = s.sb("ones", [P, P])
        keep.waited = s.sem("waited")
        keep.t = s.sb("tokens", [P, NT, C])
        keep.tscale = s.sb("tscale", [P, NT])
        keep.tshift = s.sb("tshift", [P, NT])
        keep.head8 = s.sb("head8", [P, NH])

        with ExitStack() as conv:
            s = Space(nc, conv)
            keep.xc = s.sb("xc", [P, B, T])
            keep.group4 = s.sb("group4", [P, P])
            keep.bn = s.sb("bn", [P, B, 6])
            keep.mem_t = s.sb("mem_t", [P, MEM])
            keep.rstd, keep.shift, keep.rstd2, keep.shift2 = (
                s.sb(x, [P, B]) for x in ("rstd", "shift", "rstd2", "shift2"))
            keep.pad = s.sb("pad", [P, B, HH + 2, WW + 2])
            keep.w1s = s.sb("w1s", [P, 5, C])
            keep.w2t = s.sb("w2t_sb", [P, C])
            keep.gate = s.sb("gates", [P, 3, B])
            keep.zbias = s.sb("zbias", [P, B])
            prepare_and_first_norm(nc, s, a["x"], a["memory"], keep)
            clear_slots(nc, xs_dram)
            memory_lookup(nc, s, a["memory"], keep)
            gates(nc, s, a["w1"], a["w1_t"], a["b1"], a["wa_t"], a["ba"], a["wb_t"], a["bb"], a["w2_t"], a["b2"], keep)
            shifted_convolution(nc, s, keep)

        token_stats(nc, s, keep, "norm2")
        with ExitStack() as attention:
            s = Space(nc, attention)
            keep.k_t = s.sb("k_t", [P, B * T])
            keep.vp = s.sb("vp", [P, NT, NH, HD + 1])
            soft_projections(nc, s, a["r_qkv"], a["r_wo"], q_dram, keep)
            rosa_attention(nc, s, q_dram, keep)

        def expert_layer(name, n, swiglu, router, loads, shared):
            token_stats(nc, s, keep, name + "_norm")
            with ExitStack() as layer:
                own = Space(nc, layer)
                m = Moe(own, name, n, swiglu)
                with ExitStack() as rows:
                    xn = Space(nc, rows).sb(name + "_xn", [P, NT, C])
                    route(nc, own, m, router, lambda sp: load_experts(sp, m, *loads), xn, keep)
                    dispatch(nc, own, m, xs_dram, xn, shared, keep)
                experts(nc, own, m, xs_dram, ys_dram, keep)
                combine(nc, own, m, ys_dram, keep)

        expert_layer("m2", 16, True, a["m2_router"], ([a["m2_gate"], a["m2_up"]], a["m2_down"]),
                     (a["m2_shared_up"], a["m2_shared_down"]))
        token_stats(nc, s, keep, "norm3")
        causal_attention(nc, s, a["c_qk"], a["c_v"], a["c_out"], keep)
        expert_layer("m3", 8, False, a["m3_router"], ([a["m3_w1"]], a["m3_w2"], a["m3_b1"], a["m3_b2"]), None)
        store_channels(nc, out, keep)


def clear_slots(nc, xs_dram):
    with ExitStack() as ctx:
        s = Space(nc, ctx)
        zero = s.sb("zero", [P, 8 * C])
        zeroed = s.sem("slots_zeroed")
        stored = s.sem("slots_stored")
        block = ctx.enter_context(nc.Block())
        rows = xs_dram.rearrange("(a p b) c -> a p (b c)", p=P, b=8)

        @block.gpsimd
        def _(pool):
            pool.memset(zero[:], 0.0).then_inc(zeroed, 1)

        @block.sync
        def _(sp):
            sp.wait_ge(zeroed, 1)
            for i in range(SLOTS // (8 * P)):
                sp.dma_start(rows[i], zero[:]).then_inc(stored, 16)
            sp.wait_ge(stored, 16 * (SLOTS // (8 * P)))


def store_channels(nc, out, keep):
    with ExitStack() as ctx:
        s = Space(nc, ctx)
        image = s.sb("out_image", [P, 4, T])
        ps_t = [s.ps(f"out_ps{i}", [P, 512]) for i in range(4)]
        turned = s.sem("out_turned")
        copied = s.sem("out_copied")
        stored = [s.sem(f"out_stored{i}") for i in range(4)]
        block = ctx.enter_context(nc.Block())

        @block.tensor
        def _(pe):
            for b in range(B):
                if b >= 4:
                    pe.wait_ge(copied, b - 3)
                for h in range(2):
                    last = pe.transpose(ps_t[b % 4][:, h * P:(h + 1) * P], keep.t[:, 2 * b + h, :], keep.ident[:])
                last.then_inc(turned, 1)

        @block.vector
        def _(dve):
            def copy(b, u, early):
                dve.wait_ge(turned, b + 1)
                if not early:
                    dve.wait_ge(stored[u], 4 * (b - u))
                dve.tensor_copy(image[:, u, :], ps_t[u][:, 0:T]).then_inc(copied, 1)

            in_turn(dve, B, 4, copy)

        @block.sync
        def _(sp):
            def store(b, u, early):
                sp.wait_ge(copied, b + 1)
                sp.dma_start(out[b].rearrange("c h w -> c (h w)"), image[:, u, :]).then_inc(stored[u], 16)

            in_turn(sp, B, 4, store)
            for u in range(4):
                sp.wait_ge(stored[u], 16 * B // 4)




def kernel(x, L0_conv_memory, L1_conv_w1, L1_conv_b1, L1_conv_wa, L1_conv_ba, L1_conv_wb, L1_conv_bb, L1_conv_w2,
           L1_conv_b2, L2_attn_wq, L2_attn_wk, L2_attn_wv, L2_attn_wo, L2_ffn_gate_w, L2_ffn_wg, L2_ffn_wu, L2_ffn_wd,
           L2_ffn_swg, L2_ffn_swu, L2_ffn_swd, L3_attn_w_qkv, L3_attn_w_out, L3_ffn_W_router, L3_ffn_W1, L3_ffn_b1,
           L3_ffn_W2, L3_ffn_b2):
    import concourse.bacc as bacc
    from concourse.bass_utils import run_bass_kernel_spmd

    def lay(v, *axes):
        v = np.asarray(v)
        return np.ascontiguousarray(v.transpose(*axes) if axes else v)

    def by_chunk(v):
        e, k, n = v.shape
        return lay(v.reshape(e, k // P, P, n), 2, 0, 1, 3)

    w_qkv_t = lay(L3_attn_w_qkv, 1, 0)
    arrays = {
        "x": lay(x), "memory": lay(L0_conv_memory),
        "w1": lay(L1_conv_w1), "w1_t": lay(L1_conv_w1, 1, 0), "b1": lay(np.asarray(L1_conv_b1).reshape(3, C), 1, 0),
        "wa_t": lay(L1_conv_wa, 1, 0), "ba": lay(np.asarray(L1_conv_ba).reshape(C, 1)),
        "wb_t": lay(L1_conv_wb, 1, 0), "bb": lay(np.asarray(L1_conv_bb).reshape(3, C), 1, 0),
        "w2_t": lay(L1_conv_w2, 1, 0), "b2": lay(np.asarray(L1_conv_b2).reshape(C, 1)),
        "r_qkv": np.concatenate([lay(L2_attn_wq), lay(L2_attn_wk), lay(L2_attn_wv)], axis=1), "r_wo": lay(L2_attn_wo),
        "m2_router": lay(L2_ffn_gate_w, 1, 0), "m2_gate": lay(L2_ffn_wg, 2, 0, 1), "m2_up": lay(L2_ffn_wu, 2, 0, 1),
        "m2_down": by_chunk(lay(L2_ffn_wd, 0, 2, 1)),
        "m2_shared_up": np.concatenate([lay(L2_ffn_swg, 1, 0), lay(L2_ffn_swu, 1, 0)], axis=1),
        "m2_shared_down": by_chunk(lay(L2_ffn_swd, 1, 0)[None])[:, 0],
        "c_qk": lay(w_qkv_t[:, 0:2 * C]), "c_v": lay(w_qkv_t[:, 2 * C:]), "c_out": lay(L3_attn_w_out, 1, 0),
        "m3_router": lay(L3_ffn_W_router), "m3_w1": lay(L3_ffn_W1, 1, 0, 2), "m3_b1": lay(L3_ffn_b1),
        "m3_w2": by_chunk(lay(L3_ffn_W2)), "m3_b2": lay(L3_ffn_b2),
    }
    nc = bacc.Bacc("TRN2", target_bir_lowering=False, num_devices=1)
    given = {n: nc.dram_tensor("in_" + n, v.shape, mybir.dt.from_np(v.dtype), kind="ExternalInput").ap()
             for n, v in arrays.items()}
    out = nc.dram_tensor("out", [B, C, HH, WW], F32, kind="ExternalOutput").ap()
    hybrid(nc, given, out)
    r = run_bass_kernel_spmd(nc, [{"in_" + n: v for n, v in arrays.items()}], core_ids=[0])
    return r.results[0]["out"]
```

```python
from contextlib import ExitStack

import concourse.bass as bass
from concourse import mybir
import numpy as np

F32 = mybir.dt.float32
BF16 = mybir.dt.bfloat16
I32 = mybir.dt.int32
U32 = mybir.dt.uint32
ALU = mybir.AluOpType
ACT = mybir.ActivationFunctionType
AX = mybir.AxisListType

P = 128
C = 128
B, HH, WW = 16, 16, 16
T = HH * WW
NT = B * T // P
MEM = 256
NH, HD = 8, 16
BH = B * NH


class Space:

    def __init__(self, nc, ctx):
        self.nc, self.ctx = nc, ctx
        self.sems = []
        ctx.callback(self.give_back)

    def sb(self, name, shape, dt=F32):
        return self.ctx.enter_context(self.nc.sbuf_tensor(name, shape, dt))

    def ps(self, name, shape, dt=F32):
        return self.ctx.enter_context(self.nc.psum_tensor(name, shape, dt))

    def sem(self, name):
        self.sems.append(self.nc.alloc_semaphore(name))
        return self.sems[-1]

    def give_back(self):
        if self.sems:
            self.nc.clear_and_free_semaphores(self.sems)
            self.nc.all_engine_barrier()


def in_turn(eng, n, depth, body):
    for j in range(min(depth, n)):
        body(j, j, True)
    if n > depth:
        assert n % depth == 0
        with eng.Fori(1, n // depth) as i:
            for u in range(depth):
                body(i * depth + u, u, False)


def lagged(eng, n, depth, parts):
    most = max(lag for lag, _ in parts)
    first = -(-(most + depth) // depth) * depth
    assert n % depth == 0 and n > first

    def step(k, slot, early_steps):
        for lag, body in parts:
            if not early_steps or 0 <= k - lag < n:
                body(k - lag, (slot - lag) % depth, early_steps and k - lag < depth)

    for k in range(first):
        step(k, k, True)
    with eng.Fori(first // depth, n // depth) as i:
        for u in range(depth):
            step(i * depth + u, u, False)
    for k in range(n, n + most):
        step(k, k, True)


def prepare_and_first_norm(nc, top, x, memory, keep):
    with ExitStack() as ctx:
        s = Space(nc, ctx)
        mem_rows = s.sb("mem_rows", [P, 2, C])
        mem_sq = s.sb("mem_sq", [P, 2, C])
        mem_norm = s.sb("mem_norm", [P, 4])
        ps_mem = s.ps("ps_mem", [P, 512])
        x_in = [s.sem(f"x_in{i}") for i in range(4)]
        mem_in = s.sem("mem_in")
        const_ready = s.sem("const_ready")
        mem_step = s.sem("mem_step")
        mem_len = s.sem("mem_len")
        mem_turned = s.sem("mem_turned")
        bn_done = s.sem("bn_done")
        g = norm_space(nc, s, "gn0")
        block = ctx.enter_context(nc.Block())

        @block.sync
        def _(sp):
            sp.dma_start(mem_rows[:], memory.rearrange("(m p) c -> p m c", p=P)).then_inc(mem_in, 16)
            for i in range(4):
                sp.dma_start(keep.xc[:, 4 * i:4 * i + 4, :],
                             x[4 * i:4 * i + 4].rearrange("b c h w -> c b (h w)")).then_inc(x_in[i], 16)

        @block.gpsimd
        def _(pool):
            pool.memset(keep.ident[:], 0.0).then_inc(const_ready, 1)
            pool.memset(keep.group4[:], 0.25).then_inc(const_ready, 1)
            pool.memset(keep.ones[:], 1.0).then_inc(const_ready, 1)
            pool.wait_ge(const_ready, 3)
            pool.affine_select(out=keep.ident[:], in_=keep.ident[:], compare_op=ALU.not_equal, fill=1.0,
                               base=0, pattern=[[-1, P]], channel_multiplier=1).then_inc(const_ready, 1)
            v = keep.group4[:].rearrange("p (g k) -> p g k", k=4)
            pool.affine_select(out=v, in_=v, compare_op=ALU.is_ge, fill=0.0,
                               base=0, pattern=[[-4, 32], [0, 4]], channel_multiplier=1).then_inc(const_ready, 1)
            pool.wait_ge(const_ready, 5)
            pool.affine_select(out=v, in_=v, compare_op=ALU.is_ge, fill=0.0,
                               base=3, pattern=[[4, 32], [0, 4]], channel_multiplier=-1).then_inc(const_ready, 1)

        @block.scalar
        def _(act):
            act.wait_ge(mem_len, 2)
            act.activation(mem_norm[:, 2:4], mem_norm[:, 0:2], ACT.Sqrt).then_inc(mem_len, 1)
            norm_scalar(act, g)

        @block.vector
        def _(dve):
            dve.wait_ge(mem_in, 16)
            for m in range(2):
                dve.tensor_tensor_reduce(mem_sq[:, m, :], mem_rows[:, m, :], mem_rows[:, m, :], 1.0, 0.0,
                                         ALU.mult, ALU.add, mem_norm[:, m:m + 1]).then_inc(mem_len, 1)
            dve.wait_ge(mem_len, 3)
            dve.tensor_scalar(mem_norm[:, 0:2], mem_norm[:, 2:4], 1e-12, None, ALU.max).then_inc(mem_len, 1)
            dve.wait_ge(mem_len, 4)
            dve.reciprocal(mem_norm[:, 2:4], mem_norm[:, 0:2]).then_inc(mem_len, 1)
            dve.wait_ge(mem_len, 5)
            for m in range(2):
                dve.tensor_scalar(mem_rows[:, m, :], mem_rows[:, m, :], mem_norm[:, 2 + m:3 + m], None,
                                  ALU.mult).then_inc(mem_step, 1)
            for i in range(4):
                dve.wait_ge(x_in[i], 16)
                with dve.Fori(4 * i, 4 * i + 4) as b:
                    dve.bn_stats(keep.bn[:, b, :], keep.xc[:, b, :]).then_inc(bn_done, 1)
            dve.wait_ge(mem_turned, 1)
            dve.tensor_copy(keep.mem_t[:], ps_mem[:, 0:MEM]).then_inc(mem_step, 1)
            dve.wait_ge(bn_done, B)
            norm_vector(dve, g, keep)

        @block.tensor
        def _(pe):
            pe.wait_ge(const_ready, 6)
            pe.wait_ge(mem_step, 2)
            for m in range(2):
                last = pe.transpose(ps_mem[:, m * P:(m + 1) * P], mem_rows[:, m, :], keep.ident[:])
            last.then_inc(mem_turned, 1)
            norm_tensor(pe, g, keep)


class norm_space:

    def __init__(self, nc, s, name):
        self.mv = s.sb(name + "_mv", [P, B, 2])
        self.both = s.sb(name + "_both", [P, 2, B])
        self.sq = s.sb(name + "_sq", [P, B])
        self.group = s.sb(name + "_group", [P, 2, B])
        self.gvar = s.sb(name + "_gvar", [P, B])
        self.gstd = s.sb(name + "_gstd", [P, B])
        self.ps = s.ps(name + "_ps", [P, 512])
        self.aggregated = s.sem(name + "_aggregated")
        self.channel = s.sem(name + "_channel")
        self.summed = s.sem(name + "_summed")
        self.step = s.sem(name + "_step")
        self.rstd = s.sem(name + "_rstd")


def norm_vector(dve, g, keep, eps=1e-5):
    for b in range(B):
        dve.bn_aggr(g.mv[:, b, :], keep.bn[:, b, :]).then_inc(g.aggregated, 1)
    dve.wait_ge(g.aggregated, B)
    mean, var = g.mv[:, :, 0], g.mv[:, :, 1]
    dve.tensor_tensor(g.sq[:], mean, mean, ALU.mult).then_inc(g.channel, 1)
    dve.tensor_copy(g.both[:, 0, :], mean).then_inc(g.channel, 1)
    dve.wait_ge(g.channel, 2)
    dve.tensor_tensor(g.both[:, 1, :], var, g.sq[:], ALU.add).then_inc(g.channel, 1)
    dve.wait_ge(g.summed, 1)
    dve.tensor_copy(g.group[:].rearrange("p a b -> p (a b)"), g.ps[:, 0:2 * B]).then_inc(g.step, 1)
    dve.wait_ge(g.step, 1)
    dve.tensor_tensor(g.sq[:], g.group[:, 0, :], g.group[:, 0, :], ALU.mult).then_inc(g.step, 1)
    dve.wait_ge(g.step, 2)
    dve.scalar_tensor_tensor(g.gvar[:], g.group[:, 1, :], eps, g.sq[:], ALU.add, ALU.subtract).then_inc(g.step, 1)
    dve.wait_ge(g.rstd, 1)
    dve.reciprocal(keep.rstd[:], g.gstd[:]).then_inc(g.step, 1)
    dve.wait_ge(g.step, 4)
    dve.scalar_tensor_tensor(keep.shift[:], g.group[:, 0, :], -1.0, keep.rstd[:], ALU.mult, ALU.mult).then_inc(g.step, 1)


def norm_scalar(act, g):
    act.wait_ge(g.step, 3)
    act.activation(g.gstd[:], g.gvar[:], ACT.Sqrt).then_inc(g.rstd, 1)


def norm_tensor(pe, g, keep):
    pe.wait_ge(g.channel, 3)
    pe.matmul(g.ps[:, 0:2 * B], keep.group4[:], g.both[:].rearrange("p a b -> p (a b)"),
              start=True, stop=True).then_inc(g.summed, 1)


def memory_lookup(nc, top, memory, xs_dram, keep):
    with ExitStack() as ctx:
        s = Space(nc, ctx)
        xn = s.sb("xn", [P, 2, 2, P])
        sq = s.sb("sq", [P, 2, 2, P])
        length = s.sb("length", [P, 2, 2])
        best = s.sb("best", [P, 2, 2, 8])
        where = s.sb("where", [P, 2, 2, 8], U32)
        least = s.sb("least", [P, 2, 2])
        hit = s.sb("hit", [P, 2, 2])
        row = s.sb("row", [P, 2, 2, C])
        rowm = s.sb("rowm", [P, 2, 2, C])
        ps_sim = [s.ps(f"ps_sim{i}", [P, 2, MEM]) for i in range(2)]
        ps_len = [s.ps(f"ps_len{i}", [P, 512]) for i in range(2)]
        ps_row = [s.ps(f"ps_row{i}", [P, 512]) for i in range(2)]
        zero = s.sb("zero", [P, 8 * C])
        zeroed = s.sem("slots_zeroed")
        slots_stored = s.sem("slots_stored")
        g = norm_space(nc, s, "gn1")
        normed = s.sem("l0_normed")
        squared = s.sem("l0_squared")
        similar = s.sem("l0_similar")
        len_ready = s.sem("l0_len_ready")
        peaked = s.sem("l0_peaked")
        indexed = s.sem("l0_indexed")
        least_ready = s.sem("l0_least_ready")
        hit_ready = s.sem("l0_hit_ready")
        gathered = [s.sem(f"l0_gathered{u}") for u in range(4)]
        masked = s.sem("l0_masked")
        turned = s.sem("l0_turned")
        added = s.sem("l0_added")
        bn_done = s.sem("l0_bn_done")
        block = ctx.enter_context(nc.Block())

        @block.scalar
        def _(act):
            def norm(b, u, early):
                if not early:
                    act.wait_ge(similar, b - 1)
                act.activation(xn[:, u].rearrange("p a b -> p (a b)"), keep.xc[:, b, :], ACT.Identity,
                               bias=keep.shift[:, bass.ds(b, 1)], scale=keep.rstd[:, bass.ds(b, 1)]).then_inc(normed, 1)

            def square(b, u, early):
                act.wait_ge(normed, b + 1)
                if not early:
                    act.wait_ge(similar, b - 1)
                act.activation(sq[:, u], xn[:, u], ACT.Square).then_inc(squared, 1)

            def length_out(b, u, early):
                act.wait_ge(similar, b + 1)
                if not early:
                    act.wait_ge(least_ready, b - 1)
                act.activation(length[:, u, :], ps_len[u][:, 0:2], ACT.Sqrt).then_inc(len_ready, 1)

            lagged(act, B, 2, [(3, length_out), (1, square), (0, norm)])
            norm_scalar(act, g)

        @block.tensor
        def _(pe):
            def compare(b, u, early):
                pe.wait_ge(squared, b + 1)
                if not early:
                    pe.wait_ge(indexed, 2 * (b - 1))
                    pe.wait_ge(len_ready, b - 1)
                for h in range(2):
                    pe.matmul(ps_sim[u][:, h, :], xn[:, u, h, :], keep.mem_t[:], start=True, stop=True)
                for h in range(2):
                    last = pe.matmul(ps_len[u][:, h:h + 1], sq[:, u, h, :], keep.ones[:, 0:1], start=True, stop=True)
                last.then_inc(similar, 1)

            def turn(b, u, early):
                pe.wait_ge(masked, 2 * b + 2)
                if not early:
                    pe.wait_ge(added, b - 1)
                for h in range(2):
                    last = pe.transpose(ps_row[u][:, h * P:(h + 1) * P], rowm[:, u, h, :], keep.ident[:])
                last.then_inc(turned, 1)

            lagged(pe, B, 2, [(7, turn), (2, compare)])
            norm_tensor(pe, g, keep)

        @block.gpsimd
        def _(pool):
            def gather(b, u, early):
                pool.wait_ge(indexed, 2 * b + 2)
                if not early:
                    pool.wait_ge(masked, 2 * (b - 1))
                pool.sem_inc(keep.waited)
                for h in range(2):
                    pool.indirect_dma_start(row[:, u, h, :], None, memory,
                                            bass.IndirectOffsetOnAxis(where[:, u, h, 0:1], 0)).then_inc(gathered[2 * u + h], 16)

            pool.memset(zero[:], 0.0).then_inc(zeroed, 1)
            lagged(pool, B, 2, [(4, gather)])

        @block.sync
        def _(sp):
            rows = xs_dram.rearrange("(a p b) c -> a p (b c)", p=P, b=8)
            sp.wait_ge(zeroed, 1)
            for i in range(rows.shape[0]):
                sp.dma_start(rows[i], zero[:]).then_inc(slots_stored, 16)
            sp.wait_ge(slots_stored, 16 * rows.shape[0])

        @block.vector
        def _(dve):
            def peak(b, u, early):
                dve.wait_ge(similar, b + 1)
                if not early:
                    dve.wait_ge(hit_ready, b - 1)
                dve.sem_inc(keep.waited)
                for h in range(2):
                    dve.max(best[:, u, h, :], ps_sim[u][:, h, :]).then_inc(peaked, 1)

            def index(b, u, early):
                dve.wait_ge(peaked, 2 * b + 2)
                if not early:
                    dve.wait_ge(gathered[2 * u], 8 * (b - u))
                    dve.wait_ge(gathered[2 * u + 1], 8 * (b - u))
                dve.sem_inc(keep.waited)
                for h in range(2):
                    dve.max_index(where[:, u, h, :], best[:, u, h, :], ps_sim[u][:, h, :]).then_inc(indexed, 1)

            def threshold(b, u, early):
                dve.wait_ge(len_ready, b + 1)
                if not early:
                    dve.wait_ge(hit_ready, b - 1)
                dve.tensor_scalar(least[:, u, :], length[:, u, :], 1e-12, 0.8, ALU.max, ALU.mult).then_inc(least_ready, 1)

            def decide(b, u, early):
                dve.wait_ge(peaked, 2 * b + 2)
                dve.wait_ge(least_ready, b + 1)
                if not early:
                    dve.wait_ge(masked, 2 * (b - 1))
                dve.tensor_tensor(hit[:, u, :], best[:, u, :, 0], least[:, u, :], ALU.is_gt).then_inc(hit_ready, 1)

            def mask(b, u, early):
                dve.wait_ge(hit_ready, b + 1)
                for h in range(2):
                    dve.wait_ge(gathered[2 * u + h], 8 * (b - u) + 16)
                    if not early:
                        dve.wait_ge(turned, b - 1)
                    dve.tensor_scalar(rowm[:, u, h, :], row[:, u, h, :], hit[:, u, h:h + 1], None,
                                      ALU.mult).then_inc(masked, 1)

            def add(b, u, early):
                dve.wait_ge(turned, b + 1)
                dve.tensor_tensor(keep.xc[:, b, :], keep.xc[:, b, :], ps_row[u][:, 0:T], ALU.add).then_inc(added, 1)

            def count(b, u, early):
                dve.wait_ge(added, b + 1)
                dve.bn_stats(keep.bn[:, b, :], keep.xc[:, b, :]).then_inc(bn_done, 1)

            lagged(dve, B, 2, [(6, mask), (5, decide), (3, peak), (3, index), (4, threshold), (8, add), (9, count)])
            dve.wait_ge(bn_done, B)
            k = SecondNorm(keep)
            norm_vector(dve, g, k)


class SecondNorm:

    def __init__(self, keep):
        self.bn, self.rstd, self.shift = keep.bn, keep.rstd2, keep.shift2


SHIFTS = [(0, 1), (2, 1), (1, 0), (1, 2), (1, 1)]
DOWN, UP, RIGHT, LEFT, STAY = range(5)
BRANCH_SHIFT = [[DOWN, UP, RIGHT, LEFT], [RIGHT, LEFT, DOWN, UP], [STAY] * 4]
GATE_OF_SHIFT = [0, 0, 1, 1, 2]
Q = 32


def gates(nc, top, w1_rows, w1_t, b1, wa_t, ba, wb_t, bb, w2_t, b2, keep):
    with ExitStack() as ctx:
        s = Space(nc, ctx)
        w1t = s.sb("w1t_sb", [P, 3 * C])
        wat = s.sb("wat_sb", [P, C])
        wbt = s.sb("wbt_sb", [P, 3 * C])
        b1s = s.sb("b1s", [P, 3])
        bas = s.sb("bas", [P, 1])
        bbs = s.sb("bbs", [P, 3])
        b2s = s.sb("b2s", [P, 1])
        bsum = s.sb("bsum", [P, 2])
        edge = s.sb("edge", [P, 5, B])
        diff = s.sb("diff", [P, 2, B])
        sums = s.sb("sums", [P, 5, B])
        pooled = s.sb("pooled", [P, B])
        hidden = s.sb("hidden", [P, B])
        hat = s.sb("hat", [P, 3, B])
        peak = s.sb("peak", [P, B])
        total = s.sb("total", [P, B])
        gate = s.sb("gate", [P, 3, B])
        mixed = s.sb("mixed", [P, B])
        ps_pool = s.ps("ps_pool", [P, 512])
        ps_hid = s.ps("ps_hid", [P, 512])
        ps_hat = s.ps("ps_hat", [P, 512])
        ps_bias = s.ps("ps_bias", [P, 512])
        w_in = s.sem("l1_w_in")
        rows_in = s.sem("l1_rows_in")
        zeroed = s.sem("l1_zeroed")
        padded = s.sem("l1_padded")
        edged = s.sem("l1_edged")
        summed = s.sem("l1_summed")
        pool_ps = s.sem("l1_pool_ps")
        pool_sb = s.sem("l1_pool_sb")
        hid_ps = s.sem("l1_hid_ps")
        hid_sb = s.sem("l1_hid_sb")
        hat_ps = s.sem("l1_hat_ps")
        soft = s.sem("l1_soft")
        exped = s.sem("l1_exped")
        bias_ps = s.sem("l1_bias_ps")
        block = ctx.enter_context(nc.Block())
        pad = keep.pad
        inner = pad[:, :, 1:17, 1:17]

        @block.sync
        def _(sp):
            for dst, src in ((w1t[:], w1_t), (wat[:], wa_t), (wbt[:], wb_t), (keep.w2t[:], w2_t),
                             (b1s[:], b1), (bas[:], ba),
                             (bbs[:], bb), (b2s[:], b2)):
                sp.dma_start(dst, src).then_inc(w_in, 16)
            sp.wait_ge(zeroed, 1)
            for k in range(2):
                for q in range(4):
                    sp.dma_start(keep.w1s[Q * q:Q * q + Q, BRANCH_SHIFT[k][q], :],
                                 w1_rows[k * C + Q * q:k * C + Q * q + Q, :]).then_inc(rows_in, 16)
            sp.dma_start(keep.w1s[:, STAY, :], w1_rows[2 * C:3 * C, :]).then_inc(rows_in, 16)
            sp.wait_ge(rows_in, 16 * 9)

        @block.gpsimd
        def _(pool):
            pool.memset(keep.w1s[:], 0.0).then_inc(zeroed, 1)

        @block.scalar
        def _(act):
            with act.Fori(0, B) as b:
                act.activation(pad[:, b, 1:17, 1:17], keep.xc[:, b, :].rearrange("p (h w) -> p h w", w=WW),
                               ACT.Identity, bias=keep.shift2[:, bass.ds(b, 1)],
                               scale=keep.rstd2[:, bass.ds(b, 1)]).then_inc(padded, 1)
            act.wait_ge(hid_ps, 1)
            act.activation(hidden[:], ps_hid[:, 0:B], ACT.Gelu, bias=bas[:, 0:1]).then_inc(hid_sb, 1)
            act.wait_ge(soft, 6)
            act.activation(gate[:], hat[:], ACT.Exp).then_inc(exped, 1)

        @block.vector
        def _(dve):
            dve.wait_ge(w_in, 16 * 8)
            dve.tensor_reduce(bsum[:, 0:1], b1s[:], AX.X, ALU.add).then_inc(pool_sb, 1)
            dve.wait_ge(pool_sb, 1)
            dve.tensor_scalar(bsum[:, 1:2], bsum[:, 0:1], float(T), None, ALU.mult).then_inc(pool_sb, 1)
            dve.wait_ge(padded, B)
            for dst, src in ((pad[:, :, 0, 1:17], pad[:, :, 1, 1:17]), (pad[:, :, 17, 1:17], pad[:, :, 16, 1:17]),
                             (pad[:, :, 1:17, 0], pad[:, :, 1:17, 1]), (pad[:, :, 1:17, 17], pad[:, :, 1:17, 16])):
                dve.tensor_copy(dst, src).then_inc(edged, 1)
            for n, src in enumerate((pad[:, :, 1, 1:17], pad[:, :, 16, 1:17], pad[:, :, 1:17, 1], pad[:, :, 1:17, 16])):
                dve.tensor_reduce(edge[:, n, :], src, AX.X, ALU.add).then_inc(summed, 1)
            dve.tensor_reduce(sums[:, STAY, :], inner, AX.XY, ALU.add).then_inc(summed, 1)
            dve.wait_ge(summed, 5)
            dve.tensor_tensor(diff[:, 0, :], edge[:, 0, :], edge[:, 1, :], ALU.subtract).then_inc(summed, 1)
            dve.tensor_tensor(diff[:, 1, :], edge[:, 2, :], edge[:, 3, :], ALU.subtract).then_inc(summed, 1)
            dve.wait_ge(summed, 7)
            for n, (d, op) in enumerate(((0, ALU.add), (0, ALU.subtract), (1, ALU.add), (1, ALU.subtract))):
                dve.tensor_tensor(sums[:, n, :], sums[:, STAY, :], diff[:, d, :], op).then_inc(summed, 1)
            dve.wait_ge(pool_ps, 1)
            dve.wait_ge(pool_sb, 2)
            dve.tensor_scalar(pooled[:], ps_pool[:, 0:B], bsum[:, 1:2], None, ALU.add).then_inc(pool_sb, 1)
            dve.wait_ge(hat_ps, 1)
            for k in range(3):
                dve.tensor_scalar(hat[:, k, :], ps_hat[:, k * B:(k + 1) * B], bbs[:, k:k + 1], None, ALU.add).then_inc(soft, 1)
            dve.wait_ge(soft, 3)
            dve.tensor_tensor(peak[:], hat[:, 0, :], hat[:, 1, :], ALU.max).then_inc(soft, 1)
            dve.wait_ge(soft, 4)
            dve.tensor_tensor(peak[:], peak[:], hat[:, 2, :], ALU.max).then_inc(soft, 1)
            dve.wait_ge(soft, 5)
            dve.tensor_tensor(hat[:], hat[:], peak[:, None, :].to_broadcast([P, 3, B]), ALU.subtract).then_inc(soft, 1)
            dve.wait_ge(exped, 1)
            dve.tensor_tensor(total[:], gate[:, 0, :], gate[:, 1, :], ALU.add).then_inc(soft, 1)
            dve.wait_ge(soft, 7)
            dve.tensor_tensor(total[:], total[:], gate[:, 2, :], ALU.add).then_inc(soft, 1)
            dve.wait_ge(soft, 8)
            dve.reciprocal(peak[:], total[:]).then_inc(soft, 1)
            dve.wait_ge(soft, 9)
            dve.tensor_tensor(gate[:], gate[:], peak[:, None, :].to_broadcast([P, 3, B]), ALU.mult).then_inc(soft, 1)
            dve.wait_ge(soft, 10)
            for half, (a, b) in enumerate(((0, 1), (1, 0))):
                rows = slice(64 * half, 64 * half + 64)
                dve.tensor_copy(keep.gate[rows, 0, :], gate[rows, a, :]).then_inc(soft, 1)
                dve.tensor_copy(keep.gate[rows, 1, :], gate[rows, b, :]).then_inc(soft, 1)
            dve.tensor_copy(keep.gate[:, 2, :], gate[:, 2, :]).then_inc(soft, 1)
            dve.tensor_scalar(mixed[:], gate[:, 0, :], b1s[:, 0:1], None, ALU.mult).then_inc(soft, 1)
            for k in (1, 2):
                dve.wait_ge(soft, 15 + k)
                dve.scalar_tensor_tensor(mixed[:], gate[:, k, :], b1s[:, k:k + 1], mixed[:], ALU.mult, ALU.add).then_inc(soft, 1)
            dve.wait_ge(bias_ps, 1)
            dve.tensor_scalar(keep.zbias[:], ps_bias[:, 0:B], b2s[:, 0:1], None, ALU.add).then_inc(soft, 1)

        @block.tensor
        def _(pe):
            pe.wait_ge(w_in, 16 * 8)
            pe.wait_ge(summed, 11)
            for q in range(4):
                for k in range(3):
                    last = pe.matmul(ps_pool[Q * q:Q * q + Q, 0:B], w1t[:, k * C + Q * q:k * C + Q * q + Q],
                                     sums[:, BRANCH_SHIFT[k][q], :], start=(k == 0), stop=(k == 2))
            last.then_inc(pool_ps, 1)
            pe.wait_ge(pool_sb, 3)
            pe.matmul(ps_hid[:, 0:B], wat[:], pooled[:], start=True, stop=True).then_inc(hid_ps, 1)
            pe.wait_ge(hid_sb, 1)
            for k in range(3):
                last = pe.matmul(ps_hat[:, k * B:(k + 1) * B], wbt[:, k * C:(k + 1) * C], hidden[:], start=True, stop=True)
            last.then_inc(hat_ps, 1)
            pe.wait_ge(soft, 18)
            pe.matmul(ps_bias[:, 0:B], keep.w2t[:], mixed[:], start=True, stop=True).then_inc(bias_ps, 1)


def shifted_convolution(nc, top, keep):
    with ExitStack() as ctx:
        s = Space(nc, ctx)
        w2g = s.sb("w2g", [P, 2, 3, C])
        both = s.sb("both", [P, 2, 5, C])
        xnew = s.sb("xnew", [P, 2, 2, P])
        ps_both = [s.ps(f"ps_both{i}", [P, 2, 512]) for i in range(2)]
        ps_z = [s.ps(f"ps_z{i}", [P, 512]) for i in range(2)]
        ps_t = [s.ps(f"ps_t{i}", [P, 512]) for i in range(2)]
        gated = s.sem("cv_gated")
        joined = s.sem("cv_joined")
        copied = s.sem("cv_copied")
        shifted = s.sem("cv_shifted")
        added = s.sem("cv_added")
        turned = s.sem("cv_turned")
        stored = s.sem("cv_stored")
        counted = s.sem("cv_counted")
        block = ctx.enter_context(nc.Block())

        @block.vector
        def _(dve):
            def gate(b, u, early):
                if not early:
                    dve.wait_ge(joined, b - 1)
                for k in range(3):
                    dve.tensor_scalar(w2g[:, u, k, :], keep.w2t[:], keep.gate[:, k, bass.ds(b, 1)], None,
                                      ALU.mult).then_inc(gated, 1)

            def add(b, u, early):
                dve.wait_ge(shifted, b + 1)
                if not early:
                    dve.wait_ge(turned, b - 1)
                dve.scalar_tensor_tensor(xnew[:, u].rearrange("p a b -> p (a b)"), ps_z[u][:, 0:T],
                                         keep.zbias[:, bass.ds(b, 1)], keep.xc[:, b, :], ALU.add, ALU.add).then_inc(added, 1)

            def count(b, u, early):
                dve.wait_ge(stored, b + 1)
                for h in range(2):
                    dve.bn_stats(keep.tbn[:, 2 * b + h, :], keep.t[:, 2 * b + h, :]).then_inc(counted, 1)

            lagged(dve, B, 2, [(7, count), (4, add), (0, gate)])

        @block.scalar
        def _(act):
            def copy(b, u, early):
                act.wait_ge(joined, b + 1)
                if not early:
                    act.wait_ge(shifted, b - 1)
                act.activation(both[:, u, 0:4, :], ps_both[u][:, 0, :].rearrange("p (a b) -> p a b", b=C), ACT.Copy).then_inc(copied, 1)
                act.activation(both[:, u, 4, :], ps_both[u][:, 1, 0:C], ACT.Copy).then_inc(copied, 1)

            def store(b, u, early):
                act.wait_ge(turned, b + 1)
                act.activation(keep.t[:, bass.ds(2 * b, 2), :], ps_t[u][:, 0:T].rearrange("p (a b) -> p a b", b=C),
                               ACT.Copy).then_inc(stored, 1)

            lagged(act, B, 2, [(6, store), (2, copy)])

        @block.tensor
        def _(pe):
            def join(b, u, early):
                pe.wait_ge(gated, 3 * b + 3)
                if not early:
                    pe.wait_ge(copied, 2 * (b - 1))
                for n in range(5):
                    last = pe.matmul(ps_both[u][:, n // 4, n % 4 * C:n % 4 * C + C], keep.w1s[:, n, :],
                                     w2g[:, u, GATE_OF_SHIFT[n], :], start=True, stop=True)
                last.then_inc(joined, 1)

            def shift(b, u, early):
                pe.wait_ge(copied, 2 * b + 2)
                if not early:
                    pe.wait_ge(added, b - 1)
                for n, (di, dj) in enumerate(SHIFTS):
                    last = pe.matmul(ps_z[u][:, 0:T], both[:, u, n, :], keep.pad[:, b, di:di + HH, dj:dj + WW],
                                     start=(n == 0), stop=(n == 4))
                last.then_inc(shifted, 1)

            def turn(b, u, early):
                pe.wait_ge(added, b + 1)
                if not early:
                    pe.wait_ge(stored, b - 1)
                for h in range(2):
                    last = pe.transpose(ps_t[u][:, h * P:(h + 1) * P], xnew[:, u, h, :], keep.ident[:])
                last.then_inc(turned, 1)

            lagged(pe, B, 2, [(5, turn), (3, shift), (1, join)])


def token_stats(nc, top, keep, name, eps=1e-5):
    with ExitStack() as ctx:
        s = Space(nc, ctx)
        mv = s.sb(name + "_mv", [P, NT, 2])
        var = s.sb(name + "_var", [P, NT])
        counted = s.sem(name + "_counted")
        step = s.sem(name + "_step")
        rooted = s.sem(name + "_rooted")
        block = ctx.enter_context(nc.Block())

        @block.scalar
        def _(act):
            act.wait_ge(step, 1)
            act.activation(keep.tscale[:], var[:], ACT.Sqrt).then_inc(rooted, 1)

        @block.vector
        def _(dve):
            for j in range(NT):
                dve.bn_aggr(mv[:, j, :], keep.tbn[:, j, :]).then_inc(counted, 1)
            dve.wait_ge(counted, NT)
            dve.tensor_scalar(var[:], mv[:, :, 1], eps, None, ALU.add).then_inc(step, 1)
            dve.wait_ge(rooted, 1)
            dve.reciprocal(keep.tscale[:], keep.tscale[:]).then_inc(step, 1)
            dve.wait_ge(step, 2)
            dve.scalar_tensor_tensor(keep.tshift[:], mv[:, :, 0], -1.0, keep.tscale[:], ALU.mult, ALU.mult).then_inc(step, 1)


def soft_projections(nc, top, wqkv, wo, q_dram, keep):
    NG = 3 * NH
    with ExitStack() as ctx:
        s = Space(nc, ctx)
        w = s.sb("r_w", [P, 3 * C])
        q_t = s.sb("r_q_t", [P, B * T])
        q_out = s.sem("r_q_out")
        wos = s.sb("r_wo", [P, HD])
        wod = s.sb("r_wod", [P, NH, HD])
        xn = s.sb("r_xn", [P, 2, C])
        xt = s.sb("r_xt", [P, 2, P])
        peak = s.sb("r_peak", [P, 2, NG])
        e = s.sb("r_e", [P, 2, NG, HD])
        total = s.sb("r_total", [P, 2, NG])
        inv = s.sb("r_inv", [P, 2, NG])
        soft = s.sb("r_soft", [P, 2, NG, HD])
        vt = s.sb("r_vt", [P, 2, P])
        ps_x = [s.ps(f"r_ps_x{i}", [P, 512]) for i in range(2)]
        ps_q = [s.ps(f"r_ps_q{i}", [P, 512]) for i in range(2)]
        ps_t = [s.ps(f"r_ps_t{i}", [P, 512]) for i in range(2)]
        ps_v = [s.ps(f"r_ps_v{i}", [P, 512]) for i in range(2)]
        w_in = s.sem("r_w_in")
        spread = s.sem("r_spread")
        normed = s.sem("r_normed")
        turned = s.sem("r_turned")
        xt_ready = s.sem("r_xt_ready")
        projected = s.sem("r_projected")
        peaked = s.sem("r_peaked")
        centred = s.sem("r_centred")
        exped = s.sem("r_exped")
        summed = s.sem("r_summed")
        inverted = s.sem("r_inverted")
        softened = s.sem("r_softened")
        soft_turned = s.sem("r_soft_turned")
        unpacked = s.sem("r_unpacked")
        mixed = s.sem("r_mixed")
        v_ready = s.sem("r_v_ready")
        block = ctx.enter_context(nc.Block())

        @block.sync
        def _(sp):
            sp.dma_start(w[:], wqkv).then_inc(w_in, 16)
            sp.dma_start(wos[:], wo).then_inc(w_in, 16)
            for i in range(4):
                sp.wait_ge(unpacked, 3 * NT // 4 * (i + 1))
                part = slice(i * B * T // 4, (i + 1) * B * T // 4)
                sp.dma_start(q_dram[:, part], q_t[:, part]).then_inc(q_out, 16)
            sp.wait_ge(q_out, 64)

        @block.gpsimd
        def _(pool):
            pool.memset(keep.head8[:], 1.0).then_inc(spread, 1)
            pool.memset(keep.vp[:], 1.0).then_inc(spread, 1)
            pool.wait_ge(w_in, 32)
            pool.tensor_copy(wod[:], wos[:, None, :].to_broadcast([P, NH, HD])).then_inc(spread, 1)
            pool.wait_ge(spread, 3)
            for n, (v, pat) in enumerate(((wod[:], [0, HD]), (keep.head8[:], None))):
                more = [pat] if pat else []
                pool.affine_select(out=v, in_=v, compare_op=ALU.is_ge, fill=0.0, base=0,
                                   pattern=[[-HD, NH]] + more, channel_multiplier=1).then_inc(spread, 1)
            pool.wait_ge(spread, 5)
            for n, (v, pat) in enumerate(((wod[:], [0, HD]), (keep.head8[:], None))):
                more = [pat] if pat else []
                pool.affine_select(out=v, in_=v, compare_op=ALU.is_ge, fill=0.0, base=HD - 1,
                                   pattern=[[HD, NH]] + more, channel_multiplier=-1).then_inc(spread, 1)

        @block.scalar
        def _(act):
            def norm(j, u, early):
                if not early:
                    act.wait_ge(turned, j - 1)
                act.activation(xn[:, u, :], keep.t[:, j, :], ACT.Identity, bias=keep.tshift[:, bass.ds(j, 1)],
                               scale=keep.tscale[:, bass.ds(j, 1)]).then_inc(normed, 1)

            def exp(j, u, early):
                act.wait_ge(centred, j + 1)
                act.activation(e[:, u], e[:, u], ACT.Exp, scale=10.0).then_inc(exped, 1)

            def unpack(j, u, early):
                act.wait_ge(soft_turned, j + 1)
                act.activation(q_t[:, bass.ds(j * P, P)], ps_t[u][:, 0:P], ACT.Copy).then_inc(unpacked, 1)
                act.activation(keep.k_t[:, bass.ds(j * P, P)], ps_t[u][:, P:2 * P], ACT.Copy).then_inc(unpacked, 1)
                if not early:
                    act.wait_ge(mixed, j - 1)
                act.activation(vt[:, u, :], ps_t[u][:, 2 * P:3 * P], ACT.Copy).then_inc(unpacked, 1)

            lagged(act, NT, 2, [(8, unpack), (5, exp), (0, norm)])

        @block.vector
        def _(dve):
            def x_out(j, u, early):
                dve.wait_ge(turned, j + 1)
                if not early:
                    dve.wait_ge(projected, j - 1)
                dve.tensor_copy(xt[:, u, :], ps_x[u][:, 0:P]).then_inc(xt_ready, 1)

            def centre(j, u, early):
                q = ps_q[u][:, 0:3 * C].rearrange("p (g d) -> p g d", d=HD)
                dve.wait_ge(projected, j + 1)
                dve.tensor_reduce(peak[:, u, :], q, AX.X, ALU.max).then_inc(peaked, 1)
                dve.wait_ge(peaked, j + 1)
                if not early:
                    dve.wait_ge(softened, j - 1)
                dve.tensor_tensor(e[:, u], q, peak[:, u, :, None].to_broadcast([P, NG, HD]), ALU.subtract).then_inc(centred, 1)

            def soften(j, u, early):
                dve.wait_ge(exped, j + 1)
                dve.tensor_reduce(total[:, u, :], e[:, u], AX.X, ALU.add).then_inc(summed, 1)
                dve.wait_ge(summed, j + 1)
                dve.reciprocal(inv[:, u, :], total[:, u, :]).then_inc(inverted, 1)
                dve.wait_ge(inverted, j + 1)
                if not early:
                    dve.wait_ge(soft_turned, j - 1)
                dve.tensor_tensor(soft[:, u], e[:, u], inv[:, u, :, None].to_broadcast([P, NG, HD]), ALU.mult).then_inc(softened, 1)

            def v_out(j, u, early):
                dve.wait_ge(mixed, j + 1)
                dve.tensor_copy(keep.vp[:, j, :, 0:HD], ps_v[u][:, 0:C].rearrange("p (h d) -> p h d", d=HD)).then_inc(v_ready, 1)

            dve.wait_ge(spread, 7)
            lagged(dve, NT, 2, [(10, v_out), (6, soften), (4, centre), (2, x_out)])

        @block.tensor
        def _(pe):
            def turn(j, u, early):
                pe.wait_ge(normed, j + 1)
                if not early:
                    pe.wait_ge(xt_ready, j - 1)
                pe.transpose(ps_x[u][:, 0:P], xn[:, u, :], keep.ident[:]).then_inc(turned, 1)

            def project(j, u, early):
                pe.wait_ge(xt_ready, j + 1)
                if not early:
                    pe.wait_ge(centred, j - 1)
                pe.matmul(ps_q[u][:, 0:3 * C], xt[:, u, :], w[:], start=True, stop=True).then_inc(projected, 1)

            def turn_soft(j, u, early):
                pe.wait_ge(softened, j + 1)
                if not early:
                    pe.wait_ge(unpacked, 3 * (j - 1))
                for n in range(3):
                    last = pe.transpose(ps_t[u][:, n * P:(n + 1) * P], soft[:, u, n * NH:(n + 1) * NH, :], keep.ident[:])
                last.then_inc(soft_turned, 1)

            def mix(j, u, early):
                pe.wait_ge(unpacked, 3 * j + 3)
                if not early:
                    pe.wait_ge(v_ready, j - 1)
                pe.matmul(ps_v[u][:, 0:C], vt[:, u, :], wod[:], start=True, stop=True).then_inc(mixed, 1)

            pe.wait_ge(w_in, 32)
            pe.wait_ge(spread, 7)
            lagged(pe, NT, 2, [(9, mix), (7, turn_soft), (3, project), (1, turn)])


QUARTER = 64
GROUP = 4
NGROUP = T // GROUP
PER_Q = QUARTER // GROUP
ZR = 3
QX = 3
PAIRS = B // 2


def rosa_attention(nc, top, q_dram, keep):
    with ExitStack() as ctx:
        s = Space(nc, ctx)
        held = [s.sb(f"a_held{i}", [P, QUARTER, BH]) for i in range(4)]
        qx = s.sb("a_qx", [P, QX, QUARTER, NH])
        q_in = s.sb("a_q_in", [P, 4, QUARTER])
        iota = s.sb("a_iota", [P, T])
        prior = s.sb("a_prior", [P, 4, T])
        y = s.sb("a_y", [P, 2, T + 1])
        z = s.sb("a_z", [P, ZR, GROUP, T])
        peak = s.sb("a_peak", [P, 2, GROUP])
        bias = s.sb("a_bias", [P, 2, GROUP])
        inv = s.sb("a_inv", [P, 2, 2, NH])
        o = s.sb("a_o", [P, 2, 2, NH, HD])
        iota_i = held[3][:, 0:2, :].rearrange("p a b -> p (a b)").bitcast(I32)
        ps_row = [s.ps(f"a_ps_row{i}", [P, 2, 512]) for i in range(2)]
        ps_back = [s.ps(f"a_ps_back{i}", [P, 512]) for i in range(2)]
        ps_score = s.ps("a_ps_score", [P, 512])
        ps_o = s.ps("a_ps_o", [P, 512])
        iota_ready = s.sem("a_iota_ready")
        q_loaded = [s.sem(f"a_q_loaded{i}") for i in range(4)]
        cleared = s.sem("a_cleared")
        qx_dve = s.sem("a_qx_dve")
        qx_pool = s.sem("a_qx_pool")
        scored = s.sem("a_scored")
        score_held = s.sem("a_score_held")
        row_turned = s.sem("a_row_turned")
        prior_ready = s.sem("a_prior_ready")
        scanned = s.sem("a_scanned")
        peaked = s.sem("a_peaked")
        bias_ready = s.sem("a_bias_ready")
        exped = s.sem("a_exped")
        back_turned = s.sem("a_back_turned")
        back_act = s.sem("a_back_act")
        back_dve = s.sem("a_back_dve")
        summed = s.sem("a_summed")
        inverted = s.sem("a_inverted")
        scaled = s.sem("a_scaled")
        added = s.sem("a_added")
        counted = s.sem("a_counted")
        block = ctx.enter_context(nc.Block())

        place = [[0], [1], [2, 3], [0, 1]]
        chunks = [1, 1, 2, 2]
        units = [(None, 0, b, (0,)) for b in range(B)]
        for i in range(PER_Q):
            units += [(i, 1, b, (0,)) for b in range(B) if 14 * b // B == i]
            units += [(i, 2, b, (0, 1)) for b in range(B // 2) if 1 + 3 * b // 2 == i]
        for i in range(PER_Q):
            units += [(PER_Q + i, 2, b, (0, 1)) for b in range(B // 2, B) if 3 * (b - B // 2) // 2 == i]
            units += [(PER_Q + i, 3, b, (0,)) for b in range(B) if 3 + 11 * b // B == i]
        for i in range(PER_Q):
            units += [(2 * PER_Q + i, 3, b, (1,)) for b in range(B) if 3 + 11 * b // B == i]
        U = len(units)
        assert U == 5 * B
        items = [(n, k) for n in range(U) for k in units[n][3]]
        item_no = {item: no for no, item in enumerate(items)}

        def by_dve(n):
            return units[n][0] is None or units[n][0] < PER_Q

        dve_units = sum(by_dve(n) for n in range(U))

        def wait_spread(eng, n):
            if by_dve(n):
                eng.wait_ge(qx_dve, n + 1)
            else:
                eng.wait_ge(qx_pool, n - dve_units + 1)

        def units_at(g):
            return [n for n in range(U) if units[n][0] == g]

        def items_before(q):
            return sum(units[n][0] is None or units[n][0] < PER_Q * q for n, _ in items)

        def score_buffer(no):
            return ps_score if no >= items_before(2) or no % 2 == 0 else ps_row[0][:, 1]

        def spread(eng, n, done):
            if n >= QX:
                eng.wait_ge(scored, item_no[n - QX, units[n - QX][3][-1]] + 1)
            eng.wait_ge(q_loaded[n % 4], 16 * (n // 4 + 1))
            eng.tensor_tensor(qx[:, n % QX], q_in[:, n % 4, :, None].to_broadcast([P, QUARTER, NH]),
                              keep.head8[:, None, :].to_broadcast([P, QUARTER, NH]), ALU.mult).then_inc(done, 1)

        back_no = {}
        for g in range(NGROUP):
            for k in range(chunks[g // PER_Q]):
                back_no[g, k] = len(back_no)

        def before(no):
            return (no + 1) // 2, no // 2

        def sums_at(g):
            q, i = divmod(g, PER_Q)
            return [(q - 1, i - 2)] if q >= 1 and 2 <= i < 2 + PAIRS else []

        def sum_buffer(q, m):
            return ps_score if q >= 2 and m % 2 else ps_o

        last_sums = [(3, m) for m in range(PAIRS)]

        @block.tensor
        def _(pe):
            def score(n, k):
                _, q, b, _ = units[n]
                no = item_no[n, k]
                wait_spread(pe, n)
                if no >= items_before(2):
                    pe.wait_ge(score_held, no)
                elif no >= 2:
                    pe.wait_ge(score_held, no - 1)
                pe.matmul(score_buffer(no)[:], keep.k_t[:, (2 * b + k) * P:(2 * b + k + 1) * P],
                          qx[:, n % QX], start=True, stop=True).then_inc(scored, 1)

            def turn_rows(g):
                q = g // PER_Q
                pe.wait_ge(score_held, items_before(q))
                if g >= 2:
                    pe.wait_ge(scanned, GROUP * (g - 1))
                for i in range(GROUP):
                    for k in range(chunks[q]):
                        at = (i * chunks[q] + k) * P
                        last = pe.transpose(ps_row[g % 2][:, at // 512, at % 512:at % 512 + P],
                                            held[place[q][k]][:, GROUP * g % QUARTER + i, :], keep.ident[:])
                last.then_inc(row_turned, 1)

            def turn_back(g):
                q = g // PER_Q
                pe.wait_ge(exped, GROUP * (g + 1))
                for k in range(chunks[q]):
                    no = back_no[g, k]
                    if no >= 2:
                        a, d = before(no - 1)
                        if no % 2 == 0:
                            pe.wait_ge(back_act, a)
                        else:
                            pe.wait_ge(back_dve, d)
                    for i in range(GROUP):
                        last = pe.transpose(ps_back[no % 2][:, i * P:(i + 1) * P],
                                            z[:, g % ZR, i, k * P:(k + 1) * P], keep.ident[:])
                    last.then_inc(back_turned, 1)

            def weigh(q, m):
                n = PAIRS * q + m
                if m == 0:
                    a, d = before(back_no[PER_Q * q + PER_Q - 1, chunks[q] - 1] + 1)
                    pe.wait_ge(back_act, a)
                    pe.wait_ge(back_dve, d)
                if q >= 2:
                    pe.wait_ge(scaled, n - 1)
                elif n:
                    pe.wait_ge(scaled, n)
                ps_sum = sum_buffer(q, m)
                rows = slice(QUARTER * (q % 2), QUARTER * (q % 2) + QUARTER)
                for i in range(2):
                    b = 2 * m + i
                    for h in range(NH):
                        at = (NH * i + h) * (HD + 1)
                        for k in range(chunks[q]):
                            last = pe.matmul(ps_sum[rows, at:at + HD + 1], held[place[q][k]][:, :, NH * b + h],
                                             keep.vp[:, 2 * b + k, h, :], start=(k == 0), stop=(k == chunks[q] - 1))
                last.then_inc(summed, 1)

            for n in range(B):
                score(n, 0)
            turn_rows(0)
            for g in range(NGROUP):
                beside = [(n, k) for n in units_at(g) for k in units[n][3]]
                if g + 1 < NGROUP:
                    turn_rows(g + 1)
                for q, m in sums_at(g):
                    weigh(q, m)
                for item in beside[:2]:
                    score(*item)
                if g >= 1:
                    turn_back(g - 1)
                for item in beside[2:]:
                    score(*item)
            turn_back(NGROUP - 1)
            for q, m in last_sums:
                weigh(q, m)

        @block.scalar
        def _(act):
            def hold(n, k):
                _, q, b, _ = units[n]
                no = item_no[n, k]
                act.wait_ge(scored, no + 1)
                if q == 3:
                    act.wait_ge(summed, PAIRS * k + b // 2 + 1)
                act.activation(held[place[q][k]][:, :, NH * b:NH * b + NH],
                               score_buffer(no)[:].rearrange("p (t h) -> p t h", h=NH), ACT.Copy).then_inc(score_held, 1)

            def back(g):
                q = g // PER_Q
                for k in range(chunks[q]):
                    no = back_no[g, k]
                    if no % 2 == 0:
                        act.wait_ge(back_turned, no + 1)
                        r = GROUP * g % QUARTER
                        act.activation(held[place[q][k]][:, r:r + GROUP, :].rearrange("p a b -> p (a b)"),
                                       ps_back[0][:], ACT.Copy).then_inc(back_act, 1)

            def exp(g):
                act.wait_ge(bias_ready, g + 1)
                for i in range(GROUP):
                    n = GROUP * g + i + 1
                    act.activation(z[:, g % ZR, i, 0:n], z[:, g % ZR, i, 0:n], ACT.Exp, bias=bias[:, g % 2, i:i + 1],
                                   scale=10.0).then_inc(exped, 1)

            for n in range(B):
                hold(n, 0)
            act.wait_ge(cleared, 3)
            for g in range(NGROUP):
                if g >= 2:
                    back(g - 2)
                for n in units_at(g):
                    for k in units[n][3]:
                        hold(n, k)
                exp(g)
            back(NGROUP - 2)
            back(NGROUP - 1)

        @block.vector
        def _(dve):
            def scan(r):
                g, i = divmod(r, GROUP)
                nk = chunks[g // PER_Q]
                if i == 0:
                    dve.wait_ge(row_turned, g + 1)
                if r == 0:
                    dve.wait_ge(cleared, 3)
                else:
                    dve.wait_ge(scanned, r)
                if r >= 2:
                    dve.wait_ge(peaked, r - 1)
                at = i * nk * P
                dve.scalar_tensor_tensor(y[:, r % 2, 1:r + 2], y[:, (r + 1) % 2, 0:r + 1], 1.0,
                                         ps_row[g % 2][:, at // 512, at % 512:at % 512 + r + 1],
                                         ALU.add, ALU.mult).then_inc(scanned, 1)

            def add_prior(r):
                g, i = divmod(r, GROUP)
                if i == 0 and g >= ZR:
                    dve.wait_ge(back_turned, back_no[g - ZR, chunks[(g - ZR) // PER_Q] - 1] + 1)
                if i == 0 and g >= 2:
                    dve.wait_ge(exped, GROUP * (g - 1))
                dve.wait_ge(prior_ready, r + 1)
                dve.wait_ge(scanned, r + 1)
                dve.tensor_tensor_reduce(z[:, g % ZR, i, 0:r + 1], y[:, r % 2, 1:r + 2], prior[:, r % 4, 0:r + 1],
                                         1.0, -3.0e38, ALU.add, ALU.max, peak[:, g % 2, i:i + 1]).then_inc(peaked, 1)

            def back(g):
                q = g // PER_Q
                for k in range(chunks[q]):
                    no = back_no[g, k]
                    if no % 2 == 1:
                        dve.wait_ge(back_turned, no + 1)
                        r = GROUP * g % QUARTER
                        dve.tensor_copy(held[place[q][k]][:, r:r + GROUP, :].rearrange("p a b -> p (a b)"),
                                        ps_back[1][:]).then_inc(back_dve, 1)

            def scale(q, m):
                n = PAIRS * q + m
                rows = slice(QUARTER * (q % 2), QUARTER * (q % 2) + QUARTER)
                sums = sum_buffer(q, m)[rows, 0:2 * NH * (HD + 1)].rearrange("p (i h d) -> p i h d", i=2, d=HD + 1)
                dve.wait_ge(summed, n + 1)
                dve.reciprocal(inv[rows, n % 2], sums[:, :, :, HD]).then_inc(inverted, 1)
                dve.wait_ge(inverted, n + 1)
                if n >= 2:
                    dve.wait_ge(added, n - 1)
                dve.tensor_tensor(o[rows, n % 2], sums[:, :, :, 0:HD],
                                  inv[rows, n % 2, :, :, None].to_broadcast([QUARTER, 2, NH, HD]), ALU.mult).then_inc(scaled, 1)

            def count(q, m):
                if q % 2 == 0:
                    return
                dve.wait_ge(added, PAIRS * q + m + 1)
                for b in (2 * m, 2 * m + 1):
                    j = 2 * b + q // 2
                    dve.bn_stats(keep.tbn[:, j, :], keep.t[:, j, :]).then_inc(counted, 1)

            for n in range(B):
                spread(dve, n, qx_dve)
            for n in units_at(0):
                spread(dve, n, qx_dve)
            for g in range(NGROUP):
                for i in range(GROUP):
                    scan(GROUP * g + i)
                    if g or i:
                        add_prior(GROUP * g + i - 1)
                    if i == 0 and g:
                        dve.wait_ge(peaked, GROUP * g)
                        dve.tensor_scalar(bias[:, (g - 1) % 2, :], peak[:, (g - 1) % 2, :], -10.0, None, ALU.mult).then_inc(bias_ready, 1)
                    if i == 1:
                        for q, m in (sums_at(g - 1) if g else []):
                            scale(q, m)
                if g >= 2:
                    back(g - 2)
                for q, m in (sums_at(g - 3) if g >= 3 else []):
                    count(q, m)
                for n in units_at(g + 1):
                    if by_dve(n):
                        spread(dve, n, qx_dve)
            add_prior(T - 1)
            dve.wait_ge(peaked, T)
            dve.tensor_scalar(bias[:, (NGROUP - 1) % 2, :], peak[:, (NGROUP - 1) % 2, :], -10.0, None, ALU.mult).then_inc(bias_ready, 1)
            back(NGROUP - 2)
            back(NGROUP - 1)
            for q, m in last_sums:
                scale(q, m)
                if m:
                    count(q, m - 1)
            count(3, PAIRS - 1)

        @block.sync
        def _(sp):
            for n in range(U):
                _, q, b, _ = units[n]
                if n >= 4:
                    wait_spread(sp, n - 4)
                at = T * b + QUARTER * q
                sp.dma_start(q_in[:, n % 4, :], q_dram[:, at:at + QUARTER]).then_inc(q_loaded[n % 4], 16)

        @block.gpsimd
        def _(pool):
            def position(r):
                if r >= 4:
                    pool.wait_ge(peaked, r - 3)
                pool.tensor_scalar(prior[:, r % 4, 0:r + 1], iota[:, 0:r + 1], 1.0 / (r + 1), None, ALU.mult).then_inc(prior_ready, 1)

            def add(q, m):
                n = PAIRS * q + m
                rows = slice(QUARTER * (q % 2), QUARTER * (q % 2) + QUARTER)
                pool.wait_ge(prior_ready, priors)
                pool.wait_ge(qx_pool, expanded)
                pool.wait_ge(scaled, n + 1)
                j = 4 * m + q // 2
                at = keep.t[rows, j:j + 3:2, :].rearrange("p i (h d) -> p i h d", d=HD)
                pool.tensor_tensor(at, at, o[rows, n % 2], ALU.add).then_inc(added, 1)

            pool.memset(z[:].rearrange("p a b c -> p (a b c)"), 0.0).then_inc(cleared, 1)
            pool.memset(y[:].rearrange("p a b -> p (a b)"), 0.0).then_inc(cleared, 1)
            pool.iota(iota_i, pattern=[[1, T]], base=0, channel_multiplier=0).then_inc(iota_ready, 1)
            pool.wait_ge(iota_ready, 1)
            pool.tensor_copy(iota[:], iota_i).then_inc(iota_ready, 1)
            pool.wait_ge(iota_ready, 2)
            pool.memset(bias[:].rearrange("p a b -> p (a b)"), 0.0).then_inc(cleared, 1)
            for r in range(GROUP):
                position(r)
            for g in range(NGROUP):
                if g + 1 < NGROUP:
                    for i in range(GROUP):
                        position(GROUP * (g + 1) + i)
                for n in units_at(g + 1):
                    if not by_dve(n):
                        spread(pool, n, qx_pool)
                priors = min(GROUP * (g + 2), T)
                expanded = sum(not by_dve(n) and units[n][0] <= g + 1 for n in range(U))
                for q, m in (sums_at(g - 1) if g else []):
                    add(q, m)
                    pool.wait_ge(added, PAIRS * q + m + 1)
            for q, m in last_sums:
                add(q, m)
                pool.wait_ge(added, PAIRS * q + m + 1)


TOPK = 2
LOT = 4
HID = 512
KC = HID // P
SLOTS = 80 * P
XR = 4


class Moe:

    def __init__(self, s, name, experts, swiglu):
        self.name, self.n, self.swiglu = name, experts, swiglu
        self.tiles = (B * T * TOPK // P + experts) // 2 * 2
        self.up = [s.sb(f"{name}_up{i}", [P, experts, HID]) for i in range(2 if swiglu else 1)]
        self.down = s.sb(f"{name}_down", [P, experts, KC, C])
        if not swiglu:
            self.b1 = s.sb(f"{name}_b1", [P, experts, HID])
            self.b2 = s.sb(f"{name}_b2", [P, experts, C])
        self.slot = s.sb(f"{name}_slot", [P, NT, TOPK], U32)
        self.weight = s.sb(f"{name}_weight", [P, TOPK, NT])
        self.of_tile = s.sb(f"{name}_of_tile", [P, self.tiles], I32)
        self.up_in = [s.sem(f"{name}_up_in{i}") for i in range(2)]
        self.down_in = s.sem(f"{name}_down_in")


def load_experts(sp, m, up, down, b1=None, b2=None):
    half = m.n // 2
    for lot in range(2):
        part = slice(lot * half, (lot + 1) * half)
        for dst, src in zip(m.up, up):
            sp.dma_start(dst[:, part], src[:, part]).then_inc(m.up_in[lot], 16)
        sp.dma_start(m.down[:, part], down[:, part]).then_inc(m.down_in, 16)
    if b1 is not None:
        sp.dma_start(m.b1[:], b1[None, :, :].to_broadcast([P, m.n, HID])).then_inc(m.down_in, 16)
        sp.dma_start(m.b2[:], b2[None, :, :].to_broadcast([P, m.n, C])).then_inc(m.down_in, 16)


def route(nc, top, m, router, loads, xn, keep):
    E, N = m.n, NT * m.n
    name = m.name
    with ExitStack() as ctx:
        s = Space(nc, ctx)

        def sb(what, shape, dt=F32):
            return s.sb(f"{name}_{what}", shape, dt)

        def sem(what):
            return s.sem(f"{name}_{what}")

        w = sb("router", [P, E])
        xt = sb("xt", [P, 2, LOT, P])
        lg = sb("lg", [P, NT, E])
        low = sb("low", [P, NT, E])
        pick = [sb(f"pick{k}", [P, NT, E]) for k in range(TOPK)]
        both = sb("both", [P, NT, E])
        tmp = sb("tmp", [P, NT, E])
        run = [sb(f"run{i}", [P, E, NT]) for i in range(2)]
        own = sb("own", [P, E, NT])
        at = sb("at", [P, NT])
        inv = sb("inv", [P, NT])
        idx = sb("idx", [P, NT])
        slot_f = sb("slot_f", [P, NT, TOPK])
        order_i = sb("order_i", [P, E], I32)
        order = sb("order", [P, E])
        number_i = sb("number_i", [P, m.tiles], I32)
        number = sb("number", [P, m.tiles])
        before = sb("before", [P, P])
        count = sb("count", [P, E])
        whole_i = sb("whole_i", [P, E], I32)
        whole = sb("whole", [P, E])
        end = [sb(f"end{i}", [P, E]) for i in range(2)]
        first = sb("first", [P, E])
        passed = sb("passed", [P, m.tiles, E])
        of_f = sb("of_f", [P, m.tiles])
        ps_x = [s.ps(f"{name}_ps_x{i}", [P, 512]) for i in range(2)]
        ps_l = [s.ps(f"{name}_ps_l{i}", [P, 512]) for i in range(2)]
        ps_in = s.ps(f"{name}_ps_in", [P, 512])
        ps_all = s.ps(f"{name}_ps_all", [P, 512])
        w_in, const = sem("w_in"), sem("const")
        normed, turned, xt_ready, logits, lg_ready = (sem(x) for x in ("normed", "turned", "xt_ready", "logits", "lg_ready"))
        step, exped, ranked = sem("step"), sem("exped"), sem("ranked")
        block = ctx.enter_context(nc.Block())

        @block.sync
        def _(sp):
            sp.dma_start(w[:], router).then_inc(w_in, 16)
            loads(sp)

        @block.gpsimd
        def _(pool):
            pool.memset(before[:], 1.0).then_inc(const, 1)
            pool.iota(order_i[:], pattern=[[1, E]], base=-64, channel_multiplier=0).then_inc(const, 1)
            pool.iota(number_i[:], pattern=[[1, m.tiles]], base=0, channel_multiplier=0).then_inc(const, 1)
            pool.wait_ge(const, 3)
            pool.affine_select(out=before[:], in_=before[:], compare_op=ALU.is_gt, fill=0.0, base=0,
                               pattern=[[1, P]], channel_multiplier=-1).then_inc(const, 1)
            pool.tensor_copy(order[:], order_i[:]).then_inc(const, 1)
            pool.tensor_copy(number[:], number_i[:]).then_inc(const, 1)

        @block.scalar
        def _(act):
            def norm(j, u, early):
                act.activation(xn[:, j, :], keep.t[:, j, :], ACT.Identity, bias=keep.tshift[:, bass.ds(j, 1)],
                               scale=keep.tscale[:, bass.ds(j, 1)]).then_inc(normed, 1)

            in_turn(act, NT, 2, norm)
            act.wait_ge(step, 2)
            act.activation(lg[:], lg[:], ACT.Exp).then_inc(exped, 1)

        @block.tensor
        def _(pe):
            def turn(n):
                pe.wait_ge(normed, LOT * (n + 1))
                if n >= 2:
                    pe.wait_ge(xt_ready, n - 1)
                for i in range(LOT):
                    last = pe.transpose(ps_x[n % 2][:, i * P:(i + 1) * P], xn[:, LOT * n + i, :], keep.ident[:])
                last.then_inc(turned, 1)

            def project(n):
                pe.wait_ge(xt_ready, n + 1)
                if n >= 2:
                    pe.wait_ge(lg_ready, n - 1)
                for i in range(LOT):
                    last = pe.matmul(ps_l[n % 2][:, i * E:(i + 1) * E], xt[:, n % 2, i, :], w[:], start=True, stop=True)
                last.then_inc(logits, 1)

            pe.wait_ge(w_in, 16)
            for n in range(NT // LOT):
                turn(n)
                if n:
                    project(n - 1)
            project(NT // LOT - 1)
            pe.wait_ge(ranked, 1)
            pe.wait_ge(const, 6)
            pe.matmul(ps_in[:, 0:N], before[:], both[:].rearrange("p a b -> p (a b)"), start=True, stop=True).then_inc(ranked, 1)
            pe.matmul(ps_all[:, 0:N], keep.ones[:], both[:].rearrange("p a b -> p (a b)"), start=True, stop=True).then_inc(ranked, 1)

        @block.vector
        def _(dve):
            def x_out(n, u, early):
                dve.wait_ge(turned, n + 1)
                if not early:
                    dve.wait_ge(logits, n - 1)
                dve.tensor_copy(xt[:, u].rearrange("p a b -> p (a b)"), ps_x[u][:]).then_inc(xt_ready, 1)

            def logits_out(n, u, early):
                dve.wait_ge(logits, n + 1)
                dve.tensor_copy(lg[:, bass.ds(LOT * n, LOT), :],
                                ps_l[u][:, 0:LOT * E].rearrange("p (a b) -> p a b", b=E)).then_inc(lg_ready, 1)

            lagged(dve, NT // LOT, 2, [(0, x_out), (1, logits_out)])
            dve.wait_ge(lg_ready, NT // LOT)
            dve.wait_ge(const, 6)
            done = [0]

            def then(ins):
                ins.then_inc(step, 1)
                done[0] += 1
                dve.wait_ge(step, done[0])

            def over(v):
                return v[:, :, None].to_broadcast([P, NT, E])

            orders = order[:, None, :].to_broadcast([P, NT, E])
            then(dve.tensor_reduce(at[:], lg[:], AX.X, ALU.max))
            then(dve.tensor_tensor(lg[:], lg[:], over(at), ALU.subtract))
            dve.wait_ge(exped, 1)
            then(dve.tensor_reduce(at[:], lg[:], AX.X, ALU.add))
            then(dve.reciprocal(inv[:], at[:]))
            then(dve.tensor_tensor(lg[:], lg[:], over(inv), ALU.mult))
            for k in range(TOPK):
                then(dve.tensor_reduce(m.weight[:, k, :], lg[:], AX.X, ALU.max))
                then(dve.tensor_tensor(tmp[:], lg[:], over(m.weight[:, k, :]), ALU.is_equal))
                then(dve.tensor_tensor(low[:], tmp[:], orders, ALU.mult))
                then(dve.tensor_reduce(idx[:], low[:], AX.X, ALU.min))
                then(dve.tensor_tensor(pick[k][:], orders, over(idx), ALU.is_equal))
                if k == 0:
                    then(dve.scalar_tensor_tensor(lg[:], pick[0][:], -4.0, lg[:], ALU.mult, ALU.add))
            dve.tensor_tensor(both[:], pick[0][:], pick[1][:], ALU.add).then_inc(ranked, 1)
            if not m.swiglu:
                then(dve.tensor_tensor(at[:], m.weight[:, 0, :], m.weight[:, 1, :], ALU.add))
                then(dve.reciprocal(inv[:], at[:]))
                then(dve.tensor_tensor(m.weight[:], m.weight[:], inv[:, None, :].to_broadcast([P, TOPK, NT]), ALU.mult))
            dve.wait_ge(ranked, 3)
            then(dve.tensor_copy(own[:], ps_all[:, 0:N].rearrange("p (j e) -> p e j", e=E)))
            src, n, d = own, 0, 1
            while d < NT:
                dst = run[n % 2]
                then(dve.tensor_copy(dst[:, :, 0:d], src[:, :, 0:d]))
                then(dve.tensor_tensor(dst[:, :, d:], src[:, :, d:], src[:, :, 0:NT - d], ALU.add))
                src, n, d = dst, n + 1, 2 * d
            then(dve.tensor_scalar(count[:], src[:, :, NT - 1], float(P - 1), None, ALU.add))
            then(dve.tensor_copy(whole_i[:], count[:]))
            then(dve.tensor_scalar(whole_i[:], whole_i[:], 7, None, ALU.arith_shift_right))
            then(dve.tensor_copy(whole[:], whole_i[:]))
            ends, n, d = whole, 0, 1
            while d < E:
                dst = end[n % 2]
                then(dve.tensor_copy(dst[:, 0:d], ends[:, 0:d]))
                then(dve.tensor_tensor(dst[:, d:], ends[:, d:], ends[:, 0:E - d], ALU.add))
                ends, n, d = dst, n + 1, 2 * d
            then(dve.tensor_tensor(first[:], ends[:], whole[:], ALU.subtract))
            then(dve.tensor_tensor(own[:], src[:], own[:], ALU.subtract))
            then(dve.scalar_tensor_tensor(own[:], first[:, :, None].to_broadcast([P, E, NT]), float(P), own[:], ALU.mult, ALU.add))
            then(dve.tensor_tensor(both[:], ps_in[:, 0:N].rearrange("p (j e) -> p j e", e=E),
                                   own[:].rearrange("p e j -> p j e"), ALU.add))
            for k in range(TOPK):
                then(dve.tensor_tensor(tmp[:], both[:], pick[k][:], ALU.mult))
                then(dve.tensor_reduce(slot_f[:, :, k], tmp[:], AX.X, ALU.add))
            then(dve.tensor_copy(m.slot[:], slot_f[:]))
            then(dve.tensor_tensor(passed[:], number[:, :, None].to_broadcast([P, m.tiles, E]),
                                   ends[:, None, :].to_broadcast([P, m.tiles, E]), ALU.is_ge))
            then(dve.tensor_reduce(of_f[:], passed[:], AX.X, ALU.add))
            then(dve.tensor_scalar(of_f[:], of_f[:], float(E - 1), None, ALU.min))
            then(dve.tensor_copy(m.of_tile[:], of_f[:]))


def dispatch(nc, top, m, xs_dram, xn, shared, keep):
    with ExitStack() as ctx:
        s = Space(nc, ctx)
        sent = [s.sem(f"{m.name}_sent{i}") for i in range(4)]
        if shared is not None:
            up, down = shared
            H = up.shape[1] // 2
            HC = H // P
            ws = s.sb("sh_up", [P, 2 * H])
            wd = s.sb("sh_down", [P, HC, C])
            xs = s.sb("sh_xs", [P, 2, C])
            xt = s.sb("sh_xt", [P, 2, P])
            act_g = s.sb("sh_act", [P, 2, H])
            hid = s.sb("sh_hid", [P, 2, H])
            ht = s.sb("sh_ht", [P, 2, HC, P])
            ps_x = [s.ps(f"sh_ps_x{i}", [P, 512]) for i in range(2)]
            ps_u = [s.ps(f"sh_ps_u{i}", [P, 512]) for i in range(2)]
            ps_h = [s.ps(f"sh_ps_h{i}", [P, 512]) for i in range(2)]
            ps_y = [s.ps(f"sh_ps_y{i}", [P, 512]) for i in range(2)]
            w_in, staged, turned, xt_ready, upped, silued, multiplied, h_turned, ht_ready, downed, added = (
                s.sem("sh_" + x) for x in ("w_in", "staged", "turned", "xt_ready", "upped", "silued", "multiplied",
                                           "h_turned", "ht_ready", "downed", "added"))
        block = ctx.enter_context(nc.Block())

        @block.gpsimd
        def _(pool):
            for j in range(NT):
                for k in range(TOPK):
                    n = TOPK * j + k
                    pool.indirect_dma_start(xs_dram, bass.IndirectOffsetOnAxis(m.slot[:, j, k:k + 1], 0),
                                            xn[:, j, :], None).then_inc(sent[n % 4], 16)
            for i in range(4):
                pool.wait_ge(sent[i], 16 * NT * TOPK // 4)

        if shared is None:
            return

        @block.sync
        def _(sp):
            sp.dma_start(ws[:], up).then_inc(w_in, 16)
            sp.dma_start(wd[:], down).then_inc(w_in, 16)

        @block.scalar
        def _(act):
            def stage(j, u, early):
                if not early:
                    act.wait_ge(turned, j - 1)
                act.activation(xs[:, u, :], xn[:, j, :], ACT.Copy).then_inc(staged, 1)

            def silu(j, u, early):
                act.wait_ge(upped, j + 1)
                if not early:
                    act.wait_ge(multiplied, j - 1)
                act.activation(act_g[:, u, :], ps_u[u][:, 0:H], ACT.Silu).then_inc(silued, 1)

            def h_out(j, u, early):
                act.wait_ge(h_turned, j + 1)
                if not early:
                    act.wait_ge(downed, j - 1)
                act.activation(ht[:, u], ps_h[u][:, 0:H].rearrange("p (a b) -> p a b", b=P), ACT.Copy).then_inc(ht_ready, 1)

            lagged(act, NT, 2, [(0, stage), (4, silu), (6, h_out)])

        @block.vector
        def _(dve):
            def x_out(j, u, early):
                dve.wait_ge(turned, j + 1)
                if not early:
                    dve.wait_ge(upped, j - 1)
                dve.tensor_copy(xt[:, u, :], ps_x[u][:, 0:P]).then_inc(xt_ready, 1)

            def multiply(j, u, early):
                dve.wait_ge(silued, j + 1)
                if not early:
                    dve.wait_ge(h_turned, j - 1)
                dve.tensor_tensor(hid[:, u, :], act_g[:, u, :], ps_u[u][:, H:2 * H], ALU.mult).then_inc(multiplied, 1)

            def add(j, u, early):
                dve.wait_ge(downed, j + 1)
                dve.tensor_tensor(keep.t[:, j, :], keep.t[:, j, :], ps_y[u][:, 0:C], ALU.add).then_inc(added, 1)

            lagged(dve, NT, 2, [(2, x_out), (4, multiply), (8, add)])

        @block.tensor
        def _(pe):
            def turn(j, u, early):
                pe.wait_ge(staged, j + 1)
                if not early:
                    pe.wait_ge(xt_ready, j - 1)
                pe.transpose(ps_x[u][:, 0:P], xs[:, u, :], keep.ident[:]).then_inc(turned, 1)

            def up_(j, u, early):
                pe.wait_ge(xt_ready, j + 1)
                if not early:
                    pe.wait_ge(multiplied, j - 1)
                pe.matmul(ps_u[u][:, 0:2 * H], xt[:, u, :], ws[:], start=True, stop=True).then_inc(upped, 1)

            def turn_h(j, u, early):
                pe.wait_ge(multiplied, j + 1)
                if not early:
                    pe.wait_ge(ht_ready, j - 1)
                for k in range(HC):
                    last = pe.transpose(ps_h[u][:, k * P:(k + 1) * P], hid[:, u, k * P:(k + 1) * P], keep.ident[:])
                last.then_inc(h_turned, 1)

            def down_(j, u, early):
                pe.wait_ge(ht_ready, j + 1)
                if not early:
                    pe.wait_ge(added, j - 1)
                for k in range(HC):
                    last = pe.matmul(ps_y[u][:, 0:C], ht[:, u, k, :], wd[:, k, :], start=(k == 0), stop=(k == HC - 1))
                last.then_inc(downed, 1)

            pe.wait_ge(w_in, 32)
            lagged(pe, NT, 2, [(1, turn), (3, up_), (5, turn_h), (7, down_)])


def experts(nc, top, m, xs_dram, ys_dram, keep):
    name, M = m.name, m.tiles
    with ExitStack() as ctx:
        s = Space(nc, ctx)
        xin = s.sb(f"{name}_xin", [P, XR, C])
        xt = s.sb(f"{name}_ext", [P, 2, P])
        act_g = s.sb(f"{name}_act", [P, 2, HID])
        hid = s.sb(f"{name}_hid", [P, 2, HID])
        ht = s.sb(f"{name}_ht", [P, 2, KC, P])
        yout = s.sb(f"{name}_yout", [P, XR, C])
        ps_x = s.ps(f"{name}_eps_x", [P, 512])
        ps_y = s.ps(f"{name}_eps_y", [P, 512])
        ps_h = [s.ps(f"{name}_eps_h{i}", [P, 512]) for i in range(2)]
        ps_g = [s.ps(f"{name}_eps_g{i}", [P, 512]) for i in range(2)]
        ps_u = [s.ps(f"{name}_eps_u{i}", [P, 512]) for i in range(2)] if m.swiglu else ps_g
        loaded = [s.sem(f"{name}_loaded{i}") for i in range(XR)]
        stored = [s.sem(f"{name}_stored{i}") for i in range(XR)]
        turned, xt_ready, upped, silued, hid_ready, h_turned, ht_ready, downed, y_ready = (
            s.sem(f"{name}_e_" + x) for x in ("turned", "xt_ready", "upped", "silued", "hid_ready", "h_turned",
                                              "ht_ready", "downed", "y_ready"))
        block = ctx.enter_context(nc.Block())

        def expert(eng, j):
            return eng.value_load(m.of_tile[0:1, bass.ds(j, 1)], min_val=0, max_val=m.n - 1)

        @block.sync
        def _(sp):
            def load(j, u, early):
                if not early:
                    sp.wait_ge(turned, j - XR + 1)
                sp.dma_start(xin[:, u, :], xs_dram[bass.ds(j * P, P), :]).then_inc(loaded[u], 16)

            in_turn(sp, M, XR, load)

        @block.gpsimd
        def _(pool):
            def store(j, u, early):
                pool.wait_ge(y_ready, j + 1)
                pool.dma_start(ys_dram[bass.ds(j * P, P), :], yout[:, u, :]).then_inc(stored[u], 16)

            in_turn(pool, M, XR, store)
            for u in range(XR):
                pool.wait_ge(stored[u], 16 * M // XR)

        @block.tensor
        def _(pe):
            def turn(j, u, early):
                pe.wait_ge(loaded[u], 4 * (j - u) + 16)
                if not isinstance(j, int) or j:
                    pe.wait_ge(xt_ready, j)
                pe.transpose(ps_x[:, 0:P], xin[:, u, :], keep.ident[:]).then_inc(turned, 1)

            def up(j, u, early):
                e = expert(pe, j)
                pe.wait_ge(xt_ready, j + 1)
                if not early:
                    pe.wait_ge(hid_ready, j - 1)
                for ps, w in zip((ps_g[u % 2], ps_u[u % 2]), m.up):
                    last = pe.matmul(ps[:], xt[:, u % 2, :], w[:, e, :], start=True, stop=True)
                last.then_inc(upped, 1)

            def turn_h(j, u, early):
                pe.wait_ge(hid_ready, j + 1)
                if not early:
                    pe.wait_ge(ht_ready, j - 1)
                for k in range(KC):
                    last = pe.transpose(ps_h[u % 2][:, k * P:(k + 1) * P], hid[:, u % 2, k * P:(k + 1) * P], keep.ident[:])
                last.then_inc(h_turned, 1)

            def down(j, u, early):
                e = expert(pe, j)
                pe.wait_ge(ht_ready, j + 1)
                if not isinstance(j, int) or j:
                    pe.wait_ge(y_ready, j)
                for k in range(KC):
                    last = pe.matmul(ps_y[:, 0:C], ht[:, u % 2, k, :], m.down[:, e, k, :], start=(k == 0), stop=(k == KC - 1))
                last.then_inc(downed, 1)

            for lot in range(2):
                pe.wait_ge(m.up_in[lot], 16 * len(m.up))
            pe.wait_ge(m.down_in, 16 * (2 if m.swiglu else 4))
            lagged(pe, M, XR, [(0, turn), (1, up), (2, turn_h), (3, down)])

        @block.scalar
        def _(act):
            def silu(j, u, early):
                act.wait_ge(upped, j + 1)
                if not early:
                    act.wait_ge(hid_ready, j - 1)
                act.activation(act_g[:, u % 2, :], ps_g[u % 2][:], ACT.Silu).then_inc(silued, 1)

            def h_out(j, u, early):
                act.wait_ge(h_turned, j + 1)
                if not early:
                    act.wait_ge(downed, j - 1)
                act.activation(ht[:, u % 2], ps_h[u % 2][:].rearrange("p (a b) -> p a b", b=P),
                               ACT.Copy if m.swiglu else ACT.Relu).then_inc(ht_ready, 1)

            lagged(act, M, XR, [(1, silu), (2, h_out)] if m.swiglu else [(2, h_out)])

        @block.vector
        def _(dve):
            def x_out(j, u, early):
                dve.wait_ge(turned, j + 1)
                if not early:
                    dve.wait_ge(upped, j - 1)
                dve.tensor_copy(xt[:, u % 2, :], ps_x[:, 0:P]).then_inc(xt_ready, 1)

            def hidden(j, u, early):
                if not m.swiglu:
                    e = expert(dve, j)
                dve.wait_ge(silued if m.swiglu else upped, j + 1)
                if not early:
                    dve.wait_ge(h_turned, j - 1)
                if m.swiglu:
                    dve.tensor_tensor(hid[:, u % 2, :], act_g[:, u % 2, :], ps_u[u % 2][:], ALU.mult).then_inc(hid_ready, 1)
                else:
                    dve.tensor_tensor(hid[:, u % 2, :], ps_g[u % 2][:], m.b1[:, e, :], ALU.add).then_inc(hid_ready, 1)

            def y_out(j, u, early):
                if not m.swiglu:
                    e = expert(dve, j)
                dve.wait_ge(downed, j + 1)
                if not early:
                    dve.wait_ge(stored[u], 4 * (j - u))
                if m.swiglu:
                    dve.tensor_copy(yout[:, u, :], ps_y[:, 0:C]).then_inc(y_ready, 1)
                else:
                    dve.tensor_tensor(yout[:, u, :], ps_y[:, 0:C], m.b2[:, e, :], ALU.add).then_inc(y_ready, 1)

            if not m.swiglu:
                dve.wait_ge(m.down_in, 16 * 4)
            lagged(dve, M, XR, [(0, x_out), (1, hidden), (3, y_out)])


def combine(nc, top, m, ys_dram, keep):
    name = m.name
    with ExitStack() as ctx:
        s = Space(nc, ctx)
        y = s.sb(f"{name}_y", [P, 4, TOPK, C])
        fetched = [[s.sem(f"{name}_fetched{u}_{k}") for k in range(TOPK)] for u in range(4)]
        added = s.sem(f"{name}_added")
        counted = s.sem(f"{name}_counted")
        block = ctx.enter_context(nc.Block())

        @block.gpsimd
        def _(pool):
            for j in range(NT):
                if j >= 4:
                    pool.wait_ge(added, TOPK * (j - 3))
                for k in range(TOPK):
                    pool.indirect_dma_start(y[:, j % 4, k, :], None, ys_dram[0:m.tiles * P, :],
                                            bass.IndirectOffsetOnAxis(m.slot[:, j, k:k + 1], 0)).then_inc(fetched[j % 4][k], 16)

        @block.vector
        def _(dve):
            def tile(j, u, early):
                for k in range(TOPK):
                    dve.wait_ge(fetched[u][k], 4 * (j - u) + 16)
                    if k or not isinstance(j, int) or j:
                        dve.wait_ge(added, TOPK * j + k)
                    dve.scalar_tensor_tensor(keep.t[:, j, :], y[:, u, k, :], m.weight[:, k, bass.ds(j, 1)],
                                             keep.t[:, j, :], ALU.mult, ALU.add).then_inc(added, 1)
                dve.wait_ge(added, TOPK * (j + 1))
                dve.bn_stats(keep.tbn[:, j, :], keep.t[:, j, :]).then_inc(counted, 1)

            in_turn(dve, NT, 4, tile)


UN = 6


def timetable(eng, parts):
    most = max(lag + (UN - 1 if each else 0) for lag, each, _ in parts)
    span = 2 * UN
    first = -(-(most + span) // span) * span

    def step(base, u, static):
        for lag, each, body in parts:
            ahead, i = divmod(u - lag, UN)
            if not each and i:
                continue
            if static:
                if 0 <= ahead < B:
                    body(ahead, i, ahead % 2, ahead < 2)
            else:
                body(base + ahead, i, ahead % 2, False)

    for n in range(first):
        step(0, n, True)
    with eng.Fori(first // span, B // 2) as k:
        for u in range(span):
            step(2 * k, u, False)
    for n in range(B * UN, B * UN + most + 1):
        step(0, n, True)


def causal_attention(nc, top, wqk, wv, wout, keep):
    with ExitStack() as ctx:
        s = Space(nc, ctx)
        wqk_s = s.sb("c_wqk", [P, 2 * C])
        wv_s = s.sb("c_wv", [P, C])
        wout_s = s.sb("c_wout", [P, C])
        ident_b = s.sb("c_ident_b", [P, P], BF16)
        mask = s.sb("c_mask", [P, 2, 512], BF16)
        xn = s.sb("c_xn", [P, 2, 2, C])
        xt = s.sb("c_xt", [P, 2, T])
        q = s.sb("c_q", [P, 2, T])
        k_ = s.sb("c_k", [P, 2, T])
        kx = s.sb("c_kx", [P, 2, NH, T])
        vx = s.sb("c_vx", [P, 2, 2, NH, HD + 1])
        peak = s.sb("c_peak", [P, 2, 4])
        e = s.sb("c_e", [P, 3, 512])
        pt = s.sb("c_pt", [P, 2, 512])
        inv = s.sb("c_inv", [P, 2, 2 * NH])
        on = s.sb("c_on", [P, 2, 2 * NH, HD])
        ot = s.sb("c_ot", [P, 2, 2, P])
        ps_x = s.ps("c_ps_x", [P, 512])
        ps_qk = s.ps("c_ps_qk", [P, 512])
        ps_v = s.ps("c_ps_v", [P, 512])
        ps_o = s.ps("c_ps_o", [P, 512])
        ps_s = [s.ps(f"c_ps_s{i}", [P, 512]) for i in range(2)]
        ps_t = [s.ps(f"c_ps_t{i}", [P, 512]) for i in range(2)]
        (w_in, const, normed, turned, xt_ready, qk_done, v_done, qk_out, v_out, kx_ready, scored, peaked, centred,
         exped, e_turned, back_act, back_dve, weighed, inverted, o_ready, o_turned, ot_ready, y_done, added) = (
            s.sem("c_" + x) for x in ("w_in", "const", "normed", "turned", "xt_ready", "qk_done", "v_done", "qk_out",
                                      "v_out", "kx_ready", "scored", "peaked", "centred", "exped", "e_turned",
                                      "back_act", "back_dve", "weighed", "inverted", "o_ready", "o_turned",
                                      "ot_ready", "y_done", "added"))
        counted = s.sem("c_counted")
        block = ctx.enter_context(nc.Block())

        def unit(i):
            return (0, 4 * i, 4, P) if i < 2 else (1, 2 * (i - 2), 2, T)

        def least(b, n):
            return min(b + n, B) if isinstance(b, int) else b + n

        @block.sync
        def _(sp):
            for dst, src in ((wqk_s, wqk), (wv_s, wv), (wout_s, wout)):
                sp.dma_start(dst[:], src).then_inc(w_in, 16)

        @block.gpsimd
        def _(pool):
            pool.tensor_copy(ident_b[:], keep.ident[:]).then_inc(const, 1)
            pool.memset(mask[:].rearrange("p a b -> p (a b)"), 0.0).then_inc(const, 1)
            pool.memset(vx[:].rearrange("p a b c d -> p (a b c d)"), 1.0).then_inc(const, 1)
            pool.wait_ge(const, 3)
            pool.affine_select(out=mask[:, 0, :].rearrange("p (a b) -> p a b", b=P), in_=mask[:, 0, :].rearrange("p (a b) -> p a b", b=P),
                               compare_op=ALU.is_ge, fill=-1e30, base=0, pattern=[[0, 4], [-1, P]],
                               channel_multiplier=1).then_inc(const, 1)
            pool.affine_select(out=mask[:, 1, :].rearrange("p (a b) -> p a b", b=T), in_=mask[:, 1, :].rearrange("p (a b) -> p a b", b=T),
                               compare_op=ALU.is_ge, fill=-1e30, base=P, pattern=[[0, 2], [-1, T]],
                               channel_multiplier=1).then_inc(const, 1)

            def spread(b, i, u, early):
                pool.wait_ge(qk_out, 2 * b + 2)
                if not early:
                    pool.wait_ge(scored, UN * (b - 1))
                pool.tensor_tensor(kx[:, u], k_[:, u, None, :].to_broadcast([P, NH, T]),
                                   keep.head8[:, :, None].to_broadcast([P, NH, T]), ALU.mult).then_inc(kx_ready, 1)

            timetable(pool, [(4, False, spread)])

        @block.scalar
        def _(act):
            def norm(b, i, u, early):
                if not early:
                    act.wait_ge(turned, b - 1)
                for h in range(2):
                    j = 2 * b + h
                    act.activation(xn[:, u, h, :], keep.t[:, j, :], ACT.Identity, bias=keep.tshift[:, bass.ds(j, 1)],
                                   scale=keep.tscale[:, bass.ds(j, 1)]).then_inc(normed, 1)

            def qk(b, i, u, early):
                act.wait_ge(qk_done, b + 1)
                if not early:
                    act.wait_ge(scored, UN * (b - 1))
                    act.wait_ge(kx_ready, b - 1)
                act.activation(q[:, u, :], ps_qk[:, 0:T], ACT.Copy).then_inc(qk_out, 1)
                act.activation(k_[:, u, :], ps_qk[:, T:2 * T], ACT.Copy).then_inc(qk_out, 1)

            def exp(b, i, u, early):
                act.wait_ge(centred, UN * b + i + 1)
                act.activation(e[:, i % 3, :], e[:, i % 3, :], ACT.Exp, scale=float(HD) ** -0.5).then_inc(exped, 1)

            def back(b, i, u, early):
                if i % 2 == 0:
                    act.wait_ge(e_turned, UN * b + i + 1)
                    if not early:
                        act.wait_ge(weighed, UN * b + i - 1)
                    elif UN * b + i >= 2:
                        act.wait_ge(weighed, UN * b + i - 1)
                    act.activation(pt[:, 0, :], ps_t[0][:], ACT.Copy).then_inc(back_act, 1)

            def ot_out(b, i, u, early):
                act.wait_ge(o_turned, b + 1)
                if not early:
                    act.wait_ge(y_done, b - 1)
                act.activation(ot[:, u].rearrange("p a b -> p (a b)"), ps_x[:, 0:T], ACT.Copy).then_inc(ot_ready, 1)

            timetable(act, [(0, False, norm), (4, False, qk), (10, True, back), (7, True, exp), (18, False, ot_out)])

        @block.vector
        def _(dve):
            def x_out(b, i, u, early):
                dve.wait_ge(turned, b + 1)
                if not early:
                    dve.wait_ge(v_done, b - 1)
                dve.tensor_copy(xt[:, u, :], ps_x[:, 0:T]).then_inc(xt_ready, 1)

            def v(b, i, u, early):
                dve.wait_ge(v_done, b + 1)
                if not early:
                    dve.wait_ge(weighed, UN * (b - 1))
                dve.tensor_copy(vx[:, u].rearrange("p a b c -> p (a b) c")[:, :, 0:HD],
                                ps_v[:, 0:2 * C].rearrange("p (a d) -> p a d", d=HD)).then_inc(v_out, 1)

            def centre(b, i, u, early):
                _, _, heads, keys = unit(i)
                n = UN * b + i
                sc = ps_s[i % 2][:].rearrange("p (h s) -> p h s", s=keys)
                dve.wait_ge(scored, n + 1)
                dve.tensor_reduce(peak[:, i % 2, 0:heads], sc, AX.X, ALU.max).then_inc(peaked, 1)
                dve.wait_ge(peaked, n + 1)
                if not early or UN * b + i >= 3:
                    dve.wait_ge(e_turned, n - 2)
                dve.tensor_tensor(e[:, i % 3, :].rearrange("p (h s) -> p h s", s=keys), sc,
                                  peak[:, i % 2, 0:heads, None].to_broadcast([P, heads, keys]), ALU.subtract).then_inc(centred, 1)

            def back(b, i, u, early):
                if i % 2 == 1:
                    dve.wait_ge(e_turned, UN * b + i + 1)
                    if not early or UN * b + i >= 2:
                        dve.wait_ge(weighed, UN * b + i - 1)
                    dve.tensor_copy(pt[:, 1, :], ps_t[1][:]).then_inc(back_dve, 1)

            def o_norm(b, i, u, early):
                sums = ps_o[:, 0:2 * NH * (HD + 1)].rearrange("p (g d) -> p g d", d=HD + 1)
                dve.wait_ge(weighed, UN * b + UN)
                dve.reciprocal(inv[:, u, :], sums[:, :, HD]).then_inc(inverted, 1)
                dve.wait_ge(inverted, b + 1)
                if not early:
                    dve.wait_ge(o_turned, b - 1)
                dve.tensor_tensor(on[:, u], sums[:, :, 0:HD], inv[:, u, :, None].to_broadcast([P, 2 * NH, HD]), ALU.mult).then_inc(o_ready, 1)

            def add(b, i, u, early):
                rows = keep.t[:, bass.ds(2 * b, 2), :]
                dve.wait_ge(y_done, b + 1)
                dve.tensor_tensor(rows, rows, ps_v[:, 0:2 * C].rearrange("p (a b) -> p a b", b=C), ALU.add).then_inc(added, 1)
                dve.wait_ge(added, b + 1)
                for h in range(2):
                    dve.bn_stats(keep.tbn[:, 2 * b + h, :], keep.t[:, 2 * b + h, :]).then_inc(counted, 1)

            dve.wait_ge(const, 5)
            timetable(dve, [(17, False, o_norm), (2, False, x_out), (5, False, v), (7, True, centre), (10, True, back),
                            (19, False, add)])

        @block.tensor
        def _(pe):
            def turn_x(b, i, u, early):
                pe.wait_ge(normed, 2 * b + 2)
                if not early:
                    if not isinstance(b, int) or b >= 3:
                        pe.wait_ge(ot_ready, b - 2)
                if not isinstance(b, int) or b:
                    pe.wait_ge(xt_ready, b)
                for h in range(2):
                    last = pe.transpose(ps_x[:, h * P:(h + 1) * P], xn[:, u, h, :], keep.ident[:])
                last.then_inc(turned, 1)

            def project(b, i, u, early):
                pe.wait_ge(xt_ready, b + 1)
                if not isinstance(b, int) or b:
                    pe.wait_ge(qk_out, 2 * b)
                    pe.wait_ge(v_out, b)
                if not isinstance(b, int) or b >= 3:
                    pe.wait_ge(added, b - 2)
                for n in range(2):
                    last = pe.matmul(ps_qk[:, n * T:(n + 1) * T], wqk_s[:, n * C:(n + 1) * C], xt[:, u, :], start=True, stop=True)
                last.then_inc(qk_done, 1)
                for h in range(2):
                    last = pe.matmul(ps_v[:, h * C:(h + 1) * C], xt[:, u, h * P:(h + 1) * P], wv_s[:], start=True, stop=True)
                last.then_inc(v_done, 1)

            def score(b, i, u, early):
                tile, h0, heads, keys = unit(i)
                n = UN * b + i
                if i == 0:
                    pe.wait_ge(kx_ready, b + 1)
                if not early or UN * b + i >= 2:
                    pe.wait_ge(centred, n - 1)
                pe.matmul(ps_s[i % 2][:], ident_b[:], mask[:, tile, :], start=True, stop=False)
                pe.matmul(ps_s[i % 2][:], q[:, u, tile * P:(tile + 1) * P], kx[:, u, h0:h0 + heads, 0:keys],
                          start=False, stop=True).then_inc(scored, 1)

            def turn_e(b, i, u, early):
                pe.wait_ge(exped, UN * b + i + 1)
                if not early or UN * b + i >= 2:
                    pe.wait_ge(back_act if i % 2 == 0 else back_dve, 3 * b + i // 2)
                for n in range(4):
                    last = pe.transpose(ps_t[i % 2][:, n * P:(n + 1) * P], e[:, i % 3, n * P:(n + 1) * P], keep.ident[:])
                last.then_inc(e_turned, 1)

            def weigh(b, i, u, early):
                tile, h0, heads, keys = unit(i)
                pe.wait_ge(back_act if i % 2 == 0 else back_dve, 3 * b + i // 2 + 1)
                if i == 0 and (not isinstance(b, int) or b):
                    pe.wait_ge(o_ready, b)
                chunks = keys // P
                for n in range(heads):
                    h = h0 + n
                    at = (tile * NH + h) * (HD + 1)
                    for c in range(chunks):
                        last = pe.matmul(ps_o[:, at:at + HD + 1], pt[:, i % 2, (n * chunks + c) * P:(n * chunks + c + 1) * P],
                                         vx[:, u, c, h, :], start=(c == 0), stop=(c == chunks - 1))
                last.then_inc(weighed, 1)

            def turn_o(b, i, u, early):
                pe.wait_ge(o_ready, b + 1)
                pe.wait_ge(xt_ready, least(b, 3))
                if not isinstance(b, int) or b:
                    pe.wait_ge(ot_ready, b)
                for h in range(2):
                    last = pe.transpose(ps_x[:, h * P:(h + 1) * P], on[:, u, h * NH:(h + 1) * NH, :], keep.ident[:])
                last.then_inc(o_turned, 1)

            def project_o(b, i, u, early):
                pe.wait_ge(ot_ready, b + 1)
                pe.wait_ge(v_out, least(b, 3))
                if not isinstance(b, int) or b:
                    pe.wait_ge(added, b)
                for h in range(2):
                    last = pe.matmul(ps_v[:, h * C:(h + 1) * C], ot[:, u, h, :], wout_s[:], start=True, stop=True)
                last.then_inc(y_done, 1)

            pe.wait_ge(w_in, 48)
            pe.wait_ge(const, 5)
            timetable(pe, [(19, False, project_o), (1, False, turn_x), (3, False, project), (7, True, score),
                           (9, True, turn_e), (11, True, weigh), (18, False, turn_o)])


class Keep:
    pass


def hybrid(nc, a, out):
    q_dram = nc.dram_tensor("q_scratch", [P, B * T], F32, kind="Internal").ap()
    xs_dram = nc.dram_tensor("xs_scratch", [SLOTS, C], F32, kind="Internal").ap()
    ys_dram = nc.dram_tensor("ys_scratch", [SLOTS, C], F32, kind="Internal").ap()
    with ExitStack() as ctx:
        s = Space(nc, ctx)
        keep = Keep()
        keep.ident = s.sb("ident", [P, P])
        keep.ones = s.sb("ones", [P, P])
        keep.waited = s.sem("waited")
        keep.t = s.sb("tokens", [P, NT, C])
        keep.tbn = s.sb("tbn", [P, NT, 6])
        keep.tscale = s.sb("tscale", [P, NT])
        keep.tshift = s.sb("tshift", [P, NT])
        keep.head8 = s.sb("head8", [P, NH])

        with ExitStack() as conv:
            s = Space(nc, conv)
            keep.xc = s.sb("xc", [P, B, T])
            keep.group4 = s.sb("group4", [P, P])
            keep.bn = s.sb("bn", [P, B, 6])
            keep.mem_t = s.sb("mem_t", [P, MEM])
            keep.rstd, keep.shift, keep.rstd2, keep.shift2 = (
                s.sb(x, [P, B]) for x in ("rstd", "shift", "rstd2", "shift2"))
            keep.pad = s.sb("pad", [P, B, HH + 2, WW + 2])
            keep.w1s = s.sb("w1s", [P, 5, C])
            keep.w2t = s.sb("w2t_sb", [P, C])
            keep.gate = s.sb("gates", [P, 3, B])
            keep.zbias = s.sb("zbias", [P, B])
            prepare_and_first_norm(nc, s, a["x"], a["memory"], keep)
            memory_lookup(nc, s, a["memory"], xs_dram, keep)
            gates(nc, s, a["w1"], a["w1_t"], a["b1"], a["wa_t"], a["ba"], a["wb_t"], a["bb"], a["w2_t"], a["b2"], keep)
            shifted_convolution(nc, s, keep)

        token_stats(nc, s, keep, "norm2")
        with ExitStack() as attention:
            s = Space(nc, attention)
            keep.k_t = s.sb("k_t", [P, B * T])
            keep.vp = s.sb("vp", [P, NT, NH, HD + 1])
            soft_projections(nc, s, a["r_qkv"], a["r_wo"], q_dram, keep)
            rosa_attention(nc, s, q_dram, keep)

        def expert_layer(name, n, swiglu, router, loads, shared):
            token_stats(nc, s, keep, name + "_norm")
            with ExitStack() as layer:
                own = Space(nc, layer)
                m = Moe(own, name, n, swiglu)
                with ExitStack() as rows:
                    xn = Space(nc, rows).sb(name + "_xn", [P, NT, C])
                    route(nc, own, m, router, lambda sp: load_experts(sp, m, *loads), xn, keep)
                    dispatch(nc, own, m, xs_dram, xn, shared, keep)
                experts(nc, own, m, xs_dram, ys_dram, keep)
                combine(nc, own, m, ys_dram, keep)

        expert_layer("m2", 16, True, a["m2_router"], ([a["m2_gate"], a["m2_up"]], a["m2_down"]),
                     (a["m2_shared_up"], a["m2_shared_down"]))
        token_stats(nc, s, keep, "norm3")
        causal_attention(nc, s, a["c_qk"], a["c_v"], a["c_out"], keep)
        expert_layer("m3", 8, False, a["m3_router"], ([a["m3_w1"]], a["m3_w2"], a["m3_b1"], a["m3_b2"]), None)
        store_channels(nc, out, keep)


def store_channels(nc, out, keep):
    with ExitStack() as ctx:
        s = Space(nc, ctx)
        image = s.sb("out_image", [P, 4, T])
        ps_t = [s.ps(f"out_ps{i}", [P, 512]) for i in range(4)]
        turned = s.sem("out_turned")
        copied = s.sem("out_copied")
        stored = [s.sem(f"out_stored{i}") for i in range(4)]
        block = ctx.enter_context(nc.Block())

        @block.tensor
        def _(pe):
            for b in range(B):
                if b >= 4:
                    pe.wait_ge(copied, b - 3)
                for h in range(2):
                    last = pe.transpose(ps_t[b % 4][:, h * P:(h + 1) * P], keep.t[:, 2 * b + h, :], keep.ident[:])
                last.then_inc(turned, 1)

        @block.vector
        def _(dve):
            def copy(b, u, early):
                dve.wait_ge(turned, b + 1)
                if not early:
                    dve.wait_ge(stored[u], 4 * (b - u))
                dve.tensor_copy(image[:, u, :], ps_t[u][:, 0:T]).then_inc(copied, 1)

            in_turn(dve, B, 4, copy)

        @block.sync
        def _(sp):
            def store(b, u, early):
                sp.wait_ge(copied, b + 1)
                sp.dma_start(out[b].rearrange("c h w -> c (h w)"), image[:, u, :]).then_inc(stored[u], 16)

            in_turn(sp, B, 4, store)
            for u in range(4):
                sp.wait_ge(stored[u], 16 * B // 4)




def kernel(x, L0_conv_memory, L1_conv_w1, L1_conv_b1, L1_conv_wa, L1_conv_ba, L1_conv_wb, L1_conv_bb, L1_conv_w2,
           L1_conv_b2, L2_attn_wq, L2_attn_wk, L2_attn_wv, L2_attn_wo, L2_ffn_gate_w, L2_ffn_wg, L2_ffn_wu, L2_ffn_wd,
           L2_ffn_swg, L2_ffn_swu, L2_ffn_swd, L3_attn_w_qkv, L3_attn_w_out, L3_ffn_W_router, L3_ffn_W1, L3_ffn_b1,
           L3_ffn_W2, L3_ffn_b2):
    import concourse.bacc as bacc
    from concourse.bass_utils import run_bass_kernel_spmd

    def lay(v, *axes):
        v = np.asarray(v)
        return np.ascontiguousarray(v.transpose(*axes) if axes else v)

    def by_chunk(v):
        e, k, n = v.shape
        return lay(v.reshape(e, k // P, P, n), 2, 0, 1, 3)

    w_qkv_t = lay(L3_attn_w_qkv, 1, 0)
    arrays = {
        "x": lay(x), "memory": lay(L0_conv_memory),
        "w1": lay(L1_conv_w1), "w1_t": lay(L1_conv_w1, 1, 0), "b1": lay(np.asarray(L1_conv_b1).reshape(3, C), 1, 0),
        "wa_t": lay(L1_conv_wa, 1, 0), "ba": lay(np.asarray(L1_conv_ba).reshape(C, 1)),
        "wb_t": lay(L1_conv_wb, 1, 0), "bb": lay(np.asarray(L1_conv_bb).reshape(3, C), 1, 0),
        "w2_t": lay(L1_conv_w2, 1, 0), "b2": lay(np.asarray(L1_conv_b2).reshape(C, 1)),
        "r_qkv": np.concatenate([lay(L2_attn_wq), lay(L2_attn_wk), lay(L2_attn_wv)], axis=1), "r_wo": lay(L2_attn_wo),
        "m2_router": lay(L2_ffn_gate_w, 1, 0), "m2_gate": lay(L2_ffn_wg, 2, 0, 1), "m2_up": lay(L2_ffn_wu, 2, 0, 1),
        "m2_down": by_chunk(lay(L2_ffn_wd, 0, 2, 1)),
        "m2_shared_up": np.concatenate([lay(L2_ffn_swg, 1, 0), lay(L2_ffn_swu, 1, 0)], axis=1),
        "m2_shared_down": by_chunk(lay(L2_ffn_swd, 1, 0)[None])[:, 0],
        "c_qk": lay(w_qkv_t[:, 0:2 * C]), "c_v": lay(w_qkv_t[:, 2 * C:]), "c_out": lay(L3_attn_w_out, 1, 0),
        "m3_router": lay(L3_ffn_W_router), "m3_w1": lay(L3_ffn_W1, 1, 0, 2), "m3_b1": lay(L3_ffn_b1),
        "m3_w2": by_chunk(lay(L3_ffn_W2)), "m3_b2": lay(L3_ffn_b2),
    }
    nc = bacc.Bacc("TRN2", target_bir_lowering=False, num_devices=1)
    given = {n: nc.dram_tensor("in_" + n, v.shape, mybir.dt.from_np(v.dtype), kind="ExternalInput").ap()
             for n, v in arrays.items()}
    out = nc.dram_tensor("out", [B, C, HH, WW], F32, kind="ExternalOutput").ap()
    hybrid(nc, given, out)
    r = run_bass_kernel_spmd(nc, [{"in_" + n: v for n, v in arrays.items()}], core_ids=[0])
    return r.results[0]["out"]
```

```python
from contextlib import ExitStack

import concourse.bass as bass
from concourse import mybir
import numpy as np

F32 = mybir.dt.float32
BF16 = mybir.dt.bfloat16
I32 = mybir.dt.int32
U32 = mybir.dt.uint32
ALU = mybir.AluOpType
ACT = mybir.ActivationFunctionType
AX = mybir.AxisListType

P = 128
C = 128
B, HH, WW = 16, 16, 16
T = HH * WW
NT = B * T // P
MEM = 256
NH, HD = 8, 16
TOPK = 2
SLOTS = 80 * P
ROW = C + 1
BH = B * NH


class Space:

    def __init__(self, nc, ctx, spent):
        self.nc, self.ctx, self.spent = nc, ctx, spent
        self.sems = []
        ctx.callback(self.give_back)

    def sb(self, name, shape, dt=F32):
        return self.ctx.enter_context(self.nc.sbuf_tensor(name, shape, dt))

    def ps(self, name, shape, dt=F32):
        return self.ctx.enter_context(self.nc.psum_tensor(name, shape, dt))

    def sem(self, name):
        self.sems.append(self.nc.alloc_semaphore(name))
        return self.sems[-1]

    def give_back(self):
        self.spent += self.sems


def reuse_semaphores(nc, spent):
    nc.clear_and_free_semaphores(spent)
    nc.all_engine_barrier()
    spent.clear()


def in_turn(eng, n, depth, body):
    for j in range(min(depth, n)):
        body(j, j, True)
    if n > depth:
        assert n % depth == 0
        with eng.Fori(1, n // depth) as i:
            for u in range(depth):
                body(i * depth + u, u, False)


def lagged(eng, n, depth, parts):
    most = max(lag for lag, _ in parts)
    first = -(-(most + depth) // depth) * depth
    assert n % depth == 0 and n > first

    def step(k, slot, early_steps):
        for lag, body in parts:
            if not early_steps or 0 <= k - lag < n:
                body(k - lag, (slot - lag) % depth, early_steps and k - lag < depth)

    for k in range(first):
        step(k, k, True)
    with eng.Fori(first // depth, n // depth) as i:
        for u in range(depth):
            step(i * depth + u, u, False)
    for k in range(n, n + most):
        step(k, k, True)


def prepare_and_first_norm(nc, top, x, memory, keep):
    with ExitStack() as ctx:
        s = Space(nc, ctx, keep.spent)
        mem_rows = s.sb("mem_rows", [P, 2, C])
        mem_sq = s.sb("mem_sq", [P, 2, C])
        mem_norm = s.sb("mem_norm", [P, 4])
        ps_mem = s.ps("ps_mem", [P, 512])
        x_in = [s.sem(f"x_in{i}") for i in range(4)]
        mem_in = s.sem("mem_in")
        const_ready = s.sem("const_ready")
        mem_step = s.sem("mem_step")
        mem_len = s.sem("mem_len")
        mem_turned = s.sem("mem_turned")
        bn_done = s.sem("bn_done")
        g = norm_space(nc, s, "gn0")
        block = ctx.enter_context(nc.Block())

        @block.sync
        def _(sp):
            sp.dma_start(mem_rows[:], memory.rearrange("(m p) c -> p m c", p=P)).then_inc(mem_in, 16)
            for i in range(4):
                sp.dma_start(keep.xc[:, 4 * i:4 * i + 4, :],
                             x[4 * i:4 * i + 4].rearrange("b c h w -> c b (h w)")).then_inc(x_in[i], 16)

        @block.gpsimd
        def _(pool):
            pool.memset(keep.ident[:], 0.0).then_inc(const_ready, 1)
            pool.memset(keep.group4[:], 0.25).then_inc(const_ready, 1)
            pool.memset(keep.ones[:], 1.0).then_inc(const_ready, 1)
            pool.wait_ge(const_ready, 3)
            pool.affine_select(out=keep.ident[:], in_=keep.ident[:], compare_op=ALU.not_equal, fill=1.0,
                               base=0, pattern=[[-1, P]], channel_multiplier=1).then_inc(const_ready, 1)
            v = keep.group4[:].rearrange("p (g k) -> p g k", k=4)
            pool.affine_select(out=v, in_=v, compare_op=ALU.is_ge, fill=0.0,
                               base=0, pattern=[[-4, 32], [0, 4]], channel_multiplier=1).then_inc(const_ready, 1)
            pool.wait_ge(const_ready, 5)
            pool.affine_select(out=v, in_=v, compare_op=ALU.is_ge, fill=0.0,
                               base=3, pattern=[[4, 32], [0, 4]], channel_multiplier=-1).then_inc(const_ready, 1)

        @block.scalar
        def _(act):
            act.wait_ge(mem_len, 2)
            act.activation(mem_norm[:, 2:4], mem_norm[:, 0:2], ACT.Sqrt).then_inc(mem_len, 1)
            norm_scalar(act, g)

        @block.vector
        def _(dve):
            dve.wait_ge(mem_in, 16)
            for m in range(2):
                dve.tensor_tensor_reduce(mem_sq[:, m, :], mem_rows[:, m, :], mem_rows[:, m, :], 1.0, 0.0,
                                         ALU.mult, ALU.add, mem_norm[:, m:m + 1]).then_inc(mem_len, 1)
            dve.wait_ge(mem_len, 3)
            dve.tensor_scalar(mem_norm[:, 0:2], mem_norm[:, 2:4], 1e-12, None, ALU.max).then_inc(mem_len, 1)
            dve.wait_ge(mem_len, 4)
            dve.reciprocal(mem_norm[:, 2:4], mem_norm[:, 0:2]).then_inc(mem_len, 1)
            dve.wait_ge(mem_len, 5)
            for m in range(2):
                dve.tensor_scalar(mem_rows[:, m, :], mem_rows[:, m, :], mem_norm[:, 2 + m:3 + m], None,
                                  ALU.mult).then_inc(mem_step, 1)
            for i in range(4):
                dve.wait_ge(x_in[i], 16)
                with dve.Fori(4 * i, 4 * i + 4) as b:
                    dve.bn_stats(keep.bn[:, b, :], keep.xc[:, b, :]).then_inc(bn_done, 1)
            dve.wait_ge(mem_turned, 1)
            dve.tensor_copy(keep.mem_t[:], ps_mem[:, 0:MEM]).then_inc(mem_step, 1)
            dve.wait_ge(bn_done, B)
            norm_vector(dve, g, keep)

        @block.tensor
        def _(pe):
            pe.wait_ge(const_ready, 6)
            pe.wait_ge(mem_step, 2)
            for m in range(2):
                last = pe.transpose(ps_mem[:, m * P:(m + 1) * P], mem_rows[:, m, :], keep.ident[:])
            last.then_inc(mem_turned, 1)
            norm_tensor(pe, g, keep)


class norm_space:

    def __init__(self, nc, s, name):
        self.mv = s.sb(name + "_mv", [P, B, 2])
        self.both = s.sb(name + "_both", [P, 2, B])
        self.sq = s.sb(name + "_sq", [P, B])
        self.group = s.sb(name + "_group", [P, 2, B])
        self.gvar = s.sb(name + "_gvar", [P, B])
        self.gstd = s.sb(name + "_gstd", [P, B])
        self.ps = s.ps(name + "_ps", [P, 512])
        self.aggregated = s.sem(name + "_aggregated")
        self.channel = s.sem(name + "_channel")
        self.summed = s.sem(name + "_summed")
        self.step = s.sem(name + "_step")
        self.rstd = s.sem(name + "_rstd")


def norm_vector(dve, g, keep, eps=1e-5):
    for b in range(B):
        dve.bn_aggr(g.mv[:, b, :], keep.bn[:, b, :]).then_inc(g.aggregated, 1)
    dve.wait_ge(g.aggregated, B)
    mean, var = g.mv[:, :, 0], g.mv[:, :, 1]
    dve.tensor_tensor(g.sq[:], mean, mean, ALU.mult).then_inc(g.channel, 1)
    dve.tensor_copy(g.both[:, 0, :], mean).then_inc(g.channel, 1)
    dve.wait_ge(g.channel, 2)
    dve.tensor_tensor(g.both[:, 1, :], var, g.sq[:], ALU.add).then_inc(g.channel, 1)
    dve.wait_ge(g.summed, 1)
    dve.tensor_copy(g.group[:].rearrange("p a b -> p (a b)"), g.ps[:, 0:2 * B]).then_inc(g.step, 1)
    dve.wait_ge(g.step, 1)
    dve.tensor_tensor(g.sq[:], g.group[:, 0, :], g.group[:, 0, :], ALU.mult).then_inc(g.step, 1)
    dve.wait_ge(g.step, 2)
    dve.scalar_tensor_tensor(g.gvar[:], g.group[:, 1, :], eps, g.sq[:], ALU.add, ALU.subtract).then_inc(g.step, 1)
    dve.wait_ge(g.rstd, 1)
    dve.reciprocal(keep.rstd[:], g.gstd[:]).then_inc(g.step, 1)
    dve.wait_ge(g.step, 4)
    dve.scalar_tensor_tensor(keep.shift[:], g.group[:, 0, :], -1.0, keep.rstd[:], ALU.mult, ALU.mult).then_inc(g.step, 1)


def norm_scalar(act, g):
    act.wait_ge(g.step, 3)
    act.activation(g.gstd[:], g.gvar[:], ACT.Sqrt).then_inc(g.rstd, 1)


def norm_tensor(pe, g, keep):
    pe.wait_ge(g.channel, 3)
    pe.matmul(g.ps[:, 0:2 * B], keep.group4[:], g.both[:].rearrange("p a b -> p (a b)"),
              start=True, stop=True).then_inc(g.summed, 1)


def fill_slots(sp, xs_dram, empty, stored):
    rows = xs_dram.rearrange("(n p) c -> p n c", p=P)
    for i in range(0, SLOTS // P, 8):
        sp.dma_start(rows[:, i:i + 8], empty[:, i:i + 8]).then_inc(stored, 16)
    sp.wait_ge(stored, 16 * (SLOTS // P // 8))


def memory_lookup(nc, top, memory, xs_dram, keep):
    with ExitStack() as ctx:
        s = Space(nc, ctx, keep.spent)
        xn = s.sb("xn", [P, 2, 2, P])
        sq = s.sb("sq", [P, 2, 2, P])
        length = s.sb("length", [P, 2, 2])
        best = s.sb("best", [P, 2, 2, 8])
        where = s.sb("where", [P, 2, 2, 8], U32)
        least = s.sb("least", [P, 2, 2])
        hit = s.sb("hit", [P, 2, 2])
        row = s.sb("row", [P, 2, 2, C])
        rowm = s.sb("rowm", [P, 2, 2, C])
        ps_sim = [s.ps(f"ps_sim{i}", [P, 2, MEM]) for i in range(2)]
        ps_len = [s.ps(f"ps_len{i}", [P, 512]) for i in range(2)]
        ps_row = [s.ps(f"ps_row{i}", [P, 512]) for i in range(2)]
        zeroed = s.sem("slots_zeroed")
        slots_stored = s.sem("slots_stored")
        g = norm_space(nc, s, "gn1")
        normed = s.sem("l0_normed")
        squared = s.sem("l0_squared")
        similar = s.sem("l0_similar")
        len_ready = s.sem("l0_len_ready")
        peaked = s.sem("l0_peaked")
        indexed = s.sem("l0_indexed")
        least_ready = s.sem("l0_least_ready")
        hit_ready = s.sem("l0_hit_ready")
        gathered = [s.sem(f"l0_gathered{u}") for u in range(4)]
        masked = s.sem("l0_masked")
        turned = s.sem("l0_turned")
        added = s.sem("l0_added")
        bn_done = s.sem("l0_bn_done")
        block = ctx.enter_context(nc.Block())

        @block.scalar
        def _(act):
            def norm(b, u, early):
                if not early:
                    act.wait_ge(similar, b - 1)
                act.activation(xn[:, u].rearrange("p a b -> p (a b)"), keep.xc[:, b, :], ACT.Identity,
                               bias=keep.shift[:, bass.ds(b, 1)], scale=keep.rstd[:, bass.ds(b, 1)]).then_inc(normed, 1)

            def square(b, u, early):
                act.wait_ge(normed, b + 1)
                if not early:
                    act.wait_ge(similar, b - 1)
                act.activation(sq[:, u], xn[:, u], ACT.Square).then_inc(squared, 1)

            def length_out(b, u, early):
                act.wait_ge(similar, b + 1)
                if not early:
                    act.wait_ge(least_ready, b - 1)
                act.activation(length[:, u, :], ps_len[u][:, 0:2], ACT.Sqrt).then_inc(len_ready, 1)

            lagged(act, B, 2, [(3, length_out), (1, square), (0, norm)])
            norm_scalar(act, g)

        @block.tensor
        def _(pe):
            def compare(b, u, early):
                pe.wait_ge(squared, b + 1)
                if not early:
                    pe.wait_ge(indexed, 2 * (b - 1))
                    pe.wait_ge(len_ready, b - 1)
                for h in range(2):
                    pe.matmul(ps_sim[u][:, h, :], xn[:, u, h, :], keep.mem_t[:], start=True, stop=True)
                for h in range(2):
                    last = pe.matmul(ps_len[u][:, h:h + 1], sq[:, u, h, :], keep.ones[:, 0:1], start=True, stop=True)
                last.then_inc(similar, 1)

            def turn(b, u, early):
                pe.wait_ge(masked, 2 * b + 2)
                if not early:
                    pe.wait_ge(added, b - 1)
                for h in range(2):
                    last = pe.transpose(ps_row[u][:, h * P:(h + 1) * P], rowm[:, u, h, :], keep.ident[:])
                last.then_inc(turned, 1)

            lagged(pe, B, 2, [(7, turn), (2, compare)])
            norm_tensor(pe, g, keep)

        @block.gpsimd
        def _(pool):
            def gather(b, u, early):
                pool.wait_ge(indexed, 2 * b + 2)
                if not early:
                    pool.wait_ge(masked, 2 * (b - 1))
                pool.sem_inc(keep.waited)
                for h in range(2):
                    pool.indirect_dma_start(row[:, u, h, :], None, memory,
                                            bass.IndirectOffsetOnAxis(where[:, u, h, 0:1], 0)).then_inc(gathered[2 * u + h], 16)

            pool.memset(keep.empty[:].rearrange("p a b -> p (a b)"), 0.0).then_inc(zeroed, 1)
            pool.wait_ge(zeroed, 1)
            pool.iota(keep.empty[:, :, C].bitcast(I32), pattern=[[P, SLOTS // P]], base=TOPK * B * T, channel_multiplier=1).then_inc(zeroed, 1)
            lagged(pool, B, 2, [(4, gather)])

        @block.sync
        def _(sp):
            sp.wait_ge(zeroed, 2)
            fill_slots(sp, xs_dram, keep.empty, slots_stored)

        @block.vector
        def _(dve):
            def peak(b, u, early):
                dve.wait_ge(similar, b + 1)
                if not early:
                    dve.wait_ge(hit_ready, b - 1)
                dve.sem_inc(keep.waited)
                for h in range(2):
                    dve.max(best[:, u, h, :], ps_sim[u][:, h, :]).then_inc(peaked, 1)

            def index(b, u, early):
                dve.wait_ge(peaked, 2 * b + 2)
                if not early:
                    dve.wait_ge(gathered[2 * u], 8 * (b - u))
                    dve.wait_ge(gathered[2 * u + 1], 8 * (b - u))
                dve.sem_inc(keep.waited)
                for h in range(2):
                    dve.max_index(where[:, u, h, :], best[:, u, h, :], ps_sim[u][:, h, :]).then_inc(indexed, 1)

            def threshold(b, u, early):
                dve.wait_ge(len_ready, b + 1)
                if not early:
                    dve.wait_ge(hit_ready, b - 1)
                dve.tensor_scalar(least[:, u, :], length[:, u, :], 1e-12, 0.8, ALU.max, ALU.mult).then_inc(least_ready, 1)

            def decide(b, u, early):
                dve.wait_ge(peaked, 2 * b + 2)
                dve.wait_ge(least_ready, b + 1)
                if not early:
                    dve.wait_ge(masked, 2 * (b - 1))
                dve.tensor_tensor(hit[:, u, :], best[:, u, :, 0], least[:, u, :], ALU.is_gt).then_inc(hit_ready, 1)

            def mask(b, u, early):
                dve.wait_ge(hit_ready, b + 1)
                for h in range(2):
                    dve.wait_ge(gathered[2 * u + h], 8 * (b - u) + 16)
                    if not early:
                        dve.wait_ge(turned, b - 1)
                    dve.tensor_scalar(rowm[:, u, h, :], row[:, u, h, :], hit[:, u, h:h + 1], None,
                                      ALU.mult).then_inc(masked, 1)

            def add(b, u, early):
                dve.wait_ge(turned, b + 1)
                dve.tensor_tensor(keep.xc[:, b, :], keep.xc[:, b, :], ps_row[u][:, 0:T], ALU.add).then_inc(added, 1)

            def count(b, u, early):
                dve.wait_ge(added, b + 1)
                dve.bn_stats(keep.bn[:, b, :], keep.xc[:, b, :]).then_inc(bn_done, 1)

            lagged(dve, B, 2, [(6, mask), (5, decide), (3, peak), (3, index), (4, threshold), (8, add), (9, count)])
            dve.wait_ge(bn_done, B)
            k = SecondNorm(keep)
            norm_vector(dve, g, k)


class SecondNorm:

    def __init__(self, keep):
        self.bn, self.rstd, self.shift = keep.bn, keep.rstd2, keep.shift2


SHIFTS = [(0, 1), (2, 1), (1, 0), (1, 2), (1, 1)]
DOWN, UP, RIGHT, LEFT, STAY = range(5)
BRANCH_SHIFT = [[DOWN, UP, RIGHT, LEFT], [RIGHT, LEFT, DOWN, UP], [STAY] * 4]
GATE_OF_SHIFT = [0, 0, 1, 1, 2]
Q = 32


def gates(nc, top, w1_rows, w1_t, b1, wa_t, ba, wb_t, bb, w2_t, b2, keep):
    with ExitStack() as ctx:
        s = Space(nc, ctx, keep.spent)
        w1t = s.sb("w1t_sb", [P, 3 * C])
        wat = s.sb("wat_sb", [P, C])
        wbt = s.sb("wbt_sb", [P, 3 * C])
        b1s = s.sb("b1s", [P, 3])
        bas = s.sb("bas", [P, 1])
        bbs = s.sb("bbs", [P, 3])
        b2s = s.sb("b2s", [P, 1])
        bsum = s.sb("bsum", [P, 2])
        edge = s.sb("edge", [P, 5, B])
        diff = s.sb("diff", [P, 2, B])
        sums = s.sb("sums", [P, 5, B])
        pooled = s.sb("pooled", [P, B])
        hidden = s.sb("hidden", [P, B])
        hat = s.sb("hat", [P, 3, B])
        peak = s.sb("peak", [P, B])
        total = s.sb("total", [P, B])
        gate = s.sb("gate", [P, 3, B])
        mixed = s.sb("mixed", [P, B])
        ps_pool = s.ps("ps_pool", [P, 512])
        ps_hid = s.ps("ps_hid", [P, 512])
        ps_hat = s.ps("ps_hat", [P, 512])
        ps_bias = s.ps("ps_bias", [P, 512])
        w_in = s.sem("l1_w_in")
        rows_in = s.sem("l1_rows_in")
        zeroed = s.sem("l1_zeroed")
        padded = s.sem("l1_padded")
        padded_dve = s.sem("l1_padded_dve")
        edged = s.sem("l1_edged")
        summed = s.sem("l1_summed")
        pool_ps = s.sem("l1_pool_ps")
        pool_sb = s.sem("l1_pool_sb")
        hid_ps = s.sem("l1_hid_ps")
        hid_sb = s.sem("l1_hid_sb")
        hat_ps = s.sem("l1_hat_ps")
        soft = s.sem("l1_soft")
        exped = s.sem("l1_exped")
        bias_ps = s.sem("l1_bias_ps")
        block = ctx.enter_context(nc.Block())
        pad = keep.pad
        inner = pad[:, :, 1:17, 1:17]

        @block.sync
        def _(sp):
            for dst, src in ((w1t[:], w1_t), (wat[:], wa_t), (wbt[:], wb_t), (keep.w2t[:], w2_t),
                             (b1s[:], b1), (bas[:], ba),
                             (bbs[:], bb), (b2s[:], b2)):
                sp.dma_start(dst, src).then_inc(w_in, 16)
            sp.wait_ge(zeroed, 1)
            for k in range(2):
                for q in range(4):
                    sp.dma_start(keep.w1s[Q * q:Q * q + Q, BRANCH_SHIFT[k][q], :],
                                 w1_rows[k * C + Q * q:k * C + Q * q + Q, :]).then_inc(rows_in, 16)
            sp.dma_start(keep.w1s[:, STAY, :], w1_rows[2 * C:3 * C, :]).then_inc(rows_in, 16)
            sp.wait_ge(rows_in, 16 * 9)

        @block.gpsimd
        def _(pool):
            pool.memset(keep.w1s[:], 0.0).then_inc(zeroed, 1)

        @block.scalar
        def _(act):
            with act.Fori(0, B // 2) as b:
                act.activation(pad[:, b, 1:17, 1:17], keep.xc[:, b, :].rearrange("p (h w) -> p h w", w=WW),
                               ACT.Identity, bias=keep.shift2[:, bass.ds(b, 1)],
                               scale=keep.rstd2[:, bass.ds(b, 1)]).then_inc(padded, 1)
            act.wait_ge(hid_ps, 1)
            act.activation(hidden[:], ps_hid[:, 0:B], ACT.Gelu, bias=bas[:, 0:1]).then_inc(hid_sb, 1)
            act.wait_ge(soft, 6)
            act.activation(gate[:], hat[:], ACT.Exp).then_inc(exped, 1)

        @block.vector
        def _(dve):
            with dve.Fori(B // 2, B) as b:
                dve.tensor_scalar(pad[:, b, 1:17, 1:17], keep.xc[:, b, :].rearrange("p (h w) -> p h w", w=WW),
                                  keep.rstd2[:, bass.ds(b, 1)], keep.shift2[:, bass.ds(b, 1)], ALU.mult, ALU.add).then_inc(padded_dve, 1)
            dve.wait_ge(padded, B // 2)
            dve.wait_ge(padded_dve, B // 2)
            for dst, src in ((pad[:, :, 0, 1:17], pad[:, :, 1, 1:17]), (pad[:, :, 17, 1:17], pad[:, :, 16, 1:17]),
                             (pad[:, :, 1:17, 0], pad[:, :, 1:17, 1]), (pad[:, :, 1:17, 17], pad[:, :, 1:17, 16])):
                dve.tensor_copy(dst, src).then_inc(edged, 1)
            for n, src in enumerate((pad[:, :, 1, 1:17], pad[:, :, 16, 1:17], pad[:, :, 1:17, 1], pad[:, :, 1:17, 16])):
                dve.tensor_reduce(edge[:, n, :], src, AX.X, ALU.add).then_inc(summed, 1)
            dve.tensor_reduce(sums[:, STAY, :], inner, AX.XY, ALU.add).then_inc(summed, 1)
            dve.wait_ge(summed, 5)
            dve.tensor_tensor(diff[:, 0, :], edge[:, 0, :], edge[:, 1, :], ALU.subtract).then_inc(summed, 1)
            dve.tensor_tensor(diff[:, 1, :], edge[:, 2, :], edge[:, 3, :], ALU.subtract).then_inc(summed, 1)
            dve.wait_ge(summed, 7)
            for n, (d, op) in enumerate(((0, ALU.add), (0, ALU.subtract), (1, ALU.add), (1, ALU.subtract))):
                dve.tensor_tensor(sums[:, n, :], sums[:, STAY, :], diff[:, d, :], op).then_inc(summed, 1)
            dve.wait_ge(w_in, 16 * 8)
            dve.tensor_reduce(bsum[:, 0:1], b1s[:], AX.X, ALU.add).then_inc(pool_sb, 1)
            dve.wait_ge(pool_sb, 1)
            dve.tensor_scalar(bsum[:, 1:2], bsum[:, 0:1], float(T), None, ALU.mult).then_inc(pool_sb, 1)
            dve.wait_ge(pool_ps, 1)
            dve.wait_ge(pool_sb, 2)
            dve.tensor_scalar(pooled[:], ps_pool[:, 0:B], bsum[:, 1:2], None, ALU.add).then_inc(pool_sb, 1)
            dve.wait_ge(hat_ps, 1)
            for k in range(3):
                dve.tensor_scalar(hat[:, k, :], ps_hat[:, k * B:(k + 1) * B], bbs[:, k:k + 1], None, ALU.add).then_inc(soft, 1)
            dve.wait_ge(soft, 3)
            dve.tensor_tensor(peak[:], hat[:, 0, :], hat[:, 1, :], ALU.max).then_inc(soft, 1)
            dve.wait_ge(soft, 4)
            dve.tensor_tensor(peak[:], peak[:], hat[:, 2, :], ALU.max).then_inc(soft, 1)
            dve.wait_ge(soft, 5)
            dve.tensor_tensor(hat[:], hat[:], peak[:, None, :].to_broadcast([P, 3, B]), ALU.subtract).then_inc(soft, 1)
            dve.wait_ge(exped, 1)
            dve.tensor_tensor(total[:], gate[:, 0, :], gate[:, 1, :], ALU.add).then_inc(soft, 1)
            dve.wait_ge(soft, 7)
            dve.tensor_tensor(total[:], total[:], gate[:, 2, :], ALU.add).then_inc(soft, 1)
            dve.wait_ge(soft, 8)
            dve.reciprocal(peak[:], total[:]).then_inc(soft, 1)
            dve.wait_ge(soft, 9)
            dve.tensor_tensor(gate[:], gate[:], peak[:, None, :].to_broadcast([P, 3, B]), ALU.mult).then_inc(soft, 1)
            dve.wait_ge(soft, 10)
            for half, (a, b) in enumerate(((0, 1), (1, 0))):
                rows = slice(64 * half, 64 * half + 64)
                dve.tensor_copy(keep.gate[rows, 0, :], gate[rows, a, :]).then_inc(soft, 1)
                dve.tensor_copy(keep.gate[rows, 1, :], gate[rows, b, :]).then_inc(soft, 1)
            dve.tensor_copy(keep.gate[:, 2, :], gate[:, 2, :]).then_inc(soft, 1)
            dve.tensor_scalar(mixed[:], gate[:, 0, :], b1s[:, 0:1], None, ALU.mult).then_inc(soft, 1)
            for k in (1, 2):
                dve.wait_ge(soft, 15 + k)
                dve.scalar_tensor_tensor(mixed[:], gate[:, k, :], b1s[:, k:k + 1], mixed[:], ALU.mult, ALU.add).then_inc(soft, 1)
            dve.wait_ge(bias_ps, 1)
            dve.tensor_scalar(keep.zbias[:], ps_bias[:, 0:B], b2s[:, 0:1], None, ALU.add).then_inc(soft, 1)

        @block.tensor
        def _(pe):
            pe.wait_ge(w_in, 16 * 8)
            pe.wait_ge(summed, 11)
            for q in range(4):
                for k in range(3):
                    last = pe.matmul(ps_pool[Q * q:Q * q + Q, 0:B], w1t[:, k * C + Q * q:k * C + Q * q + Q],
                                     sums[:, BRANCH_SHIFT[k][q], :], start=(k == 0), stop=(k == 2))
            last.then_inc(pool_ps, 1)
            pe.wait_ge(pool_sb, 3)
            pe.matmul(ps_hid[:, 0:B], wat[:], pooled[:], start=True, stop=True).then_inc(hid_ps, 1)
            pe.wait_ge(hid_sb, 1)
            for k in range(3):
                last = pe.matmul(ps_hat[:, k * B:(k + 1) * B], wbt[:, k * C:(k + 1) * C], hidden[:], start=True, stop=True)
            last.then_inc(hat_ps, 1)
            pe.wait_ge(soft, 18)
            pe.matmul(ps_bias[:, 0:B], keep.w2t[:], mixed[:], start=True, stop=True).then_inc(bias_ps, 1)


def shifted_convolution(nc, top, xs_dram, keep):
    with ExitStack() as ctx:
        s = Space(nc, ctx, keep.spent)
        w2g = s.sb("w2g", [P, 2, 3, C])
        both = s.sb("both", [P, 2, 5, C])
        xnew = s.sb("xnew", [P, 2, 2, P])
        ps_both = [s.ps(f"ps_both{i}", [P, 2, 512]) for i in range(2)]
        ps_z = [s.ps(f"ps_z{i}", [P, 512]) for i in range(2)]
        ps_t = [s.ps(f"ps_t{i}", [P, 512]) for i in range(2)]
        gated = s.sem("cv_gated")
        joined = s.sem("cv_joined")
        copied = s.sem("cv_copied")
        shifted = s.sem("cv_shifted")
        added = s.sem("cv_added")
        turned = s.sem("cv_turned")
        stored = s.sem("cv_stored")
        slots_stored = s.sem("cv_slots_stored")
        counted = s.sem("cv_counted")
        block = ctx.enter_context(nc.Block())

        @block.sync
        def _(sp):
            fill_slots(sp, xs_dram, keep.empty, slots_stored)

        @block.vector
        def _(dve):
            def gate(b, u, early):
                if not early:
                    dve.wait_ge(joined, b - 1)
                for k in range(3):
                    dve.tensor_scalar(w2g[:, u, k, :], keep.w2t[:], keep.gate[:, k, bass.ds(b, 1)], None,
                                      ALU.mult).then_inc(gated, 1)

            def add(b, u, early):
                dve.wait_ge(shifted, b + 1)
                if not early:
                    dve.wait_ge(turned, b - 1)
                dve.scalar_tensor_tensor(xnew[:, u].rearrange("p a b -> p (a b)"), ps_z[u][:, 0:T],
                                         keep.zbias[:, bass.ds(b, 1)], keep.xc[:, b, :], ALU.add, ALU.add).then_inc(added, 1)

            def count(b, u, early):
                dve.wait_ge(stored, b + 1)
                for h in range(2):
                    dve.bn_stats(keep.tbn[:, 2 * b + h, :], keep.t[:, 2 * b + h, :]).then_inc(counted, 1)

            lagged(dve, B, 2, [(7, count), (4, add), (0, gate)])

        @block.scalar
        def _(act):
            def copy(b, u, early):
                act.wait_ge(joined, b + 1)
                if not early:
                    act.wait_ge(shifted, b - 1)
                act.activation(both[:, u, 0:4, :], ps_both[u][:, 0, :].rearrange("p (a b) -> p a b", b=C), ACT.Copy).then_inc(copied, 1)
                act.activation(both[:, u, 4, :], ps_both[u][:, 1, 0:C], ACT.Copy).then_inc(copied, 1)

            def store(b, u, early):
                act.wait_ge(turned, b + 1)
                act.activation(keep.t[:, bass.ds(2 * b, 2), :], ps_t[u][:, 0:T].rearrange("p (a b) -> p a b", b=C),
                               ACT.Copy).then_inc(stored, 1)

            lagged(act, B, 2, [(6, store), (2, copy)])

        @block.tensor
        def _(pe):
            def join(b, u, early):
                pe.wait_ge(gated, 3 * b + 3)
                if not early:
                    pe.wait_ge(copied, 2 * (b - 1))
                for n in range(5):
                    last = pe.matmul(ps_both[u][:, n // 4, n % 4 * C:n % 4 * C + C], keep.w1s[:, n, :],
                                     w2g[:, u, GATE_OF_SHIFT[n], :], start=True, stop=True)
                last.then_inc(joined, 1)

            def shift(b, u, early):
                pe.wait_ge(copied, 2 * b + 2)
                if not early:
                    pe.wait_ge(added, b - 1)
                for n, (di, dj) in enumerate(SHIFTS):
                    last = pe.matmul(ps_z[u][:, 0:T], both[:, u, n, :], keep.pad[:, b, di:di + HH, dj:dj + WW],
                                     start=(n == 0), stop=(n == 4))
                last.then_inc(shifted, 1)

            def turn(b, u, early):
                pe.wait_ge(added, b + 1)
                if not early:
                    pe.wait_ge(stored, b - 1)
                for h in range(2):
                    last = pe.transpose(ps_t[u][:, h * P:(h + 1) * P], xnew[:, u, h, :], keep.ident[:])
                last.then_inc(turned, 1)

            lagged(pe, B, 2, [(5, turn), (3, shift), (1, join)])


class TokenNorm:

    def __init__(self, s, keep, name, first=0, end=NT, eps=1e-5):
        self.keep, self.first, self.end, self.eps = keep, first, end, eps
        self.mv = s.sb(name + "_mv", [P, end - first, 2])
        self.var = s.sb(name + "_var", [P, end - first])
        self.aggregated = s.sem(name + "_aggregated")
        self.varied = s.sem(name + "_varied")
        self.rooted = s.sem(name + "_rooted")
        self.inverted = s.sem(name + "_inverted")
        self.ready = s.sem(name + "_ready")

    def collect(self, dve):
        for j in range(self.first, self.end):
            dve.bn_aggr(self.mv[:, j - self.first, :], self.keep.tbn[:, j, :]).then_inc(self.aggregated, 1)
        dve.wait_ge(self.aggregated, self.end - self.first)
        dve.tensor_scalar(self.var[:], self.mv[:, :, 1], self.eps, None, ALU.add).then_inc(self.varied, 1)

    def root(self, act):
        act.wait_ge(self.varied, 1)
        act.activation(self.keep.tscale[:, self.first:self.end], self.var[:], ACT.Sqrt).then_inc(self.rooted, 1)

    def finish(self, dve):
        scale, shift = (v[:, self.first:self.end] for v in (self.keep.tscale, self.keep.tshift))
        dve.wait_ge(self.rooted, 1)
        dve.reciprocal(scale, scale).then_inc(self.inverted, 1)
        dve.wait_ge(self.inverted, 1)
        dve.scalar_tensor_tensor(shift, self.mv[:, :, 0], -1.0, scale, ALU.mult, ALU.mult).then_inc(self.ready, 1)


def soft_projections(nc, top, wqkv, wo, q_dram, keep):
    NG = 3 * NH
    with ExitStack() as ctx:
        s = Space(nc, ctx, keep.spent)
        w = s.sb("r_w", [P, 3 * C])
        q_t = s.sb("r_q_t", [P, B * T])
        q_out = s.sem("r_q_out")
        wos = s.sb("r_wo", [P, HD])
        wod = s.sb("r_wod", [P, NH, HD])
        xn = s.sb("r_xn", [P, 2, C])
        xt = s.sb("r_xt", [P, 2, P])
        peak = s.sb("r_peak", [P, 2, NG])
        e = s.sb("r_e", [P, 2, NG, HD])
        ex = s.sb("r_ex", [P, 2, NG, HD])
        total = s.sb("r_total", [P, 2, NG])
        inv = s.sb("r_inv", [P, 2, NG])
        soft = s.sb("r_soft", [P, 2, NG, HD])
        vt = s.sb("r_vt", [P, 2, P])
        ps_x = [s.ps(f"r_ps_x{i}", [P, 512]) for i in range(2)]
        ps_q = [s.ps(f"r_ps_q{i}", [P, 512]) for i in range(2)]
        ps_t = [s.ps(f"r_ps_t{i}", [P, 512]) for i in range(2)]
        ps_v = [s.ps(f"r_ps_v{i}", [P, 512]) for i in range(2)]
        norm_of = TokenNorm(s, keep, "norm2")
        w_in = s.sem("r_w_in")
        spread = s.sem("r_spread")
        normed = s.sem("r_normed")
        turned = s.sem("r_turned")
        xt_ready = s.sem("r_xt_ready")
        projected = s.sem("r_projected")
        peaked = s.sem("r_peaked")
        centred = s.sem("r_centred")
        exped = s.sem("r_exped")
        summed = s.sem("r_summed")
        inverted = s.sem("r_inverted")
        softened = s.sem("r_softened")
        soft_turned = s.sem("r_soft_turned")
        unpacked = s.sem("r_unpacked")
        mixed = s.sem("r_mixed")
        v_ready = s.sem("r_v_ready")
        block = ctx.enter_context(nc.Block())

        @block.sync
        def _(sp):
            sp.dma_start(w[:], wqkv).then_inc(w_in, 16)
            sp.dma_start(wos[:], wo).then_inc(w_in, 16)
            for i in range(4):
                sp.wait_ge(unpacked, 3 * NT // 4 * (i + 1))
                part = slice(i * B * T // 4, (i + 1) * B * T // 4)
                sp.dma_start(q_dram[:, part], q_t[:, part]).then_inc(q_out, 16)
            sp.wait_ge(q_out, 64)

        @block.gpsimd
        def _(pool):
            pool.memset(keep.head8[:], 1.0).then_inc(spread, 1)
            pool.memset(keep.vp[:], 1.0).then_inc(spread, 1)
            pool.wait_ge(w_in, 32)
            pool.tensor_copy(wod[:], wos[:, None, :].to_broadcast([P, NH, HD])).then_inc(spread, 1)
            pool.wait_ge(spread, 3)
            for n, (v, pat) in enumerate(((wod[:], [0, HD]), (keep.head8[:], None))):
                more = [pat] if pat else []
                pool.affine_select(out=v, in_=v, compare_op=ALU.is_ge, fill=0.0, base=0,
                                   pattern=[[-HD, NH]] + more, channel_multiplier=1).then_inc(spread, 1)
            pool.wait_ge(spread, 5)
            for n, (v, pat) in enumerate(((wod[:], [0, HD]), (keep.head8[:], None))):
                more = [pat] if pat else []
                pool.affine_select(out=v, in_=v, compare_op=ALU.is_ge, fill=0.0, base=HD - 1,
                                   pattern=[[HD, NH]] + more, channel_multiplier=-1).then_inc(spread, 1)

            def soften(j, u, early):
                pool.wait_ge(inverted, j + 1)
                if not early:
                    pool.wait_ge(soft_turned, j - 1)
                pool.tensor_tensor(soft[:, u], ex[:, u], inv[:, u, :, None].to_broadcast([P, NG, HD]), ALU.mult).then_inc(softened, 1)

            lagged(pool, NT, 2, [(6, soften)])

        @block.scalar
        def _(act):
            def norm(j, u, early):
                if not early:
                    act.wait_ge(turned, j - 1)
                act.activation(xn[:, u, :], keep.t[:, j, :], ACT.Identity, bias=keep.tshift[:, bass.ds(j, 1)],
                               scale=keep.tscale[:, bass.ds(j, 1)]).then_inc(normed, 1)

            def exp(j, u, early):
                act.wait_ge(centred, j + 1)
                if not early:
                    act.wait_ge(softened, j - 1)
                act.activation(ex[:, u], e[:, u], ACT.Exp, scale=10.0).then_inc(exped, 1)

            def unpack(j, u, early):
                act.wait_ge(soft_turned, j + 1)
                act.activation(q_t[:, bass.ds(j * P, P)], ps_t[u][:, 0:P], ACT.Copy).then_inc(unpacked, 1)
                act.activation(keep.k_t[:, bass.ds(j * P, P)], ps_t[u][:, P:2 * P], ACT.Copy).then_inc(unpacked, 1)
                if not early:
                    act.wait_ge(mixed, j - 1)
                act.activation(vt[:, u, :], ps_t[u][:, 2 * P:3 * P], ACT.Copy).then_inc(unpacked, 1)

            norm_of.root(act)
            act.wait_ge(norm_of.ready, 1)
            lagged(act, NT, 2, [(8, unpack), (5, exp), (0, norm)])

        @block.vector
        def _(dve):
            def x_out(j, u, early):
                dve.wait_ge(turned, j + 1)
                if not early:
                    dve.wait_ge(projected, j - 1)
                dve.tensor_copy(xt[:, u, :], ps_x[u][:, 0:P]).then_inc(xt_ready, 1)

            def find_peak(j, u, early):
                dve.wait_ge(projected, j + 1)
                if not early:
                    dve.wait_ge(centred, j - 1)
                dve.tensor_reduce(peak[:, u, :], ps_q[u][:, 0:3 * C].rearrange("p (g d) -> p g d", d=HD),
                                  AX.X, ALU.max).then_inc(peaked, 1)

            def centre(j, u, early):
                dve.wait_ge(peaked, j + 1)
                if not early:
                    dve.wait_ge(exped, j - 1)
                dve.tensor_tensor(e[:, u], ps_q[u][:, 0:3 * C].rearrange("p (g d) -> p g d", d=HD),
                                  peak[:, u, :, None].to_broadcast([P, NG, HD]), ALU.subtract).then_inc(centred, 1)

            def add_up(j, u, early):
                dve.wait_ge(exped, j + 1)
                if not early:
                    dve.wait_ge(inverted, j - 1)
                dve.tensor_reduce(total[:, u, :], ex[:, u], AX.X, ALU.add).then_inc(summed, 1)

            def invert(j, u, early):
                dve.wait_ge(summed, j + 1)
                if not early:
                    dve.wait_ge(softened, j - 1)
                dve.reciprocal(inv[:, u, :], total[:, u, :]).then_inc(inverted, 1)

            def v_out(j, u, early):
                dve.wait_ge(mixed, j + 1)
                dve.tensor_copy(keep.vp[:, j, :, 0:HD], ps_v[u][:, 0:C].rearrange("p (h d) -> p h d", d=HD)).then_inc(v_ready, 1)

            norm_of.collect(dve)
            norm_of.finish(dve)
            dve.wait_ge(spread, 7)
            lagged(dve, NT, 2, [(6, add_up), (4, find_peak), (6, invert), (4, centre), (10, v_out), (2, x_out)])

        @block.tensor
        def _(pe):
            def turn(j, u, early):
                pe.wait_ge(normed, j + 1)
                if not early:
                    pe.wait_ge(xt_ready, j - 1)
                pe.transpose(ps_x[u][:, 0:P], xn[:, u, :], keep.ident[:]).then_inc(turned, 1)

            def project(j, u, early):
                pe.wait_ge(xt_ready, j + 1)
                if not early:
                    pe.wait_ge(centred, j - 1)
                pe.matmul(ps_q[u][:, 0:3 * C], xt[:, u, :], w[:], start=True, stop=True).then_inc(projected, 1)

            def turn_soft(j, u, early):
                pe.wait_ge(softened, j + 1)
                if not early:
                    pe.wait_ge(unpacked, 3 * (j - 1))
                for n in range(3):
                    last = pe.transpose(ps_t[u][:, n * P:(n + 1) * P], soft[:, u, n * NH:(n + 1) * NH, :], keep.ident[:])
                last.then_inc(soft_turned, 1)

            def mix(j, u, early):
                pe.wait_ge(unpacked, 3 * j + 3)
                if not early:
                    pe.wait_ge(v_ready, j - 1)
                pe.matmul(ps_v[u][:, 0:C], vt[:, u, :], wod[:], start=True, stop=True).then_inc(mixed, 1)

            pe.wait_ge(w_in, 32)
            pe.wait_ge(spread, 7)
            lagged(pe, NT, 2, [(9, mix), (7, turn_soft), (3, project), (1, turn)])


QUARTER = 64
GROUP = 4
NGROUP = T // GROUP
PER_Q = QUARTER // GROUP
ZR = 3
QX = 3
PAIRS = B // 2


def rosa_attention(nc, top, q_dram, keep):
    with ExitStack() as ctx:
        s = Space(nc, ctx, keep.spent)
        held = [s.sb(f"a_held{i}", [P, QUARTER, BH]) for i in range(4)]
        qx = s.sb("a_qx", [P, QX, QUARTER, NH])
        q_in = s.sb("a_q_in", [P, 4, QUARTER])
        iota = s.sb("a_iota", [P, T])
        prior = s.sb("a_prior", [P, 4, T])
        y = s.sb("a_y", [P, 2, T + 1])
        z = s.sb("a_z", [P, ZR, GROUP, T])
        peak = s.sb("a_peak", [P, 2, GROUP])
        bias = s.sb("a_bias", [P, 2, GROUP])
        inv = s.sb("a_inv", [P, 2, 2, NH])
        o = s.sb("a_o", [P, 2, 2, NH, HD])
        iota_i = held[3][:, 0:2, :].rearrange("p a b -> p (a b)").bitcast(I32)
        ps_row = [s.ps(f"a_ps_row{i}", [P, 2, 512]) for i in range(2)]
        ps_back = [s.ps(f"a_ps_back{i}", [P, 512]) for i in range(2)]
        ps_score = s.ps("a_ps_score", [P, 512])
        ps_o = s.ps("a_ps_o", [P, 512])
        iota_ready = s.sem("a_iota_ready")
        q_loaded = [s.sem(f"a_q_loaded{i}") for i in range(4)]
        cleared = s.sem("a_cleared")
        qx_dve = s.sem("a_qx_dve")
        qx_pool = s.sem("a_qx_pool")
        scored = s.sem("a_scored")
        score_held = s.sem("a_score_held")
        row_turned = s.sem("a_row_turned")
        prior_ready = s.sem("a_prior_ready")
        scanned = s.sem("a_scanned")
        peaked = s.sem("a_peaked")
        bias_ready = s.sem("a_bias_ready")
        exped = s.sem("a_exped")
        back_turned = s.sem("a_back_turned")
        back_act = s.sem("a_back_act")
        back_dve = s.sem("a_back_dve")
        summed = s.sem("a_summed")
        inverted = s.sem("a_inverted")
        scaled = s.sem("a_scaled")
        added = s.sem("a_added")
        counted = s.sem("a_counted")
        block = ctx.enter_context(nc.Block())

        place = [[0], [1], [2, 3], [0, 1]]
        chunks = [1, 1, 2, 2]
        units = [(None, 0, b, (0,)) for b in range(B)]
        for i in range(PER_Q):
            units += [(i, 1, b, (0,)) for b in range(B) if 14 * b // B == i]
            units += [(i, 2, b, (0, 1)) for b in range(B // 2) if 1 + 3 * b // 2 == i]
        for i in range(PER_Q):
            units += [(PER_Q + i, 2, b, (0, 1)) for b in range(B // 2, B) if 3 * (b - B // 2) // 2 == i]
            units += [(PER_Q + i, 3, b, (0,)) for b in range(B) if 3 + 11 * b // B == i]
        for i in range(PER_Q):
            units += [(2 * PER_Q + i, 3, b, (1,)) for b in range(B) if 3 + 11 * b // B == i]
        U = len(units)
        assert U == 5 * B
        items = [(n, k) for n in range(U) for k in units[n][3]]
        item_no = {item: no for no, item in enumerate(items)}

        def by_dve(n):
            return units[n][0] is None or units[n][0] < PER_Q

        dve_units = sum(by_dve(n) for n in range(U))

        def wait_spread(eng, n):
            if by_dve(n):
                eng.wait_ge(qx_dve, n + 1)
            else:
                eng.wait_ge(qx_pool, n - dve_units + 1)

        def units_at(g):
            return [n for n in range(U) if units[n][0] == g]

        def items_before(q):
            return sum(units[n][0] is None or units[n][0] < PER_Q * q for n, _ in items)

        def score_buffer(no):
            return ps_score if no >= items_before(2) or no % 2 == 0 else ps_row[0][:, 1]

        def spread(eng, n, done):
            if n >= QX:
                eng.wait_ge(scored, item_no[n - QX, units[n - QX][3][-1]] + 1)
            eng.wait_ge(q_loaded[n % 4], 16 * (n // 4 + 1))
            eng.tensor_tensor(qx[:, n % QX], q_in[:, n % 4, :, None].to_broadcast([P, QUARTER, NH]),
                              keep.head8[:, None, :].to_broadcast([P, QUARTER, NH]), ALU.mult).then_inc(done, 1)

        back_no = {}
        for g in range(NGROUP):
            for k in range(chunks[g // PER_Q]):
                back_no[g, k] = len(back_no)

        def before(no):
            return (no + 1) // 2, no // 2

        def sums_at(g):
            q, i = divmod(g, PER_Q)
            return [(q - 1, i - 2)] if q >= 1 and 2 <= i < 2 + PAIRS else []

        def sum_buffer(q, m):
            return ps_score if q >= 2 and m % 2 else ps_o

        last_sums = [(3, m) for m in range(PAIRS)]

        @block.tensor
        def _(pe):
            def score(n, k):
                _, q, b, _ = units[n]
                no = item_no[n, k]
                wait_spread(pe, n)
                if no >= items_before(2):
                    pe.wait_ge(score_held, no)
                elif no >= 2:
                    pe.wait_ge(score_held, no - 1)
                pe.matmul(score_buffer(no)[:], keep.k_t[:, (2 * b + k) * P:(2 * b + k + 1) * P],
                          qx[:, n % QX], start=True, stop=True).then_inc(scored, 1)

            def turn_rows(g):
                q = g // PER_Q
                pe.wait_ge(score_held, items_before(q))
                if g >= 2:
                    pe.wait_ge(scanned, GROUP * (g - 1))
                for i in range(GROUP):
                    for k in range(chunks[q]):
                        at = (i * chunks[q] + k) * P
                        last = pe.transpose(ps_row[g % 2][:, at // 512, at % 512:at % 512 + P],
                                            held[place[q][k]][:, GROUP * g % QUARTER + i, :], keep.ident[:])
                last.then_inc(row_turned, 1)

            def turn_back(g):
                q = g // PER_Q
                pe.wait_ge(exped, GROUP * (g + 1))
                for k in range(chunks[q]):
                    no = back_no[g, k]
                    if no >= 2:
                        a, d = before(no - 1)
                        if no % 2 == 0:
                            pe.wait_ge(back_act, a)
                        else:
                            pe.wait_ge(back_dve, d)
                    for i in range(GROUP):
                        last = pe.transpose(ps_back[no % 2][:, i * P:(i + 1) * P],
                                            z[:, g % ZR, i, k * P:(k + 1) * P], keep.ident[:])
                    last.then_inc(back_turned, 1)

            def weigh(q, m):
                n = PAIRS * q + m
                if m == 0:
                    a, d = before(back_no[PER_Q * q + PER_Q - 1, chunks[q] - 1] + 1)
                    pe.wait_ge(back_act, a)
                    pe.wait_ge(back_dve, d)
                if q >= 2:
                    pe.wait_ge(scaled, n - 1)
                elif n:
                    pe.wait_ge(scaled, n)
                ps_sum = sum_buffer(q, m)
                rows = slice(QUARTER * (q % 2), QUARTER * (q % 2) + QUARTER)
                for i in range(2):
                    b = 2 * m + i
                    for h in range(NH):
                        at = (NH * i + h) * (HD + 1)
                        for k in range(chunks[q]):
                            last = pe.matmul(ps_sum[rows, at:at + HD + 1], held[place[q][k]][:, :, NH * b + h],
                                             keep.vp[:, 2 * b + k, h, :], start=(k == 0), stop=(k == chunks[q] - 1))
                last.then_inc(summed, 1)

            for n in range(B):
                score(n, 0)
            turn_rows(0)
            for g in range(NGROUP):
                beside = [(n, k) for n in units_at(g) for k in units[n][3]]
                if g + 1 < NGROUP:
                    turn_rows(g + 1)
                for q, m in sums_at(g):
                    weigh(q, m)
                for item in beside[:2]:
                    score(*item)
                if g >= 1:
                    turn_back(g - 1)
                for item in beside[2:]:
                    score(*item)
            turn_back(NGROUP - 1)
            for q, m in last_sums:
                weigh(q, m)

        @block.scalar
        def _(act):
            def hold(n, k):
                _, q, b, _ = units[n]
                no = item_no[n, k]
                act.wait_ge(scored, no + 1)
                if q == 3:
                    act.wait_ge(summed, PAIRS * k + b // 2 + 1)
                act.activation(held[place[q][k]][:, :, NH * b:NH * b + NH],
                               score_buffer(no)[:].rearrange("p (t h) -> p t h", h=NH), ACT.Copy).then_inc(score_held, 1)

            def back(g):
                q = g // PER_Q
                for k in range(chunks[q]):
                    no = back_no[g, k]
                    if no % 2 == 0:
                        act.wait_ge(back_turned, no + 1)
                        r = GROUP * g % QUARTER
                        act.activation(held[place[q][k]][:, r:r + GROUP, :].rearrange("p a b -> p (a b)"),
                                       ps_back[0][:], ACT.Copy).then_inc(back_act, 1)

            def exp(g):
                act.wait_ge(bias_ready, g + 1)
                for i in range(GROUP):
                    n = GROUP * g + i + 1
                    act.activation(z[:, g % ZR, i, 0:n], z[:, g % ZR, i, 0:n], ACT.Exp, bias=bias[:, g % 2, i:i + 1],
                                   scale=10.0).then_inc(exped, 1)

            for n in range(B):
                hold(n, 0)
            act.wait_ge(cleared, 3)
            for g in range(NGROUP):
                if g >= 2:
                    back(g - 2)
                for n in units_at(g):
                    for k in units[n][3]:
                        hold(n, k)
                exp(g)
            back(NGROUP - 2)
            back(NGROUP - 1)

        @block.vector
        def _(dve):
            def scan(r):
                g, i = divmod(r, GROUP)
                nk = chunks[g // PER_Q]
                if i == 0:
                    dve.wait_ge(row_turned, g + 1)
                if r == 0:
                    dve.wait_ge(cleared, 3)
                else:
                    dve.wait_ge(scanned, r)
                if r >= 2:
                    dve.wait_ge(peaked, r - 1)
                at = i * nk * P
                dve.scalar_tensor_tensor(y[:, r % 2, 1:r + 2], y[:, (r + 1) % 2, 0:r + 1], 1.0,
                                         ps_row[g % 2][:, at // 512, at % 512:at % 512 + r + 1],
                                         ALU.add, ALU.mult).then_inc(scanned, 1)

            def add_prior(r):
                g, i = divmod(r, GROUP)
                if i == 0 and g >= ZR:
                    dve.wait_ge(back_turned, back_no[g - ZR, chunks[(g - ZR) // PER_Q] - 1] + 1)
                if i == 0 and g >= 2:
                    dve.wait_ge(exped, GROUP * (g - 1))
                dve.wait_ge(prior_ready, r + 1)
                dve.wait_ge(scanned, r + 1)
                dve.tensor_tensor_reduce(z[:, g % ZR, i, 0:r + 1], y[:, r % 2, 1:r + 2], prior[:, r % 4, 0:r + 1],
                                         1.0, -3.0e38, ALU.add, ALU.max, peak[:, g % 2, i:i + 1]).then_inc(peaked, 1)

            def back(g):
                q = g // PER_Q
                for k in range(chunks[q]):
                    no = back_no[g, k]
                    if no % 2 == 1:
                        dve.wait_ge(back_turned, no + 1)
                        r = GROUP * g % QUARTER
                        dve.tensor_copy(held[place[q][k]][:, r:r + GROUP, :].rearrange("p a b -> p (a b)"),
                                        ps_back[1][:]).then_inc(back_dve, 1)

            def scale(q, m):
                n = PAIRS * q + m
                rows = slice(QUARTER * (q % 2), QUARTER * (q % 2) + QUARTER)
                sums = sum_buffer(q, m)[rows, 0:2 * NH * (HD + 1)].rearrange("p (i h d) -> p i h d", i=2, d=HD + 1)
                dve.wait_ge(summed, n + 1)
                dve.reciprocal(inv[rows, n % 2], sums[:, :, :, HD]).then_inc(inverted, 1)
                dve.wait_ge(inverted, n + 1)
                if n >= 2:
                    dve.wait_ge(added, n - 1)
                dve.tensor_tensor(o[rows, n % 2], sums[:, :, :, 0:HD],
                                  inv[rows, n % 2, :, :, None].to_broadcast([QUARTER, 2, NH, HD]), ALU.mult).then_inc(scaled, 1)

            def count(q, m):
                if q % 2 == 0:
                    return
                dve.wait_ge(added, PAIRS * q + m + 1)
                for b in (2 * m, 2 * m + 1):
                    j = 2 * b + q // 2
                    dve.bn_stats(keep.tbn[:, j, :], keep.t[:, j, :]).then_inc(counted, 1)

            for n in range(B):
                spread(dve, n, qx_dve)
            for n in units_at(0):
                spread(dve, n, qx_dve)
            for g in range(NGROUP):
                for i in range(GROUP):
                    scan(GROUP * g + i)
                    if g or i:
                        add_prior(GROUP * g + i - 1)
                    if i == 0 and g:
                        dve.wait_ge(peaked, GROUP * g)
                        dve.tensor_scalar(bias[:, (g - 1) % 2, :], peak[:, (g - 1) % 2, :], -10.0, None, ALU.mult).then_inc(bias_ready, 1)
                    if i == 2:
                        for q, m in (sums_at(g - 1) if g else []):
                            scale(q, m)
                if g >= 2:
                    back(g - 2)
                for q, m in (sums_at(g - 3) if g >= 3 else []):
                    count(q, m)
                for n in units_at(g + 1):
                    if by_dve(n):
                        spread(dve, n, qx_dve)
            add_prior(T - 1)
            dve.wait_ge(peaked, T)
            dve.tensor_scalar(bias[:, (NGROUP - 1) % 2, :], peak[:, (NGROUP - 1) % 2, :], -10.0, None, ALU.mult).then_inc(bias_ready, 1)
            back(NGROUP - 2)
            back(NGROUP - 1)
            for q, m in last_sums:
                scale(q, m)
                if m:
                    count(q, m - 1)
            count(3, PAIRS - 1)

        @block.sync
        def _(sp):
            for n in range(U):
                _, q, b, _ = units[n]
                if n >= 4:
                    wait_spread(sp, n - 4)
                at = T * b + QUARTER * q
                sp.dma_start(q_in[:, n % 4, :], q_dram[:, at:at + QUARTER]).then_inc(q_loaded[n % 4], 16)

        @block.gpsimd
        def _(pool):
            def position(r):
                if r >= 4:
                    pool.wait_ge(peaked, r - 3)
                pool.tensor_scalar(prior[:, r % 4, 0:r + 1], iota[:, 0:r + 1], 1.0 / (r + 1), None, ALU.mult).then_inc(prior_ready, 1)

            def add(q, m):
                n = PAIRS * q + m
                rows = slice(QUARTER * (q % 2), QUARTER * (q % 2) + QUARTER)
                pool.wait_ge(prior_ready, priors)
                pool.wait_ge(qx_pool, expanded)
                pool.wait_ge(scaled, n + 1)
                j = 4 * m + q // 2
                at = keep.t[rows, j:j + 3:2, :].rearrange("p i (h d) -> p i h d", d=HD)
                pool.tensor_tensor(at, at, o[rows, n % 2], ALU.add).then_inc(added, 1)

            pool.memset(z[:].rearrange("p a b c -> p (a b c)"), 0.0).then_inc(cleared, 1)
            pool.memset(y[:].rearrange("p a b -> p (a b)"), 0.0).then_inc(cleared, 1)
            pool.iota(iota_i, pattern=[[1, T]], base=0, channel_multiplier=0).then_inc(iota_ready, 1)
            pool.wait_ge(iota_ready, 1)
            pool.tensor_copy(iota[:], iota_i).then_inc(iota_ready, 1)
            pool.wait_ge(iota_ready, 2)
            pool.memset(bias[:].rearrange("p a b -> p (a b)"), 0.0).then_inc(cleared, 1)
            for r in range(GROUP):
                position(r)
            for g in range(NGROUP):
                if g + 1 < NGROUP:
                    for i in range(GROUP):
                        position(GROUP * (g + 1) + i)
                for n in units_at(g + 1):
                    if not by_dve(n):
                        spread(pool, n, qx_pool)
                priors = min(GROUP * (g + 2), T)
                expanded = sum(not by_dve(n) and units[n][0] <= g + 1 for n in range(U))
                for q, m in (sums_at(g - 1) if g else []):
                    add(q, m)
                    pool.wait_ge(added, PAIRS * q + m + 1)
            for q, m in last_sums:
                add(q, m)
                pool.wait_ge(added, PAIRS * q + m + 1)


LOT = 4
HID = 512
KC = HID // P
XR = 8


class Moe:

    def __init__(self, s, name, experts, swiglu):
        self.name, self.n, self.swiglu = name, experts, swiglu
        self.tiles = (B * T * TOPK // P + experts) // 2 * 2
        self.up = [s.sb(f"{name}_up{i}", [P, experts, HID]) for i in range(2 if swiglu else 1)]
        self.down = s.sb(f"{name}_down", [P, experts, KC, C])
        if not swiglu:
            self.b1 = s.sb(f"{name}_b1", [P, experts, KC])
            self.b2 = s.sb(f"{name}_b2", [P, experts, C])
        self.slot = s.sb(f"{name}_slot", [P, NT, TOPK], U32)
        self.weight = s.sb(f"{name}_weight", [P, TOPK, NT])
        self.of_tile = s.sb(f"{name}_of_tile", [P, self.tiles], I32)
        self.up_in = [s.sem(f"{name}_up_in{i}") for i in range(2)]
        self.down_in = s.sem(f"{name}_down_in")


def load_experts(sp, m, up, down, b1=None, b2=None):
    half = m.n // 2
    for lot in range(2):
        part = slice(lot * half, (lot + 1) * half)
        for dst, src in zip(m.up, up):
            sp.dma_start(dst[:, part], src[:, part]).then_inc(m.up_in[lot], 16)
        sp.dma_start(m.down[:, part], down[:, part]).then_inc(m.down_in, 16)
    if b1 is not None:
        sp.dma_start(m.b1[:], b1).then_inc(m.down_in, 16)
        sp.dma_start(m.b2[:], b2[None, :, :].to_broadcast([P, m.n, C])).then_inc(m.down_in, 16)


def route(nc, top, m, router, loads, xn, keep):
    E, N = m.n, NT * m.n
    name = m.name
    with ExitStack() as ctx:
        s = Space(nc, ctx, keep.spent)

        def sb(what, shape, dt=F32):
            return s.sb(f"{name}_{what}", shape, dt)

        def sem(what):
            return s.sem(f"{name}_{what}")

        w = sb("router", [P, E])
        xt = sb("xt", [P, 2, LOT, P])
        lg = sb("lg", [P, NT, E])
        low = sb("low", [P, NT, E])
        pick = [sb(f"pick{k}", [P, NT, E]) for k in range(TOPK)]
        both = sb("both", [P, NT, E])
        tmp = sb("tmp", [P, NT, E])
        run = [sb(f"run{i}", [P, E, NT]) for i in range(2)]
        own = sb("own", [P, E, NT])
        at = sb("at", [P, NT])
        inv = sb("inv", [P, NT])
        idx = sb("idx", [P, NT])
        slot_f = sb("slot_f", [P, NT, TOPK])
        order_i = sb("order_i", [P, E], I32)
        order = sb("order", [P, E])
        number_i = sb("number_i", [P, m.tiles], I32)
        number = sb("number", [P, m.tiles])
        before = sb("before", [P, P])
        count = sb("count", [P, E])
        whole_i = sb("whole_i", [P, E], I32)
        whole = sb("whole", [P, E])
        end = [sb(f"end{i}", [P, E]) for i in range(2)]
        first = sb("first", [P, E])
        passed = sb("passed", [P, m.tiles, E])
        of_f = sb("of_f", [P, m.tiles])
        norm_of = TokenNorm(s, keep, name + "_norm")
        ps_x = [s.ps(f"{name}_ps_x{i}", [P, 512]) for i in range(2)]
        ps_l = [s.ps(f"{name}_ps_l{i}", [P, 512]) for i in range(2)]
        ps_in = s.ps(f"{name}_ps_in", [P, 512])
        ps_all = s.ps(f"{name}_ps_all", [P, 512])
        w_in, const, numbered, copied = sem("w_in"), sem("const"), sem("numbered"), sem("copied")
        normed, turned, xt_ready, logits, lg_ready = (sem(x) for x in ("normed", "turned", "xt_ready", "logits", "lg_ready"))
        step, exped, ranked = sem("step"), sem("exped"), sem("ranked")
        block = ctx.enter_context(nc.Block())

        @block.sync
        def _(sp):
            sp.dma_start(w[:], router).then_inc(w_in, 16)
            loads(sp)

        @block.gpsimd
        def _(pool):
            for k in range(TOPK):
                pool.iota(xn[k][:, :, C].bitcast(I32), pattern=[[P, NT]], base=k * B * T, channel_multiplier=1).then_inc(numbered, 1)
            pool.memset(before[:], 1.0).then_inc(const, 1)
            pool.iota(order_i[:], pattern=[[1, E]], base=-64, channel_multiplier=0).then_inc(const, 1)
            pool.iota(number_i[:], pattern=[[1, m.tiles]], base=0, channel_multiplier=0).then_inc(const, 1)
            pool.wait_ge(const, 3)
            pool.affine_select(out=before[:], in_=before[:], compare_op=ALU.is_gt, fill=0.0, base=0,
                               pattern=[[1, P]], channel_multiplier=-1).then_inc(const, 1)
            pool.tensor_copy(order[:], order_i[:]).then_inc(const, 1)
            pool.tensor_copy(number[:], number_i[:]).then_inc(const, 1)

            def copy(n, u, early):
                pool.wait_ge(normed, LOT * (n + 1))
                pool.tensor_copy(xn[1][:, bass.ds(LOT * n, LOT), 0:C], xn[0][:, bass.ds(LOT * n, LOT), 0:C]).then_inc(copied, 1)

            in_turn(pool, NT // LOT, 2, copy)

        @block.scalar
        def _(act):
            def norm(j, u, early):
                act.activation(xn[0][:, j, 0:C], keep.t[:, j, :], ACT.Identity, bias=keep.tshift[:, bass.ds(j, 1)],
                               scale=keep.tscale[:, bass.ds(j, 1)]).then_inc(normed, 1)

            norm_of.root(act)
            act.wait_ge(norm_of.ready, 1)
            in_turn(act, NT, 2, norm)
            act.wait_ge(step, 2)
            act.activation(lg[:], lg[:], ACT.Exp).then_inc(exped, 1)

        @block.tensor
        def _(pe):
            def turn(n):
                pe.wait_ge(normed, LOT * (n + 1))
                if n >= 2:
                    pe.wait_ge(xt_ready, n - 1)
                for i in range(LOT):
                    last = pe.transpose(ps_x[n % 2][:, i * P:(i + 1) * P], xn[0][:, LOT * n + i, 0:C], keep.ident[:])
                last.then_inc(turned, 1)

            def project(n):
                pe.wait_ge(xt_ready, n + 1)
                if n >= 2:
                    pe.wait_ge(lg_ready, n - 1)
                for i in range(LOT):
                    last = pe.matmul(ps_l[n % 2][:, i * E:(i + 1) * E], xt[:, n % 2, i, :], w[:], start=True, stop=True)
                last.then_inc(logits, 1)

            pe.wait_ge(w_in, 16)
            for n in range(NT // LOT):
                turn(n)
                if n:
                    project(n - 1)
            project(NT // LOT - 1)
            pe.wait_ge(ranked, 1)
            pe.wait_ge(const, 6)
            pe.matmul(ps_in[:, 0:N], before[:], both[:].rearrange("p a b -> p (a b)"), start=True, stop=True).then_inc(ranked, 1)
            pe.matmul(ps_all[:, 0:N], keep.ones[:], both[:].rearrange("p a b -> p (a b)"), start=True, stop=True).then_inc(ranked, 1)

        @block.vector
        def _(dve):
            def x_out(n, u, early):
                dve.wait_ge(turned, n + 1)
                if not early:
                    dve.wait_ge(logits, n - 1)
                dve.tensor_copy(xt[:, u].rearrange("p a b -> p (a b)"), ps_x[u][:]).then_inc(xt_ready, 1)

            def logits_out(n, u, early):
                dve.wait_ge(logits, n + 1)
                dve.tensor_copy(lg[:, bass.ds(LOT * n, LOT), :],
                                ps_l[u][:, 0:LOT * E].rearrange("p (a b) -> p a b", b=E)).then_inc(lg_ready, 1)

            norm_of.collect(dve)
            norm_of.finish(dve)
            lagged(dve, NT // LOT, 2, [(0, x_out), (1, logits_out)])
            dve.wait_ge(lg_ready, NT // LOT)
            dve.wait_ge(const, 6)
            done = [0]

            def then(ins):
                ins.then_inc(step, 1)
                done[0] += 1
                dve.wait_ge(step, done[0])

            def over(v):
                return v[:, :, None].to_broadcast([P, NT, E])

            orders = order[:, None, :].to_broadcast([P, NT, E])
            then(dve.tensor_reduce(at[:], lg[:], AX.X, ALU.max))
            then(dve.tensor_tensor(lg[:], lg[:], over(at), ALU.subtract))
            dve.wait_ge(exped, 1)
            then(dve.tensor_reduce(at[:], lg[:], AX.X, ALU.add))
            then(dve.reciprocal(inv[:], at[:]))
            then(dve.tensor_tensor(lg[:], lg[:], over(inv), ALU.mult))
            for k in range(TOPK):
                then(dve.tensor_reduce(m.weight[:, k, :], lg[:], AX.X, ALU.max))
                then(dve.tensor_tensor(tmp[:], lg[:], over(m.weight[:, k, :]), ALU.is_equal))
                then(dve.tensor_tensor(low[:], tmp[:], orders, ALU.mult))
                then(dve.tensor_reduce(idx[:], low[:], AX.X, ALU.min))
                then(dve.tensor_tensor(pick[k][:], orders, over(idx), ALU.is_equal))
                if k == 0:
                    then(dve.scalar_tensor_tensor(lg[:], pick[0][:], -4.0, lg[:], ALU.mult, ALU.add))
            dve.tensor_tensor(both[:], pick[0][:], pick[1][:], ALU.add).then_inc(ranked, 1)
            if not m.swiglu:
                then(dve.tensor_tensor(at[:], m.weight[:, 0, :], m.weight[:, 1, :], ALU.add))
                then(dve.reciprocal(inv[:], at[:]))
                then(dve.tensor_tensor(m.weight[:], m.weight[:], inv[:, None, :].to_broadcast([P, TOPK, NT]), ALU.mult))
            dve.wait_ge(ranked, 3)
            then(dve.tensor_copy(own[:], ps_all[:, 0:N].rearrange("p (j e) -> p e j", e=E)))
            src, n, d = own, 0, 1
            while d < NT:
                dst = run[n % 2]
                then(dve.tensor_copy(dst[:, :, 0:d], src[:, :, 0:d]))
                then(dve.tensor_tensor(dst[:, :, d:], src[:, :, d:], src[:, :, 0:NT - d], ALU.add))
                src, n, d = dst, n + 1, 2 * d
            then(dve.tensor_scalar(count[:], src[:, :, NT - 1], float(P - 1), None, ALU.add))
            then(dve.tensor_copy(whole_i[:], count[:]))
            then(dve.tensor_scalar(whole_i[:], whole_i[:], 7, None, ALU.arith_shift_right))
            then(dve.tensor_copy(whole[:], whole_i[:]))
            ends, n, d = whole, 0, 1
            while d < E:
                dst = end[n % 2]
                then(dve.tensor_copy(dst[:, 0:d], ends[:, 0:d]))
                then(dve.tensor_tensor(dst[:, d:], ends[:, d:], ends[:, 0:E - d], ALU.add))
                ends, n, d = dst, n + 1, 2 * d
            then(dve.tensor_tensor(first[:], ends[:], whole[:], ALU.subtract))
            then(dve.tensor_tensor(own[:], src[:], own[:], ALU.subtract))
            then(dve.scalar_tensor_tensor(own[:], first[:, :, None].to_broadcast([P, E, NT]), float(P), own[:], ALU.mult, ALU.add))
            then(dve.tensor_tensor(both[:], ps_in[:, 0:N].rearrange("p (j e) -> p j e", e=E),
                                   own[:].rearrange("p e j -> p j e"), ALU.add))
            for k in range(TOPK):
                then(dve.tensor_tensor(tmp[:], both[:], pick[k][:], ALU.mult))
                then(dve.tensor_reduce(slot_f[:, :, k], tmp[:], AX.X, ALU.add))
            then(dve.tensor_copy(m.slot[:], slot_f[:]))
            then(dve.tensor_tensor(passed[:], number[:, :, None].to_broadcast([P, m.tiles, E]),
                                   ends[:, None, :].to_broadcast([P, m.tiles, E]), ALU.is_ge))
            then(dve.tensor_reduce(of_f[:], passed[:], AX.X, ALU.add))
            then(dve.tensor_scalar(of_f[:], of_f[:], float(E - 1), None, ALU.min))
            then(dve.tensor_copy(m.of_tile[:], of_f[:]))


def dispatch(nc, top, m, xs_dram, xn, shared, keep):
    with ExitStack() as ctx:
        s = Space(nc, ctx, keep.spent)
        sent = [s.sem(f"{m.name}_sent{i}") for i in range(4)]
        if shared is not None:
            up, down = shared
            H = up.shape[1] // 2
            HC = H // P
            ws = s.sb("sh_up", [P, 2 * H])
            wd = s.sb("sh_down", [P, HC, C])
            xs = s.sb("sh_xs", [P, 2, C])
            xt = s.sb("sh_xt", [P, 2, P])
            act_g = s.sb("sh_act", [P, 2, H])
            hid = s.sb("sh_hid", [P, 2, H])
            ht = s.sb("sh_ht", [P, 2, HC, P])
            ps_x = [s.ps(f"sh_ps_x{i}", [P, 512]) for i in range(2)]
            ps_u = [s.ps(f"sh_ps_u{i}", [P, 512]) for i in range(2)]
            ps_h = [s.ps(f"sh_ps_h{i}", [P, 512]) for i in range(2)]
            ps_y = [s.ps(f"sh_ps_y{i}", [P, 512]) for i in range(2)]
            w_in, staged, turned, xt_ready, upped, silued, multiplied, h_turned, ht_ready, downed, added = (
                s.sem("sh_" + x) for x in ("w_in", "staged", "turned", "xt_ready", "upped", "silued", "multiplied",
                                           "h_turned", "ht_ready", "downed", "added"))
        block = ctx.enter_context(nc.Block())

        @block.gpsimd
        def _(pool):
            for j in range(NT):
                for k in range(TOPK):
                    n = TOPK * j + k
                    pool.indirect_dma_start(xs_dram, bass.IndirectOffsetOnAxis(m.slot[:, j, k:k + 1], 0),
                                            xn[k][:, j, :], None).then_inc(sent[n % 4], 16)
            for i in range(4):
                pool.wait_ge(sent[i], 16 * NT * TOPK // 4)

        if shared is None:
            return

        @block.sync
        def _(sp):
            sp.dma_start(ws[:], up).then_inc(w_in, 16)
            sp.dma_start(wd[:], down).then_inc(w_in, 16)

        @block.scalar
        def _(act):
            def stage(j, u, early):
                if not early:
                    act.wait_ge(turned, j - 1)
                act.activation(xs[:, u, :], xn[0][:, j, 0:C], ACT.Copy).then_inc(staged, 1)

            def silu(j, u, early):
                act.wait_ge(upped, j + 1)
                if not early:
                    act.wait_ge(multiplied, j - 1)
                act.activation(act_g[:, u, :], ps_u[u][:, 0:H], ACT.Silu).then_inc(silued, 1)

            def h_out(j, u, early):
                act.wait_ge(h_turned, j + 1)
                if not early:
                    act.wait_ge(downed, j - 1)
                act.activation(ht[:, u], ps_h[u][:, 0:H].rearrange("p (a b) -> p a b", b=P), ACT.Copy).then_inc(ht_ready, 1)

            lagged(act, NT, 2, [(0, stage), (4, silu), (6, h_out)])

        @block.vector
        def _(dve):
            def x_out(j, u, early):
                dve.wait_ge(turned, j + 1)
                if not early:
                    dve.wait_ge(upped, j - 1)
                dve.tensor_copy(xt[:, u, :], ps_x[u][:, 0:P]).then_inc(xt_ready, 1)

            def multiply(j, u, early):
                dve.wait_ge(silued, j + 1)
                if not early:
                    dve.wait_ge(h_turned, j - 1)
                dve.tensor_tensor(hid[:, u, :], act_g[:, u, :], ps_u[u][:, H:2 * H], ALU.mult).then_inc(multiplied, 1)

            def add(j, u, early):
                dve.wait_ge(downed, j + 1)
                dve.tensor_tensor(keep.t[:, j, :], keep.t[:, j, :], ps_y[u][:, 0:C], ALU.add).then_inc(added, 1)

            lagged(dve, NT, 2, [(2, x_out), (4, multiply), (8, add)])

        @block.tensor
        def _(pe):
            def turn(j, u, early):
                pe.wait_ge(staged, j + 1)
                if not early:
                    pe.wait_ge(xt_ready, j - 1)
                pe.transpose(ps_x[u][:, 0:P], xs[:, u, :], keep.ident[:]).then_inc(turned, 1)

            def up_(j, u, early):
                pe.wait_ge(xt_ready, j + 1)
                if not early:
                    pe.wait_ge(multiplied, j - 1)
                pe.matmul(ps_u[u][:, 0:2 * H], xt[:, u, :], ws[:], start=True, stop=True).then_inc(upped, 1)

            def turn_h(j, u, early):
                pe.wait_ge(multiplied, j + 1)
                if not early:
                    pe.wait_ge(ht_ready, j - 1)
                for k in range(HC):
                    last = pe.transpose(ps_h[u][:, k * P:(k + 1) * P], hid[:, u, k * P:(k + 1) * P], keep.ident[:])
                last.then_inc(h_turned, 1)

            def down_(j, u, early):
                pe.wait_ge(ht_ready, j + 1)
                if not early:
                    pe.wait_ge(added, j - 1)
                for k in range(HC):
                    last = pe.matmul(ps_y[u][:, 0:C], ht[:, u, k, :], wd[:, k, :], start=(k == 0), stop=(k == HC - 1))
                last.then_inc(downed, 1)

            pe.wait_ge(w_in, 32)
            lagged(pe, NT, 2, [(1, turn), (3, up_), (5, turn_h), (7, down_)])


def again(j, depth):
    return not isinstance(j, int) or j >= depth


def experts(nc, top, m, xs_dram, ys_dram, keep):
    name, M = m.name, m.tiles
    with ExitStack() as ctx:
        s = Space(nc, ctx, keep.spent)
        xin = s.sb(f"{name}_xin", [P, XR, ROW])
        xt = s.sb(f"{name}_ext", [P, 2, P])
        w_up = [s.sb(f"{name}_w_up{i}", [P, 2, HID]) for i in range(len(m.up))]
        w_down = s.sb(f"{name}_w_down", [P, 4, KC, C])
        if not m.swiglu:
            b_up = s.sb(f"{name}_b_up", [P, XR, KC])
            b_down = s.sb(f"{name}_b_down", [P, XR, C])
        act_g = s.sb(f"{name}_act", [P, 2, HID])
        ht = s.sb(f"{name}_ht", [P, 2, KC, P])
        yout = s.sb(f"{name}_yout", [P, XR, C])
        ps_x = [s.ps(f"{name}_eps_x{i}", [P, 512]) for i in range(2)]
        ps_y = [s.ps(f"{name}_eps_y{i}", [P, 512]) for i in range(2)]
        ps_up = [[s.ps(f"{name}_eps_up{k}_{i}", [P, 512]) for i in range(2)] for k in range(len(m.up))]
        loaded = [s.sem(f"{name}_loaded{i}") for i in range(XR)]
        stored = [s.sem(f"{name}_stored{i}") for i in range(XR)]
        placed = [s.sem(f"{name}_placed{i}") for i in range(len(m.up))]
        down_placed = s.sem(f"{name}_down_placed")
        bias_placed = s.sem(f"{name}_bias_placed")
        turned, xt_ready, upped, silued, ht_ready, downed, y_ready = (
            s.sem(f"{name}_e_" + x) for x in ("turned", "xt_ready", "upped", "silued", "ht_ready", "downed", "y_ready"))
        block = ctx.enter_context(nc.Block())
        ht_steps = 1 if m.swiglu else KC

        def expert(eng, j):
            return eng.value_load(m.of_tile[0:1, bass.ds(j, 1)], min_val=0, max_val=m.n - 1)

        def weights_in(eng):
            for lot in range(2):
                eng.wait_ge(m.up_in[lot], 16 * len(m.up))
            eng.wait_ge(m.down_in, 16 * (2 if m.swiglu else 4))

        @block.sync
        def _(sp):
            def load(j, u, early):
                if not early:
                    sp.wait_ge(stored[u], 16 // XR * (j - u))
                sp.dma_start(xin[:, u, :], xs_dram[bass.ds(j * P, P), :]).then_inc(loaded[u], 16)

            in_turn(sp, M, XR, load)

        @block.gpsimd
        def _(pool):
            def store(j, u, early):
                pool.wait_ge(y_ready, j + 1)
                pool.sem_inc(keep.waited)
                pool.indirect_dma_start(ys_dram, bass.IndirectOffsetOnAxis(xin[:, u, C:C + 1].bitcast(U32), 0),
                                        yout[:, u, :], None).then_inc(stored[u], 16)

            def place(j, u, early):
                e = expert(pool, j)
                if again(j, XR):
                    pool.wait_ge(y_ready, j - XR + 1)
                pool.tensor_copy(b_up[:, u, :], m.b1[:, e, :]).then_inc(bias_placed, 1)
                pool.tensor_copy(b_down[:, u, :], m.b2[:, e, :]).then_inc(bias_placed, 1)

            if m.swiglu:
                in_turn(pool, M, XR, store)
            else:
                weights_in(pool)
                lagged(pool, M, XR, [(0, place), (6, store)])
            for u in range(XR):
                pool.wait_ge(stored[u], 16 * M // XR)

        @block.tensor
        def _(pe):
            def turn(j, u, early):
                pe.wait_ge(loaded[u], 16 // XR * (j - u) + 16)
                if again(j, 2):
                    pe.wait_ge(xt_ready, j - 1)
                pe.transpose(ps_x[u % 2][:, 0:P], xin[:, u, 0:C], keep.ident[:]).then_inc(turned, 1)

            def up(j, u, early):
                pe.wait_ge(xt_ready, j + 1)
                for sem in placed:
                    pe.wait_ge(sem, j + 1)
                if again(j, 2):
                    pe.wait_ge(ht_ready, ht_steps * (j - 1))
                for ps, w in zip(ps_up, w_up):
                    for k in range(KC):
                        last = pe.matmul(ps[u % 2][:, k * P:(k + 1) * P], w[:, u % 2, k * P:(k + 1) * P], xt[:, u % 2, :],
                                         start=True, stop=True)
                last.then_inc(upped, 1)

            def down(j, u, early):
                pe.wait_ge(ht_ready, ht_steps * (j + 1))
                pe.wait_ge(down_placed, j + 1)
                if again(j, 2):
                    pe.wait_ge(y_ready, j - 1)
                for k in range(KC):
                    last = pe.matmul(ps_y[u % 2][:, 0:C], ht[:, u % 2, k, :], w_down[:, u % 4, k, :], start=(k == 0), stop=(k == KC - 1))
                last.then_inc(downed, 1)

            lagged(pe, M, XR, [(0, turn), (2, up), (4, down)])

        @block.scalar
        def _(act):
            def place(j, u, early):
                e = expert(act, j)
                if again(j, 2):
                    act.wait_ge(upped, j - 1)
                act.activation(w_up[0][:, u % 2, :], m.up[0][:, e, :], ACT.Copy).then_inc(placed[0], 1)
                if again(j, 4):
                    act.wait_ge(downed, j - 3)
                act.activation(w_down[:, u % 4], m.down[:, e], ACT.Copy).then_inc(down_placed, 1)

            def silu(j, u, early):
                act.wait_ge(upped, j + 1)
                if again(j, 2):
                    act.wait_ge(ht_ready, j - 1)
                act.activation(act_g[:, u % 2, :], ps_up[0][u % 2][:], ACT.Silu).then_inc(silued, 1)

            weights_in(act)
            lagged(act, M, XR, ([(3, silu)] if m.swiglu else []) + [(1, place)])

        @block.vector
        def _(dve):
            def x_out(j, u, early):
                dve.wait_ge(turned, j + 1)
                if again(j, 2):
                    dve.wait_ge(upped, j - 1)
                dve.tensor_copy(xt[:, u % 2, :], ps_x[u % 2][:, 0:P]).then_inc(xt_ready, 1)

            def place(j, u, early):
                e = expert(dve, j)
                if again(j, 2):
                    dve.wait_ge(upped, j - 1)
                dve.tensor_copy(w_up[1][:, u % 2, :], m.up[1][:, e, :]).then_inc(placed[1], 1)

            def hidden(j, u, early):
                dve.wait_ge(silued if m.swiglu else upped, j + 1)
                if not m.swiglu:
                    dve.wait_ge(bias_placed, 2 * j + 2)
                if again(j, 2):
                    dve.wait_ge(downed, j - 1)
                if m.swiglu:
                    dve.tensor_tensor(ht[:, u % 2].rearrange("p a b -> p (a b)"), act_g[:, u % 2, :], ps_up[1][u % 2][:],
                                      ALU.mult).then_inc(ht_ready, 1)
                else:
                    for k in range(KC):
                        dve.tensor_scalar(ht[:, u % 2, k, :], ps_up[0][u % 2][:, k * P:(k + 1) * P],
                                          b_up[:, u, k:k + 1], 0.0, ALU.add, ALU.max).then_inc(ht_ready, 1)

            def y_out(j, u, early):
                dve.wait_ge(downed, j + 1)
                if again(j, XR):
                    dve.wait_ge(stored[u], 16 // XR * (j - u))
                if m.swiglu:
                    dve.tensor_copy(yout[:, u, :], ps_y[u % 2][:, 0:C]).then_inc(y_ready, 1)
                else:
                    dve.tensor_tensor(yout[:, u, :], ps_y[u % 2][:, 0:C], b_down[:, u, :], ALU.add).then_inc(y_ready, 1)

            if m.swiglu:
                weights_in(dve)
            lagged(dve, M, XR, [(5, y_out), (1, x_out)] + ([(1, place)] if m.swiglu else []) + [(3, hidden)])


def fetch(sp, ys_dram, y, n, done):
    rows = ys_dram[0:TOPK * B * T, :].rearrange("(k n i p) c -> n k p i c", k=TOPK, i=LOT, p=P)
    for k in range(TOPK):
        sp.dma_start(y[:, :, k, :], rows[n, k]).then_inc(done[k], 16)


def combine(nc, top, m, ys_dram, keep, tiles=NT, out=None):
    name = m.name
    with ExitStack() as ctx:
        s = Space(nc, ctx, keep.spent)
        y = s.sb(f"{name}_y", [P, 4, LOT, TOPK, C])
        fetched = [[s.sem(f"{name}_fetched{u}_{k}") for k in range(TOPK)] for u in range(4)]
        added = s.sem(f"{name}_added")
        counted = s.sem(f"{name}_counted")
        if out is not None:
            image = s.sb("out_image", [P, 4, T])
            ps_t = [s.ps(f"out_ps{i}", [P, 512]) for i in range(4)]
            turned = s.sem("out_turned")
            copied = s.sem("out_copied")
            stored = [s.sem(f"out_stored{i}") for i in range(4)]
        block = ctx.enter_context(nc.Block())

        @block.sync
        def _(sp):
            for n in range(tiles // LOT):
                if n >= 4:
                    sp.wait_ge(added, TOPK * LOT * (n - 3))
                fetch(sp, ys_dram, y[:, n % 4], n, fetched[n % 4])
            if out is None:
                return

            def store(b, u, early):
                sp.wait_ge(copied, b + 1)
                sp.dma_start(out[b].rearrange("c h w -> c (h w)"), image[:, u, :]).then_inc(stored[u], 16)

            in_turn(sp, B, 4, store)
            for u in range(4):
                sp.wait_ge(stored[u], 16 * B // 4)

        @block.vector
        def _(dve):
            for n in range(tiles // LOT):
                for k in range(TOPK):
                    dve.wait_ge(fetched[n % 4][k], 16 * (n // 4 + 1))
                    for i in range(LOT):
                        j = LOT * n + i
                        if k:
                            dve.wait_ge(added, TOPK * LOT * n + i + 1)
                        dve.scalar_tensor_tensor(keep.t[:, j, :], y[:, n % 4, i, k, :], m.weight[:, k, j:j + 1],
                                                 keep.t[:, j, :], ALU.mult, ALU.add).then_inc(added, 1)
                if out is None:
                    for i in range(LOT):
                        j = LOT * n + i
                        dve.wait_ge(added, TOPK * LOT * n + LOT + i + 1)
                        dve.bn_stats(keep.tbn[:, j, :], keep.t[:, j, :]).then_inc(counted, 1)

        if out is None:
            return

        @block.tensor
        def _(pe):
            for b in range(B):
                pe.wait_ge(added, TOPK * LOT * (b // 2 + 1))
                if b >= 4:
                    pe.wait_ge(copied, b - 3)
                for h in range(2):
                    last = pe.transpose(ps_t[b % 4][:, h * P:(h + 1) * P], keep.t[:, 2 * b + h, :], keep.ident[:])
                last.then_inc(turned, 1)

        @block.scalar
        def _(act):
            def copy(b, u, early):
                act.wait_ge(turned, b + 1)
                if not early:
                    act.wait_ge(stored[u], 4 * (b - u))
                act.activation(image[:, u, :], ps_t[u][:, 0:T], ACT.Copy).then_inc(copied, 1)

            in_turn(act, B, 4, copy)


UN = 6


def timetable(eng, parts):
    most = max(lag + (UN - 1 if each else 0) for lag, each, _ in parts)
    span = 2 * UN
    first = -(-(most + span) // span) * span

    def step(base, u, static):
        for lag, each, body in parts:
            ahead, i = divmod(u - lag, UN)
            if not each and i:
                continue
            if static:
                if 0 <= ahead < B:
                    body(ahead, i, ahead % 2, ahead < 2)
            else:
                body(base + ahead, i, ahead % 2, False)

    for n in range(first):
        step(0, n, True)
    with eng.Fori(first // span, B // 2) as k:
        for u in range(span):
            step(2 * k, u, False)
    for n in range(B * UN, B * UN + most + 1):
        step(0, n, True)


EARLY = 12
LATE = NT - EARLY


def causal_attention(nc, top, wqk, wv, wout, m, ys_dram, keep):
    with ExitStack() as ctx:
        s = Space(nc, ctx, keep.spent)
        wqk_s = s.sb("c_wqk", [P, 2 * C])
        wv_s = s.sb("c_wv", [P, C])
        wout_s = s.sb("c_wout", [P, C])
        ident_b = s.sb("c_ident_b", [P, P], BF16)
        mask = s.sb("c_mask", [P, 2, 512], BF16)
        xn = s.sb("c_xn", [P, 2, 2, C])
        xt = s.sb("c_xt", [P, 2, T])
        q = s.sb("c_q", [P, 2, T])
        k_ = s.sb("c_k", [P, 2, T])
        kx = s.sb("c_kx", [P, 2, NH, T])
        vx = s.sb("c_vx", [P, 2, 2, NH, HD + 1])
        peak = s.sb("c_peak", [P, 2, 4])
        e = s.sb("c_e", [P, 3, 512])
        pt = s.sb("c_pt", [P, 2, 512])
        inv = s.sb("c_inv", [P, 2, 2 * NH])
        on = s.sb("c_on", [P, 2, 2 * NH, HD])
        ot = s.sb("c_ot", [P, 2, 2, P])
        ps_x = s.ps("c_ps_x", [P, 512])
        ps_qk = s.ps("c_ps_qk", [P, 512])
        ps_v = s.ps("c_ps_v", [P, 512])
        ps_o = s.ps("c_ps_o", [P, 512])
        ps_s = [s.ps(f"c_ps_s{i}", [P, 512]) for i in range(2)]
        ps_t = [s.ps(f"c_ps_t{i}", [P, 512]) for i in range(2)]
        (w_in, const, normed, turned, xt_ready, qk_done, v_done, qk_out, v_out, kx_ready, scored, peaked, centred,
         exped, e_turned, back_act, back_dve, weighed, inverted, o_ready, o_turned, ot_ready, y_done, added) = (
            s.sem("c_" + x) for x in ("w_in", "const", "normed", "turned", "xt_ready", "qk_done", "v_done", "qk_out",
                                      "v_out", "kx_ready", "scored", "peaked", "centred", "exped", "e_turned",
                                      "back_act", "back_dve", "weighed", "inverted", "o_ready", "o_turned",
                                      "ot_ready", "y_done", "added"))
        counted = s.sem("c_counted")
        rows = s.sb("c_rows", [P, 2, LOT, TOPK, C])
        fetched = [[s.sem(f"c_fetched{u}_{k}") for k in range(TOPK)] for u in range(2)]
        taken = s.sem("c_taken")
        late_counted = s.sem("c_late_counted")
        early_norm = TokenNorm(s, keep, "norm3", 0, EARLY)
        late_norm = TokenNorm(s, keep, "norm3_late", EARLY, NT)
        block = ctx.enter_context(nc.Block())

        def unit(i):
            return (0, 4 * i, 4, P) if i < 2 else (1, 2 * (i - 2), 2, T)

        def least(b, n):
            return min(b + n, B) if isinstance(b, int) else b + n

        @block.sync
        def _(sp):
            for dst, src in ((wqk_s, wqk), (wv_s, wv), (wout_s, wout)):
                sp.dma_start(dst[:], src).then_inc(w_in, 16)
            for n in range(LATE // LOT):
                if n >= 2:
                    sp.wait_ge(taken, TOPK * LOT * (n - 1))
                fetch(sp, ys_dram, rows[:, n % 2], EARLY // LOT + n, fetched[n % 2])

        @block.gpsimd
        def _(pool):
            pool.tensor_copy(ident_b[:], keep.ident[:]).then_inc(const, 1)
            pool.memset(mask[:].rearrange("p a b -> p (a b)"), 0.0).then_inc(const, 1)
            pool.memset(vx[:].rearrange("p a b c d -> p (a b c d)"), 1.0).then_inc(const, 1)
            pool.wait_ge(const, 3)
            pool.affine_select(out=mask[:, 0, :].rearrange("p (a b) -> p a b", b=P), in_=mask[:, 0, :].rearrange("p (a b) -> p a b", b=P),
                               compare_op=ALU.is_ge, fill=-1e30, base=0, pattern=[[0, 4], [-1, P]],
                               channel_multiplier=1).then_inc(const, 1)
            pool.affine_select(out=mask[:, 1, :].rearrange("p (a b) -> p a b", b=T), in_=mask[:, 1, :].rearrange("p (a b) -> p a b", b=T),
                               compare_op=ALU.is_ge, fill=-1e30, base=P, pattern=[[0, 2], [-1, T]],
                               channel_multiplier=1).then_inc(const, 1)

            def spread(b, i, u, early):
                pool.wait_ge(qk_out, 2 * b + 2)
                if not early:
                    pool.wait_ge(scored, UN * (b - 1))
                pool.tensor_tensor(kx[:, u], k_[:, u, None, :].to_broadcast([P, NH, T]),
                                   keep.head8[:, :, None].to_broadcast([P, NH, T]), ALU.mult).then_inc(kx_ready, 1)

            timetable(pool, [(4, False, spread)])

        @block.scalar
        def _(act):
            def norm(b, i, u, early):
                if not early:
                    act.wait_ge(turned, b - 1)
                if isinstance(b, int) and b == EARLY // 2 - 1:
                    act.wait_ge(late_norm.ready, 1)
                for h in range(2):
                    j = 2 * b + h
                    act.activation(xn[:, u, h, :], keep.t[:, j, :], ACT.Identity, bias=keep.tshift[:, bass.ds(j, 1)],
                                   scale=keep.tscale[:, bass.ds(j, 1)]).then_inc(normed, 1)

            def qk(b, i, u, early):
                act.wait_ge(qk_done, b + 1)
                if not early:
                    act.wait_ge(scored, UN * (b - 1))
                    act.wait_ge(kx_ready, b - 1)
                act.activation(q[:, u, :], ps_qk[:, 0:T], ACT.Copy).then_inc(qk_out, 1)
                act.activation(k_[:, u, :], ps_qk[:, T:2 * T], ACT.Copy).then_inc(qk_out, 1)

            def exp(b, i, u, early):
                act.wait_ge(centred, UN * b + i + 1)
                act.activation(e[:, i % 3, :], e[:, i % 3, :], ACT.Exp, scale=float(HD) ** -0.5).then_inc(exped, 1)

            def back(b, i, u, early):
                if i % 2 == 0:
                    act.wait_ge(e_turned, UN * b + i + 1)
                    if not early:
                        act.wait_ge(weighed, UN * b + i - 1)
                    elif UN * b + i >= 2:
                        act.wait_ge(weighed, UN * b + i - 1)
                    act.activation(pt[:, 0, :], ps_t[0][:], ACT.Copy).then_inc(back_act, 1)

            def ot_out(b, i, u, early):
                act.wait_ge(o_turned, b + 1)
                if not early:
                    act.wait_ge(y_done, b - 1)
                act.activation(ot[:, u].rearrange("p a b -> p (a b)"), ps_x[:, 0:T], ACT.Copy).then_inc(ot_ready, 1)

            def root_late(b, i, u, early):
                if isinstance(b, int) and UN * b + i == LATE:
                    late_norm.root(act)

            early_norm.root(act)
            act.wait_ge(early_norm.ready, 1)
            timetable(act, [(3, True, root_late), (0, False, norm), (4, False, qk), (10, True, back), (7, True, exp), (18, False, ot_out)])

        @block.vector
        def _(dve):
            def x_out(b, i, u, early):
                dve.wait_ge(turned, b + 1)
                if not early:
                    dve.wait_ge(v_done, b - 1)
                dve.tensor_copy(xt[:, u, :], ps_x[:, 0:T]).then_inc(xt_ready, 1)

            def v(b, i, u, early):
                dve.wait_ge(v_done, b + 1)
                if not early:
                    dve.wait_ge(weighed, UN * (b - 1))
                dve.tensor_copy(vx[:, u].rearrange("p a b c -> p (a b) c")[:, :, 0:HD],
                                ps_v[:, 0:2 * C].rearrange("p (a d) -> p a d", d=HD)).then_inc(v_out, 1)

            def centre(b, i, u, early):
                _, _, heads, keys = unit(i)
                n = UN * b + i
                sc = ps_s[i % 2][:].rearrange("p (h s) -> p h s", s=keys)
                dve.wait_ge(scored, n + 1)
                dve.tensor_reduce(peak[:, i % 2, 0:heads], sc, AX.X, ALU.max).then_inc(peaked, 1)
                dve.wait_ge(peaked, n + 1)
                if not early or UN * b + i >= 3:
                    dve.wait_ge(e_turned, n - 2)
                dve.tensor_tensor(e[:, i % 3, :].rearrange("p (h s) -> p h s", s=keys), sc,
                                  peak[:, i % 2, 0:heads, None].to_broadcast([P, heads, keys]), ALU.subtract).then_inc(centred, 1)

            def back(b, i, u, early):
                if i % 2 == 1:
                    dve.wait_ge(e_turned, UN * b + i + 1)
                    if not early or UN * b + i >= 2:
                        dve.wait_ge(weighed, UN * b + i - 1)
                    dve.tensor_copy(pt[:, 1, :], ps_t[1][:]).then_inc(back_dve, 1)

            def o_norm(b, i, u, early):
                sums = ps_o[:, 0:2 * NH * (HD + 1)].rearrange("p (g d) -> p g d", d=HD + 1)
                dve.wait_ge(weighed, UN * b + UN)
                dve.reciprocal(inv[:, u, :], sums[:, :, HD]).then_inc(inverted, 1)
                dve.wait_ge(inverted, b + 1)
                if not early:
                    dve.wait_ge(o_turned, b - 1)
                dve.tensor_tensor(on[:, u], sums[:, :, 0:HD], inv[:, u, :, None].to_broadcast([P, 2 * NH, HD]), ALU.mult).then_inc(o_ready, 1)

            def add(b, i, u, early):
                tiles = keep.t[:, bass.ds(2 * b, 2), :]
                dve.wait_ge(y_done, b + 1)
                dve.tensor_tensor(tiles, tiles, ps_v[:, 0:2 * C].rearrange("p (a b) -> p a b", b=C), ALU.add).then_inc(added, 1)
                dve.wait_ge(added, b + 1)
                for h in range(2):
                    dve.bn_stats(keep.tbn[:, 2 * b + h, :], keep.t[:, 2 * b + h, :]).then_inc(counted, 1)

            def take_late(b, i, u, early):
                n = UN * b + i if isinstance(b, int) else LATE
                if n < LATE:
                    j = EARLY + n
                    for k in range(TOPK):
                        dve.wait_ge(fetched[n // LOT % 2][k], 16 * (n // LOT // 2 + 1))
                        if n or k:
                            dve.wait_ge(taken, TOPK * n + k)
                        dve.scalar_tensor_tensor(keep.t[:, j, :], rows[:, n // LOT % 2, n % LOT, k, :], m.weight[:, k, j:j + 1],
                                                 keep.t[:, j, :], ALU.mult, ALU.add).then_inc(taken, 1)
                    dve.wait_ge(taken, TOPK * (n + 1))
                    dve.bn_stats(keep.tbn[:, j, :], keep.t[:, j, :]).then_inc(late_counted, 1)

            def norm_late(b, i, u, early):
                if isinstance(b, int) and UN * b + i == LATE:
                    dve.wait_ge(late_counted, LATE)
                    late_norm.collect(dve)
                if isinstance(b, int) and UN * b + i == LATE + 2:
                    late_norm.finish(dve)

            early_norm.collect(dve)
            early_norm.finish(dve)
            dve.wait_ge(const, 5)
            timetable(dve, [(2, True, take_late), (3, True, norm_late), (17, False, o_norm), (2, False, x_out), (5, False, v), (7, True, centre), (10, True, back),
                            (19, False, add)])

        @block.tensor
        def _(pe):
            def turn_x(b, i, u, early):
                pe.wait_ge(normed, 2 * b + 2)
                if not early:
                    if not isinstance(b, int) or b >= 3:
                        pe.wait_ge(ot_ready, b - 2)
                if not isinstance(b, int) or b:
                    pe.wait_ge(xt_ready, b)
                for h in range(2):
                    last = pe.transpose(ps_x[:, h * P:(h + 1) * P], xn[:, u, h, :], keep.ident[:])
                last.then_inc(turned, 1)

            def project(b, i, u, early):
                pe.wait_ge(xt_ready, b + 1)
                if not isinstance(b, int) or b:
                    pe.wait_ge(qk_out, 2 * b)
                    pe.wait_ge(v_out, b)
                if not isinstance(b, int) or b >= 3:
                    pe.wait_ge(added, b - 2)
                for n in range(2):
                    last = pe.matmul(ps_qk[:, n * T:(n + 1) * T], wqk_s[:, n * C:(n + 1) * C], xt[:, u, :], start=True, stop=True)
                last.then_inc(qk_done, 1)
                for h in range(2):
                    last = pe.matmul(ps_v[:, h * C:(h + 1) * C], xt[:, u, h * P:(h + 1) * P], wv_s[:], start=True, stop=True)
                last.then_inc(v_done, 1)

            def score(b, i, u, early):
                tile, h0, heads, keys = unit(i)
                n = UN * b + i
                if i == 0:
                    pe.wait_ge(kx_ready, b + 1)
                if not early or UN * b + i >= 2:
                    pe.wait_ge(centred, n - 1)
                pe.matmul(ps_s[i % 2][:], ident_b[:], mask[:, tile, :], start=True, stop=False)
                pe.matmul(ps_s[i % 2][:], q[:, u, tile * P:(tile + 1) * P], kx[:, u, h0:h0 + heads, 0:keys],
                          start=False, stop=True).then_inc(scored, 1)

            def turn_e(b, i, u, early):
                pe.wait_ge(exped, UN * b + i + 1)
                if not early or UN * b + i >= 2:
                    pe.wait_ge(back_act if i % 2 == 0 else back_dve, 3 * b + i // 2)
                for n in range(4):
                    last = pe.transpose(ps_t[i % 2][:, n * P:(n + 1) * P], e[:, i % 3, n * P:(n + 1) * P], keep.ident[:])
                last.then_inc(e_turned, 1)

            def weigh(b, i, u, early):
                tile, h0, heads, keys = unit(i)
                pe.wait_ge(back_act if i % 2 == 0 else back_dve, 3 * b + i // 2 + 1)
                if i == 0 and (not isinstance(b, int) or b):
                    pe.wait_ge(o_ready, b)
                chunks = keys // P
                for n in range(heads):
                    h = h0 + n
                    at = (tile * NH + h) * (HD + 1)
                    for c in range(chunks):
                        last = pe.matmul(ps_o[:, at:at + HD + 1], pt[:, i % 2, (n * chunks + c) * P:(n * chunks + c + 1) * P],
                                         vx[:, u, c, h, :], start=(c == 0), stop=(c == chunks - 1))
                last.then_inc(weighed, 1)

            def turn_o(b, i, u, early):
                pe.wait_ge(o_ready, b + 1)
                pe.wait_ge(xt_ready, least(b, 3))
                if not isinstance(b, int) or b:
                    pe.wait_ge(ot_ready, b)
                for h in range(2):
                    last = pe.transpose(ps_x[:, h * P:(h + 1) * P], on[:, u, h * NH:(h + 1) * NH, :], keep.ident[:])
                last.then_inc(o_turned, 1)

            def project_o(b, i, u, early):
                pe.wait_ge(ot_ready, b + 1)
                pe.wait_ge(v_out, least(b, 3))
                if not isinstance(b, int) or b:
                    pe.wait_ge(added, b)
                for h in range(2):
                    last = pe.matmul(ps_v[:, h * C:(h + 1) * C], ot[:, u, h, :], wout_s[:], start=True, stop=True)
                last.then_inc(y_done, 1)

            pe.wait_ge(w_in, 48)
            pe.wait_ge(const, 5)
            timetable(pe, [(19, False, project_o), (1, False, turn_x), (3, False, project), (7, True, score),
                           (9, True, turn_e), (11, True, weigh), (18, False, turn_o)])


class Keep:
    pass


def hybrid(nc, a, out):
    q_dram = nc.dram_tensor("q_scratch", [P, B * T], F32, kind="Internal").ap()
    xs_drams = [nc.dram_tensor(f"xs_scratch{i}", [SLOTS, ROW], F32, kind="Internal").ap() for i in range(2)]
    ys_dram = nc.dram_tensor("ys_scratch", [TOPK * B * T + SLOTS, C], F32, kind="Internal").ap()
    with ExitStack() as ctx:
        keep = Keep()
        keep.spent = []
        s = Space(nc, ctx, keep.spent)
        keep.ident = s.sb("ident", [P, P])
        keep.ones = s.sb("ones", [P, P])
        keep.waited = s.sem("waited")
        keep.t = s.sb("tokens", [P, NT, C])
        keep.tbn = s.sb("tbn", [P, NT, 6])
        keep.tscale = s.sb("tscale", [P, NT])
        keep.tshift = s.sb("tshift", [P, NT])
        keep.head8 = s.sb("head8", [P, NH])

        with ExitStack() as conv:
            s = Space(nc, conv, keep.spent)
            keep.xc = s.sb("xc", [P, B, T])
            keep.empty = s.sb("empty", [P, SLOTS // P, ROW])
            keep.group4 = s.sb("group4", [P, P])
            keep.bn = s.sb("bn", [P, B, 6])
            keep.mem_t = s.sb("mem_t", [P, MEM])
            keep.rstd, keep.shift, keep.rstd2, keep.shift2 = (
                s.sb(x, [P, B]) for x in ("rstd", "shift", "rstd2", "shift2"))
            keep.pad = s.sb("pad", [P, B, HH + 2, WW + 2])
            keep.w1s = s.sb("w1s", [P, 5, C])
            keep.w2t = s.sb("w2t_sb", [P, C])
            keep.gate = s.sb("gates", [P, 3, B])
            keep.zbias = s.sb("zbias", [P, B])
            prepare_and_first_norm(nc, s, a["x"], a["memory"], keep)
            memory_lookup(nc, s, a["memory"], xs_drams[0], keep)
            gates(nc, s, a["w1"], a["w1_t"], a["b1"], a["wa_t"], a["ba"], a["wb_t"], a["bb"], a["w2_t"], a["b2"], keep)
            shifted_convolution(nc, s, xs_drams[1], keep)

        with ExitStack() as attention:
            s = Space(nc, attention, keep.spent)
            keep.k_t = s.sb("k_t", [P, B * T])
            keep.vp = s.sb("vp", [P, NT, NH, HD + 1])
            soft_projections(nc, s, a["r_qkv"], a["r_wo"], q_dram, keep)
            rosa_attention(nc, s, q_dram, keep)
        reuse_semaphores(nc, keep.spent)

        def expert_layer(name, xs_dram, n, swiglu, router, loads, shared, finish):
            with ExitStack() as layer:
                own = Space(nc, layer, keep.spent)
                m = Moe(own, name, n, swiglu)
                with ExitStack() as rows:
                    space = Space(nc, rows, keep.spent)
                    xn = [space.sb(f"{name}_xn{k}", [P, NT, ROW]) for k in range(TOPK)]
                    route(nc, own, m, router, lambda sp: load_experts(sp, m, *loads), xn, keep)
                    dispatch(nc, own, m, xs_dram, xn, shared, keep)
                experts(nc, own, m, xs_dram, ys_dram, keep)
                finish(own, m)

        def into_attention(s, m):
            combine(nc, s, m, ys_dram, keep, tiles=EARLY)
            reuse_semaphores(nc, keep.spent)
            causal_attention(nc, s, a["c_qk"], a["c_v"], a["c_out"], m, ys_dram, keep)

        expert_layer("m2", xs_drams[0], 16, True, a["m2_router"], ([a["m2_gate"], a["m2_up"]], a["m2_down"]),
                     (a["m2_shared_up"], a["m2_shared_down"]), into_attention)
        expert_layer("m3", xs_drams[1], 8, False, a["m3_router"], ([a["m3_w1"]], a["m3_w2"], a["m3_b1"], a["m3_b2"]), None,
                     lambda s, m: combine(nc, s, m, ys_dram, keep, out=out))




def kernel(x, L0_conv_memory, L1_conv_w1, L1_conv_b1, L1_conv_wa, L1_conv_ba, L1_conv_wb, L1_conv_bb, L1_conv_w2,
           L1_conv_b2, L2_attn_wq, L2_attn_wk, L2_attn_wv, L2_attn_wo, L2_ffn_gate_w, L2_ffn_wg, L2_ffn_wu, L2_ffn_wd,
           L2_ffn_swg, L2_ffn_swu, L2_ffn_swd, L3_attn_w_qkv, L3_attn_w_out, L3_ffn_W_router, L3_ffn_W1, L3_ffn_b1,
           L3_ffn_W2, L3_ffn_b2):
    import concourse.bacc as bacc
    from concourse.bass_utils import run_bass_kernel_spmd

    def lay(v, *axes):
        v = np.asarray(v)
        return np.ascontiguousarray(v.transpose(*axes) if axes else v)

    def by_chunk(v):
        e, k, n = v.shape
        return lay(v.reshape(e, k // P, P, n), 2, 0, 1, 3)

    w_qkv_t = lay(L3_attn_w_qkv, 1, 0)
    arrays = {
        "x": lay(x), "memory": lay(L0_conv_memory),
        "w1": lay(L1_conv_w1), "w1_t": lay(L1_conv_w1, 1, 0), "b1": lay(np.asarray(L1_conv_b1).reshape(3, C), 1, 0),
        "wa_t": lay(L1_conv_wa, 1, 0), "ba": lay(np.asarray(L1_conv_ba).reshape(C, 1)),
        "wb_t": lay(L1_conv_wb, 1, 0), "bb": lay(np.asarray(L1_conv_bb).reshape(3, C), 1, 0),
        "w2_t": lay(L1_conv_w2, 1, 0), "b2": lay(np.asarray(L1_conv_b2).reshape(C, 1)),
        "r_qkv": np.concatenate([lay(L2_attn_wq), lay(L2_attn_wk), lay(L2_attn_wv)], axis=1), "r_wo": lay(L2_attn_wo),
        "m2_router": lay(L2_ffn_gate_w, 1, 0), "m2_gate": lay(L2_ffn_wg, 2, 0, 1), "m2_up": lay(L2_ffn_wu, 2, 0, 1),
        "m2_down": by_chunk(lay(L2_ffn_wd, 0, 2, 1)),
        "m2_shared_up": np.concatenate([lay(L2_ffn_swg, 1, 0), lay(L2_ffn_swu, 1, 0)], axis=1),
        "m2_shared_down": by_chunk(lay(L2_ffn_swd, 1, 0)[None])[:, 0],
        "c_qk": lay(w_qkv_t[:, 0:2 * C]), "c_v": lay(w_qkv_t[:, 2 * C:]), "c_out": lay(L3_attn_w_out, 1, 0),
        "m3_router": lay(L3_ffn_W_router), "m3_w1": lay(L3_ffn_W1, 1, 0, 2), "m3_b1": lay(np.asarray(L3_ffn_b1).reshape(-1, KC, P), 2, 0, 1),
        "m3_w2": by_chunk(lay(L3_ffn_W2)), "m3_b2": lay(L3_ffn_b2),
    }
    nc = bacc.Bacc("TRN2", target_bir_lowering=False, num_devices=1)
    given = {n: nc.dram_tensor("in_" + n, v.shape, mybir.dt.from_np(v.dtype), kind="ExternalInput").ap()
             for n, v in arrays.items()}
    out = nc.dram_tensor("out", [B, C, HH, WW], F32, kind="ExternalOutput").ap()
    hybrid(nc, given, out)
    r = run_bass_kernel_spmd(nc, [{"in_" + n: v for n, v in arrays.items()}], core_ids=[0])
    return r.results[0]["out"]
```
